# Optimizing a Trainium2 kernel written in Bass

```python
import numpy as np
import jax
import jax.numpy as jnp

def _softmax(x, axis=-1):
    return jax.nn.softmax(x, axis=axis)

def _gelu(x):
    return jax.nn.gelu(x, approximate=True)

def _silu(x):
    return jax.nn.silu(x)

def _sigmoid(x):
    return jax.nn.sigmoid(x)

def _layernorm(x, axis=-1, eps=1e-05):
    m = jnp.mean(x, axis=axis, keepdims=True)
    v = jnp.var(x, axis=axis, keepdims=True)
    return (x - m) / jnp.sqrt(v + eps)

def _scatter_add(tgt, idx, src, axis=0):
    return tgt.at[idx].add(src)

def _segment_sum(src, seg, n):
    return jax.ops.segment_sum(src, seg, n)
kernel_name = 'mk_seq_postln_d2_jaxref_r8_41e072'

def setup_inputs(seed: int=0):
    np.random.seed(seed)
    _w = jnp.asarray

    def _L0_attn_setup():
        import jax, jax.numpy as jnp
        import numpy as np
        B, S, HID = (1, 256, 512)
        H, NOPE, ROPE, VD = (32, 128, 64, 128)
        QKD = NOPE + ROPE
        Q_RANK, KV_RANK = (192, 64)
        IDX_H, IDX_D, TOPK = (16, 128, 128)
        EPS, THETA = (1e-05, 10000.0)

        def rmsnorm(x, w):
            return x * jax.lax.rsqrt(jnp.mean(x * x, axis=-1, keepdims=True) + EPS) * w

        def rope_interleaved(x, pos):
            d = x.shape[-1]
            inv_freq = 1.0 / THETA ** (jnp.arange(0, d, 2, dtype=jnp.float32) / d)
            ang = pos[:, None] * inv_freq[None, :]
            cos, sin = (jnp.cos(ang), jnp.sin(ang))
            x2 = x.reshape(*x.shape[:-1], d // 2, 2)
            x0, x1 = (x2[..., 0], x2[..., 1])
            return jnp.stack([x0 * cos - x1 * sin, x1 * cos + x0 * sin], axis=-1).reshape(x.shape)
        key = jax.random.key(seed)
        ks = jax.random.split(key, 12)
        s = 0.02
        return {'hidden_states': jax.random.normal(ks[0], (B, S, HID), jnp.float32), 'q_a_w': jax.random.normal(ks[1], (HID, Q_RANK), jnp.float32) * s, 'q_a_norm_w': jnp.ones((Q_RANK,), jnp.float32), 'q_b_w': jax.random.normal(ks[2], (Q_RANK, H * QKD), jnp.float32) * s, 'kv_a_w': jax.random.normal(ks[3], (HID, KV_RANK + ROPE), jnp.float32) * s, 'kv_a_norm_w': jnp.ones((KV_RANK,), jnp.float32), 'kv_b_w': jax.random.normal(ks[4], (KV_RANK, H * (NOPE + VD)), jnp.float32) * s, 'o_w': jax.random.normal(ks[5], (H * VD, HID), jnp.float32) * s, 'idx_wq_w': jax.random.normal(ks[6], (HID, IDX_H * IDX_D), jnp.float32) * s, 'idx_wk_w': jax.random.normal(ks[7], (HID, IDX_D), jnp.float32) * s, 'idx_weights_w': jax.random.normal(ks[8], (HID, IDX_H), jnp.float32) * s}
    _L0_attn_in = _L0_attn_setup()

    def _L0_ffn_setup():
        import jax, jax.numpy as jnp
        import numpy as np
        HIDDEN = 512
        INTER = 1376
        GROUPSIZE = 128
        PACK = 8

        def dequant_gptq(qweight, scales, zeros, groupsize):
            K = qweight.shape[0] * PACK
            N = qweight.shape[1]
            k = jnp.arange(K)
            q = qweight[k // PACK, :] >> (k % PACK * 4)[:, None] & 15
            n = jnp.arange(N)
            z = zeros[:, n // PACK] >> (n % PACK * 4)[None, :] & 15
            s = scales.astype(jnp.float32)
            zp = (z.astype(jnp.float32) + 1.0) * s
            g = k // groupsize
            return q.astype(jnp.float32) * s[g] - zp[g]
        key = jax.random.key(seed)
        ks = jax.random.split(key, 11)
        imax = 2147483647
        G_h = HIDDEN // GROUPSIZE
        G_i = (INTER + GROUPSIZE - 1) // GROUPSIZE
        x = (jax.random.normal(ks[0], (2, 256, HIDDEN), dtype=jnp.float32) * 0.5).astype(jnp.float16)
        return {'x': x, 'gate_qweight': jax.random.randint(ks[1], (HIDDEN // PACK, INTER), 0, imax, dtype=jnp.int32), 'gate_scales': (jax.random.uniform(ks[2], (G_h, INTER), dtype=jnp.float32) * 0.01 + 0.001).astype(jnp.float16), 'gate_zeros': jax.random.randint(ks[3], (G_h, INTER // PACK), 0, imax, dtype=jnp.int32), 'up_qweight': jax.random.randint(ks[4], (HIDDEN // PACK, INTER), 0, imax, dtype=jnp.int32), 'up_scales': (jax.random.uniform(ks[5], (G_h, INTER), dtype=jnp.float32) * 0.01 + 0.001).astype(jnp.float16), 'up_zeros': jax.random.randint(ks[6], (G_h, INTER // PACK), 0, imax, dtype=jnp.int32), 'down_qweight': jax.random.randint(ks[7], (INTER // PACK, HIDDEN), 0, imax, dtype=jnp.int32), 'down_scales': (jax.random.uniform(ks[8], (G_i, HIDDEN), dtype=jnp.float32) * 0.01 + 0.001).astype(jnp.float16), 'down_zeros': jax.random.randint(ks[9], (G_i, HIDDEN // PACK), 0, imax, dtype=jnp.int32)}
    _L0_ffn_in = _L0_ffn_setup()

    def _L1_attn_setup():
        import jax, jax.numpy as jnp
        import numpy as np
        N_Q_HEAD = 32
        N_KV_HEAD = 8
        N_EMBD = 512
        B, T = (2, 256)
        key = jax.random.key(seed)
        ks = jax.random.split(key, 5)
        s = 0.02
        return {'x': jax.random.normal(ks[0], (B, T, N_EMBD), dtype=jnp.float32), 'Wq': jax.random.normal(ks[1], (N_EMBD, N_EMBD), dtype=jnp.float32) * s, 'Wk': jax.random.normal(ks[2], (N_EMBD // (N_Q_HEAD // N_KV_HEAD), N_EMBD), dtype=jnp.float32) * s, 'Wv': jax.random.normal(ks[3], (N_EMBD // (N_Q_HEAD // N_KV_HEAD), N_EMBD), dtype=jnp.float32) * s, 'Wo': jax.random.normal(ks[4], (N_EMBD, N_EMBD), dtype=jnp.float32) * s, 'bo': jnp.zeros((N_EMBD,), dtype=jnp.float32)}
    _L1_attn_in = _L1_attn_setup()

    def _L1_ffn_setup():
        import jax, jax.numpy as jnp
        import numpy as np
        B, S, DIN, DOUT, R = (2, 256, 512, 512, 32)
        key = jax.random.key(seed)
        k1, k2, k3, k4, k5 = jax.random.split(key, 5)
        std = 1.0 / np.sqrt(R)
        return {'x': jax.random.normal(k1, (B, S, DIN), dtype=jnp.float32), 'W': jax.random.normal(k2, (DOUT, DIN), dtype=jnp.float32) * 0.02, 'lora_A': jax.random.normal(k3, (R, DIN), dtype=jnp.float32) * std, 'lora_B': jax.random.normal(k4, (DOUT, R), dtype=jnp.float32) * 0.01, 'magnitude': jax.random.uniform(k5, (DOUT,), dtype=jnp.float32) + 0.5}
    _L1_ffn_in = _L1_ffn_setup()
    _d = {'L0_attn_hidden_states': _L0_attn_in['hidden_states'], 'L0_attn_q_a_w': _L0_attn_in['q_a_w'], 'L0_attn_q_a_norm_w': _L0_attn_in['q_a_norm_w'], 'L0_attn_q_b_w': _L0_attn_in['q_b_w'], 'L0_attn_kv_a_w': _L0_attn_in['kv_a_w'], 'L0_attn_kv_a_norm_w': _L0_attn_in['kv_a_norm_w'], 'L0_attn_kv_b_w': _L0_attn_in['kv_b_w'], 'L0_attn_o_w': _L0_attn_in['o_w'], 'L0_attn_idx_wq_w': _L0_attn_in['idx_wq_w'], 'L0_attn_idx_wk_w': _L0_attn_in['idx_wk_w'], 'L0_attn_idx_weights_w': _L0_attn_in['idx_weights_w'], 'L0_ffn_gate_qweight': _L0_ffn_in['gate_qweight'], 'L0_ffn_gate_scales': _L0_ffn_in['gate_scales'], 'L0_ffn_gate_zeros': _L0_ffn_in['gate_zeros'], 'L0_ffn_up_qweight': _L0_ffn_in['up_qweight'], 'L0_ffn_up_scales': _L0_ffn_in['up_scales'], 'L0_ffn_up_zeros': _L0_ffn_in['up_zeros'], 'L0_ffn_down_qweight': _L0_ffn_in['down_qweight'], 'L0_ffn_down_scales': _L0_ffn_in['down_scales'], 'L0_ffn_down_zeros': _L0_ffn_in['down_zeros'], 'L1_attn_Wq': _L1_attn_in['Wq'], 'L1_attn_Wk': _L1_attn_in['Wk'], 'L1_attn_Wv': _L1_attn_in['Wv'], 'L1_attn_Wo': _L1_attn_in['Wo'], 'L1_attn_bo': _L1_attn_in['bo'], 'L1_ffn_W': _L1_ffn_in['W'], 'L1_ffn_lora_A': _L1_ffn_in['lora_A'], 'L1_ffn_lora_B': _L1_ffn_in['lora_B'], 'L1_ffn_magnitude': _L1_ffn_in['magnitude']}
    _x0 = _d['L0_attn_hidden_states']
    _d['L0_attn_hidden_states'] = jax.random.normal(jax.random.fold_in(jax.random.key(seed), 1), (8, 256, 512), dtype=_x0.dtype)
    del _x0
    return _d

def reference(L0_attn_hidden_states, L0_attn_q_a_w, L0_attn_q_a_norm_w, L0_attn_q_b_w, L0_attn_kv_a_w, L0_attn_kv_a_norm_w, L0_attn_kv_b_w, L0_attn_o_w, L0_attn_idx_wq_w, L0_attn_idx_wk_w, L0_attn_idx_weights_w, L0_ffn_gate_qweight, L0_ffn_gate_scales, L0_ffn_gate_zeros, L0_ffn_up_qweight, L0_ffn_up_scales, L0_ffn_up_zeros, L0_ffn_down_qweight, L0_ffn_down_scales, L0_ffn_down_zeros, L1_attn_Wq, L1_attn_Wk, L1_attn_Wv, L1_attn_Wo, L1_attn_bo, L1_ffn_W, L1_ffn_lora_A, L1_ffn_lora_B, L1_ffn_magnitude):

    def _L0_attn_ref(hidden_states, q_a_w, q_a_norm_w, q_b_w, kv_a_w, kv_a_norm_w, kv_b_w, o_w, idx_wq_w, idx_wk_w, idx_weights_w):
        import jax, jax.numpy as jnp
        import numpy as np
        B, S, HID = (1, 256, 512)
        H, NOPE, ROPE, VD = (32, 128, 64, 128)
        QKD = NOPE + ROPE
        Q_RANK, KV_RANK = (192, 64)
        IDX_H, IDX_D, TOPK = (16, 128, 128)
        EPS, THETA = (1e-05, 10000.0)

        def rmsnorm(x, w):
            return x * jax.lax.rsqrt(jnp.mean(x * x, axis=-1, keepdims=True) + EPS) * w

        def rope_interleaved(x, pos):
            d = x.shape[-1]
            inv_freq = 1.0 / THETA ** (jnp.arange(0, d, 2, dtype=jnp.float32) / d)
            ang = pos[:, None] * inv_freq[None, :]
            cos, sin = (jnp.cos(ang), jnp.sin(ang))
            x2 = x.reshape(*x.shape[:-1], d // 2, 2)
            x0, x1 = (x2[..., 0], x2[..., 1])
            return jnp.stack([x0 * cos - x1 * sin, x1 * cos + x0 * sin], axis=-1).reshape(x.shape)
        b, s, _ = hidden_states.shape
        pos = jnp.arange(s, dtype=jnp.float32)
        q_lat = rmsnorm(hidden_states @ q_a_w, q_a_norm_w)
        q = (q_lat @ q_b_w).reshape(b, s, H, QKD).transpose(0, 2, 1, 3)
        q_nope, q_pe = (q[..., :NOPE], q[..., NOPE:])
        ckv = hidden_states @ kv_a_w
        kv_lat, k_pe = (ckv[..., :KV_RANK], ckv[..., KV_RANK:])
        kv = (rmsnorm(kv_lat, kv_a_norm_w) @ kv_b_w).reshape(b, s, H, NOPE + VD).transpose(0, 2, 1, 3)
        k_nope, v = (kv[..., :NOPE], kv[..., NOPE:])
        q_pe = rope_interleaved(q_pe, pos)
        k_pe = rope_interleaved(k_pe[:, None, :, :], pos)
        scores = (jnp.einsum('bhqd,bhkd->bhqk', q_nope, k_nope) + jnp.einsum('bhqd,bhkd->bhqk', q_pe, k_pe)) * QKD ** (-0.5)
        iq = (hidden_states @ idx_wq_w).reshape(b, s, IDX_H, IDX_D)
        ik = hidden_states @ idx_wk_w
        iw = hidden_states @ idx_weights_w * IDX_H ** (-0.5)
        idx_scores = jnp.einsum('bqn,bnqk->bqk', iw, jax.nn.relu(jnp.einsum('bqnd,bkd->bnqk', iq, ik))) * IDX_D ** (-0.5)
        causal = pos[:, None] >= pos[None, :]
        idx_scores = jnp.where(causal, idx_scores, -jnp.inf)
        _, topk_idx = jax.lax.top_k(idx_scores, TOPK)
        bi = jnp.arange(b)[:, None, None]
        qi = jnp.arange(s)[None, :, None]
        topk_mask = jnp.zeros((b, s, s), bool).at[bi, qi, topk_idx].set(True)
        mask = topk_mask & causal
        scores = jnp.where(mask[:, None], scores, -jnp.inf)
        attn = jax.nn.softmax(scores, axis=-1)
        out = jnp.einsum('bhqk,bhkd->bqhd', attn, v).reshape(b, s, H * VD)
        return out @ o_w

    def _L0_ffn_ref(x, gate_qweight, gate_scales, gate_zeros, up_qweight, up_scales, up_zeros, down_qweight, down_scales, down_zeros):
        import jax, jax.numpy as jnp
        import numpy as np
        HIDDEN = 512
        INTER = 1376
        GROUPSIZE = 128
        PACK = 8

        def dequant_gptq(qweight, scales, zeros, groupsize):
            K = qweight.shape[0] * PACK
            N = qweight.shape[1]
            k = jnp.arange(K)
            q = qweight[k // PACK, :] >> (k % PACK * 4)[:, None] & 15
            n = jnp.arange(N)
            z = zeros[:, n // PACK] >> (n % PACK * 4)[None, :] & 15
            s = scales.astype(jnp.float32)
            zp = (z.astype(jnp.float32) + 1.0) * s
            g = k // groupsize
            return q.astype(jnp.float32) * s[g] - zp[g]
        B, S, H = x.shape
        x2 = x.reshape(-1, H).astype(jnp.float32)
        Wg = dequant_gptq(gate_qweight, gate_scales, gate_zeros, GROUPSIZE)
        Wu = dequant_gptq(up_qweight, up_scales, up_zeros, GROUPSIZE)
        Wd = dequant_gptq(down_qweight, down_scales, down_zeros, GROUPSIZE)
        gate = x2 @ Wg
        up = x2 @ Wu
        inter = gate * jax.nn.sigmoid(gate) * up
        out = (inter @ Wd).astype(jnp.float16)
        return out.reshape(B, S, H)

    def _L1_attn_ref(x, Wq, Wk, Wv, Wo, bo):
        import jax, jax.numpy as jnp
        import numpy as np
        N_Q_HEAD = 32
        N_KV_HEAD = 8
        N_EMBD = 512
        B, T = (2, 256)
        b, t, e = x.shape
        h_kv = N_KV_HEAD
        g = N_Q_HEAD // N_KV_HEAD
        d = e // N_Q_HEAD
        q = (x @ Wq.T).reshape(b, t, h_kv, g, d).transpose(0, 2, 3, 1, 4)
        k = (x @ Wk.T).reshape(b, t, h_kv, d).transpose(0, 2, 1, 3)
        v = (x @ Wv.T).reshape(b, t, h_kv, d).transpose(0, 2, 1, 3)
        scale = jnp.sqrt(jnp.asarray(d, dtype=x.dtype))
        att = jnp.einsum('bhgqd,bhkd->bhgqk', q, k) / scale
        att = jax.nn.softmax(att, axis=-1)
        y = jnp.einsum('bhgqk,bhkd->bhgqd', att, v)
        y = y.transpose(0, 3, 1, 2, 4).reshape(b, t, e)
        return y @ Wo.T + bo

    def _L1_ffn_ref(x, W, lora_A, lora_B, magnitude):
        import jax, jax.numpy as jnp
        import numpy as np
        B, S, DIN, DOUT, R = (2, 256, 512, 512, 32)
        base = jnp.einsum('bsi,oi->bso', x, W)
        lora = jnp.einsum('bsr,or->bso', jnp.einsum('bsi,ri->bsr', x, lora_A), lora_B)
        eff_W = W + lora_B @ lora_A
        column_norm = jax.lax.stop_gradient(jnp.sqrt(jnp.sum(eff_W * eff_W, axis=1)))
        result = (base + lora) / column_norm[None, None, :]
        return result * magnitude[None, None, :]
    x = L0_attn_hidden_states
    x = _layernorm(x + _L0_attn_ref(x, L0_attn_q_a_w, L0_attn_q_a_norm_w, L0_attn_q_b_w, L0_attn_kv_a_w, L0_attn_kv_a_norm_w, L0_attn_kv_b_w, L0_attn_o_w, L0_attn_idx_wq_w, L0_attn_idx_wk_w, L0_attn_idx_weights_w), axis=-1)
    x = _layernorm(x + _L0_ffn_ref(x, L0_ffn_gate_qweight, L0_ffn_gate_scales, L0_ffn_gate_zeros, L0_ffn_up_qweight, L0_ffn_up_scales, L0_ffn_up_zeros, L0_ffn_down_qweight, L0_ffn_down_scales, L0_ffn_down_zeros), axis=-1)
    x = _layernorm(x + _L1_attn_ref(x, L1_attn_Wq, L1_attn_Wk, L1_attn_Wv, L1_attn_Wo, L1_attn_bo), axis=-1)
    x = _layernorm(x + _L1_ffn_ref(x, L1_ffn_W, L1_ffn_lora_A, L1_ffn_lora_B, L1_ffn_magnitude), axis=-1)
    return x

_drawn_inputs = setup_inputs


def setup_inputs(seed=0):
    import zlib

    import numpy as np

    out = dict(_drawn_inputs(seed))
    spreads = {'L0_attn_q_a_norm_w': (1.0, 0.6),
     'L0_attn_kv_a_norm_w': (1.0, 0.6),
     'L1_attn_bo': (0.0, 0.1)}
    factors = {'L0_attn_q_a_w': 8.0,
     'L0_attn_q_b_w': 8.0,
     'L0_attn_idx_wq_w': 6.281,
     'L0_attn_idx_wk_w': 6.335,
     'L0_attn_idx_weights_w': 6.291,
     'L1_attn_Wq': 8.0,
     'L1_attn_Wk': 8.0}
    for name, (base, spread) in spreads.items():
        noise = np.random.default_rng([zlib.crc32(name.encode()), seed]).standard_normal(out[name].shape)
        drawn = base * np.exp(spread * noise) if base else spread * noise
        out[name] = jnp.asarray(drawn.astype(out[name].dtype))
    for name, factor in factors.items():
        out[name] = (out[name] * factor).astype(out[name].dtype)
    return out
```

```python
from contextlib import ExitStack

import numpy as np

import concourse.bass as bass
from concourse import mybir

F32 = mybir.dt.float32
F16 = mybir.dt.float16
BF16 = mybir.dt.bfloat16
I32 = mybir.dt.int32
F32R = mybir.dt.float32r
ALU = mybir.AluOpType
ACT = mybir.ActivationFunctionType
AX = mybir.AxisListType

P = 128
B, S, D = 8, 256, 512
TOK = B * S
NT = TOK // P
KT = D // P
H, NOPE, ROPE, VD = 32, 128, 64, 128
QR, KVR = 192, 64
IH, ID, TOPK = 16, 128, 128
A1N = QR + KVR + ROPE
HC = 4
NC = H // HC
QSCALE = float((NOPE + ROPE) ** -0.5)
FI = 1376
FM = -(-FI // P)
FLAST = FI - (FM - 1) * P
UNITS = 3 * FM
QUARTER = TOK // 4
KVH, G, HD = 8, 4, 16
R = 32
EPS = 1e-5

MASKED = -1.0e30
NOT_CAUSAL = -3.0e38
TAKEN = -3.4e38


class Track:

    def __init__(self, nc, ctx, name, step=1):
        self.sem, self.step, self.count = ctx.enter_context(nc.semaphore(name)), step, 0

    def add(self, ins):
        ins.then_inc(self.sem, self.step)
        self.count += self.step
        return self.count


def build(nc, a, out):
    ctx = ExitStack()
    pe, act, dve, pool, sync = nc.tensor, nc.scalar, nc.vector, nc.gpsimd, nc.sync
    done = {}
    waited = {}
    transfers = {}

    with ctx:
        by_pe, by_act = Track(nc, ctx, "by_pe"), Track(nc, ctx, "by_act")
        by_dve, by_pool = Track(nc, ctx, "by_dve"), Track(nc, ctx, "by_pool")

        def sig(track, ins, *name):
            done[name] = (track, track.add(ins))
            return name

        def need(eng, *name):
            track, value = done[name]
            key = (id(eng), id(track))
            if waited.get(key, 0) < value:
                eng.wait_ge(track.sem, value)
                waited[key] = value

        def load(name, dst, src, eng=sync, group=None):
            key = (name,) if isinstance(name, str) else name
            kind, *index = group or key
            slot = "_".join([kind] + [str(n % (NT if kind == "store" else 4)) for n in index])
            if slot not in transfers:
                transfers[slot] = Track(nc, ctx, "dma_" + slot, 16)
            done[group or key] = (transfers[slot], transfers[slot].add(eng.dma_start(dst, src)))

        def sb(stack, name, shape, dt=F32):
            return stack.enter_context(nc.sbuf_tensor(name, shape, dt))

        X = sb(ctx, "X", [P, NT, D])
        ident = sb(ctx, "ident", [P, P])
        PS = ctx.enter_context(nc.psum_tensor("PS", [P, 8, 512], F32))
        minus_half = sb(ctx, "minus_half", [P, 2])
        qpack = [sb(ctx, f"qpack{i}", [P, 512], I32) for i in range(2)]
        zrep = [sb(ctx, f"zrep{i}", [P, 512], I32) for i in range(2)]
        gsc = [sb(ctx, f"gsc{i}", [P, 512], F16) for i in range(2)]
        nib_par = sb(ctx, "nib_par", [P, 2], I32)
        zshift = sb(ctx, "zshift", [P, 8], I32)
        stat = sb(ctx, "stat", [P, 4, 6])
        mv = sb(ctx, "mv", [P, 4, 2])
        rstd = sb(ctx, "rstd", [P, 4, 1])

        load("ident", ident[:], a["ident"])
        sig(by_dve, dve.memset(minus_half[:], -0.5), "minus_half")

        ln_count = [0]

        def layer_norm(t, bank, tag, bank_ready, extra=None, y16=None):
            k = ln_count[0] % 4
            ln_count[0] += 1
            x = X[:, t, :]
            need(dve, *bank_ready)
            if extra is not None:
                need(dve, *extra)
            sig(by_dve, dve.tensor_tensor(x, x, bank, ALU.add), tag, "added", t)
            need(dve, tag, "added", t)
            if ln_count[0] > 4:
                need(dve, "ln_applied", ln_count[0] - 5)
            sig(by_dve, dve.bn_stats(stat[:, k, :], x), tag, "stats", t)
            need(dve, tag, "stats", t)
            sig(by_dve, dve.bn_aggr(mv[:, k, :], stat[:, k, :]), tag, "aggr", t)
            need(dve, tag, "aggr", t)
            sig(by_dve, dve.tensor_scalar(stat[:, k, 0:1], mv[:, k, 1:2], EPS, None, ALU.add), tag, "var", t)
            need(pool, tag, "var", t)
            need(pool, "minus_half")
            sig(by_pool, pool.tensor_tensor(rstd[:, k, :], stat[:, k, 0:1], minus_half[:, 0:1], ALU.pow),
                tag, "rstd", t)
            need(pool, tag, "rstd", t)
            sig(by_pool, pool.tensor_scalar(x, x, mv[:, k, 0:1], rstd[:, k, :], ALU.subtract, ALU.mult),
                tag, "normed", t)
            done[("ln_applied", ln_count[0] - 1)] = done[(tag, "normed", t)]

        attn = ExitStack()
        XT = [sb(attn, f"XT{i}", [P, KT, S]) for i in range(2)]
        mask1 = sb(attn, "mask1", [P, B, S], BF16)
        mask0 = sb(attn, "mask0", [P, P], BF16)
        Wq0 = sb(attn, "Wq0", [P, NC, 512])
        Wq1 = sb(attn, "Wq1", [QR - P, NC, 512])
        Wvo = sb(attn, "Wvo", [P, H // 2, D])
        a1w = sb(attn, "a1w", [P, KT, A1N])

        xT_view = a["xT"].rearrange("(k p) n -> p k n", p=P)

        def load_xT(n):
            if n >= 2:
                need(sync, "xT_used", n - 2)
            load(("xT", n), XT[n % 2][:], xT_view[:, :, (n % B) * S:(n % B + 1) * S])

        idx = ExitStack()
        wk_i = sb(idx, "wk_i", [P, KT, ID])
        ww_i = sb(idx, "ww_i", [P, KT, IH])
        wq_i = sb(idx, "wq_i", [P, KT, IH * ID])
        causal1 = sb(idx, "causal1", [P, S])
        ikT = [sb(idx, f"ikT{i}", [P, S]) for i in range(2)]
        iw = [sb(idx, f"iw{i}", [P, IH]) for i in range(2)]
        iqT = [sb(idx, f"iqT{i}", [P, 4 * P]) for i in range(2)]
        rel = [sb(idx, f"rel{i}", [P, 2 * S]) for i in range(3)]
        accs = [sb(idx, f"acc{i}", [P, S]) for i in range(2)]
        top8 = sb(idx, "top8", [P, 8])

        load_xT(0)
        load("wk_i", wk_i[:], a["wk_i"].rearrange("(k p) n -> p k n", p=P))
        load("ww_i", ww_i[:], a["ww_i"].rearrange("(k p) n -> p k n", p=P))
        for g in range(4):
            load(("wq_i", g), wq_i[:, :, g * 512:(g + 1) * 512],
                 a["wq_i"].rearrange("(k p) n -> p k n", p=P)[:, :, g * 512:(g + 1) * 512])
        load("causal1", causal1[:], a["causal1"])
        load("mask0", mask0[:], a["mask0"])
        load_xT(1)

        def idx_keys(b):
            need(pe, "xT", b)
            need(pe, "wk_i")
            need(pe, "ww_i")
            if b >= 1:
                need(pe, "ikT", b - 1)
                need(pe, "iw", b - 1)
            for k in range(KT):
                m = pe.matmul(PS[:, 0, 0:S], wk_i[:, k, :], XT[b % 2][:, k, :], start=(k == 0), stop=(k == KT - 1))
            for k in range(KT):
                m = pe.matmul(PS[:, 0, S:S + IH], XT[b % 2][:, k, P:S], ww_i[:, k, :],
                              start=(k == 0), stop=(k == KT - 1))
            sig(by_pe, m, "idx_keys", b)
            need(dve, "idx_keys", b)
            if b >= 2:
                need(dve, "idx_scores", b - 2, 7)
            sig(by_dve, dve.tensor_copy(ikT[b % 2][:], PS[:, 0, 0:S]), "ikT", b)
            sig(by_dve, dve.tensor_scalar(iw[b % 2][:], PS[:, 0, S:S + IH], float(IH ** -0.5), None, ALU.mult),
                "iw", b)

        def idx_queries(b, g):
            need(pe, "wq_i", g)
            n = 4 * b + g
            if n >= 2:
                need(pe, "iqT", n - 2)
            for h in range(4):
                for k in range(KT):
                    m = pe.matmul(PS[:, 1 + n % 2, h * P:(h + 1) * P],
                                  wq_i[:, k, (4 * g + h) * ID:(4 * g + h + 1) * ID], XT[b % 2][:, k, P:S],
                                  start=(k == 0), stop=(k == KT - 1))
            sig(by_pe, m, "idx_q", n)
            if g == 3:
                done[("xT_used", b)] = done[("idx_q", n)]
            need(act, "idx_q", n)
            if n >= 2:
                need(act, "idx_scores", (n - 2) // 4, 2 * ((n - 2) % 4) + 1)
            sig(by_act, act.activation(iqT[n % 2][:], PS[:, 1 + n % 2, :], ACT.Copy), "iqT", n)

        def idx_scores(b, g):
            n = 4 * b + g
            need(pe, "iqT", n)
            need(pe, "ikT", b)
            for pr in range(2):
                u = 8 * b + 2 * g + pr
                if u >= 4:
                    need(pe, "relu", u - 4)
                for h in range(2):
                    m = pe.matmul(PS[:, 3 + u % 4, h * S:(h + 1) * S],
                                  iqT[n % 2][:, (2 * pr + h) * P:(2 * pr + h + 1) * P], ikT[b % 2][:],
                                  start=True, stop=True)
                sig(by_pe, m, "idx_scores", b, 2 * g + pr)
                need(act, "idx_scores", b, 2 * g + pr)
                if u >= 3:
                    need(act, "idx_sum", u - 3)
                sig(by_act, act.activation(rel[u % 3][:], PS[:, 3 + u % 4, :], ACT.Relu), "relu", u)
                need(dve, "relu", u)
                for h in range(2):
                    head = 4 * g + 2 * pr + h
                    acc, w = accs[b % 2][:], iw[b % 2][:, head:head + 1]
                    r = rel[u % 3][:, h * S:(h + 1) * S]
                    if head == 0:
                        need(dve, "iw", b)
                        ins = dve.tensor_scalar(acc, r, w, None, ALU.mult)
                    else:
                        need(dve, "idx_acc", b, head - 1)
                        ins = dve.scalar_tensor_tensor(acc, r, w, acc, ALU.mult, ALU.add)
                    sig(by_dve, ins, "idx_acc", b, head)
                done[("idx_sum", u)] = done[("idx_acc", b, 4 * g + 2 * pr + 1)]

        def idx_topk_parts(b):
            acc = accs[b % 2][:]

            def scale():
                need(dve, "idx_acc", b, IH - 1)
                need(dve, "causal1")
                sig(by_dve, dve.scalar_tensor_tensor(acc, acc, float(ID ** -0.5), causal1[:], ALU.mult, ALU.add),
                    "taken", b, -1)

            def round_(r):
                need(dve, "taken", b, r - 1)
                sig(by_dve, dve.max(top8[:], acc), "top8", b, r)
                need(dve, "top8", b, r)
                sig(by_dve, dve.match_replace(acc, top8[:], acc, TAKEN), "taken", b, r)

            def finish():
                need(dve, "taken", b, TOPK // 8 - 1)
                sig(by_dve, dve.tensor_scalar(mask1[:, b, :], acc, (TAKEN + NOT_CAUSAL) / 2, MASKED,
                                              ALU.is_gt, ALU.mult), "mask1", b)
            return [scale] + [lambda r=r: round_(r) for r in range(TOPK // 8)] + [finish]

        pending = []
        for b in range(B):
            idx_keys(b)
            idx_queries(b, 0)
            for g in range(4):
                if g < 3:
                    idx_queries(b, g + 1)
                idx_scores(b, g)
                for _ in range(5):
                    if pending:
                        pending.pop(0)()
            pending = idx_topk_parts(b)
            load_xT(b + 2)
            if b == 0:
                load("a1w", a1w[:], a["a1w"].rearrange("(k p) n -> p k n", p=P))
                pe_view = a["q_pe_w"].rearrange("r (c n) -> r c n", c=NC)
                load("Wq0_pe", Wq0[:, :, 256:512], pe_view[0:P])
                load("Wq1_pe", Wq1[:, :, 256:512], pe_view[P:QR])
        for f in pending:
            f()
        idx_end = [("idx_scores", B - 1, 7), ("relu", 8 * B - 1), ("mask1", B - 1)]

        fold = ExitStack()
        wt_qn = [sb(fold, f"wt_qn{i}", [P, HC, QR]) for i in range(2)]
        wt_k = [sb(fold, f"wt_k{i}", [P, HC, KVR]) for i in range(2)]
        wt_v = [sb(fold, f"wt_v{i}", [P, HC, KVR]) for i in range(2)]
        wt_o = [sb(fold, f"wt_o{i}", [P, HC, D]) for i in range(2)]

        def fold_load(c):
            i = c % 2
            if c >= 2:
                need(sync, "fold_vo", c - 2)
            hs = slice(HC * c, HC * (c + 1))
            load(("wt_qn", c), wt_qn[i][:], a["qnT"][:, hs, :])
            load(("wt_k", c), wt_k[i][:], a["wkT"][:, hs, :])
            load(("wt_v", c), wt_v[i][:], a["wvT"][:, hs, :])
            load(("wt_o", c), wt_o[i][:], a["o_w"].rearrange("(h p) n -> p h n", p=P)[:, hs, :])

        fold_load(0)
        fold_load(1)
        for c in range(NC):
            i = c % 2
            need(pe, "wt_qn", c)
            need(pe, "wt_k", c)
            if c == 0:
                for n in idx_end:
                    need(pe, *n)
                need(pe, "iqT", 4 * B - 1)
            else:
                need(pe, "fold_q1", c - 1)
            for h in range(HC):
                pe.matmul(PS[:, 1, h * KVR:(h + 1) * KVR], wt_qn[i][:, h, 0:P], wt_k[i][:, h, :], start=True, stop=True)
            for h in range(HC):
                m = pe.matmul(PS[0:QR - P, 2, h * KVR:(h + 1) * KVR], wt_qn[i][:, h, P:QR], wt_k[i][:, h, :],
                              start=True, stop=True)
            sig(by_pe, m, "fold_qk", c)
            need(act, "fold_qk", c)
            sig(by_act, act.activation(Wq0[:, c, 0:256], PS[:, 1, 0:256], ACT.Copy), "fold_q0", c)
            sig(by_act, act.activation(Wq1[:, c, 0:256], PS[0:QR - P, 2, 0:256], ACT.Copy), "fold_q1", c)
            need(pe, "wt_v", c)
            need(pe, "wt_o", c)
            if c >= 1:
                need(pe, "Wvo", c - 1)
            for h in range(HC):
                half = h % 2 * KVR
                m = pe.matmul(PS[half:half + KVR, 3 + h // 2, :], wt_v[i][:, h, :], wt_o[i][:, h, :],
                              start=True, stop=True)
            sig(by_pe, m, "fold_vo", c)
            need(dve, "fold_vo", c)
            sig(by_dve, dve.tensor_copy(Wvo[:, 2 * c:2 * c + 2, :], PS[:, 3:5, :]), "Wvo", c)
            if c + 2 < NC:
                fold_load(c + 2)
        fold.close()
        idx.close()

        work = ExitStack()
        rc = sb(work, "rc", [P, 2, ROPE])
        rs = sb(work, "rs", [P, 2, ROPE])
        wq_b = sb(work, "wq_b", [P, QR])
        wkv_b = sb(work, "wkv_b", [P, KVR])
        ssq = sb(work, "ssq", [P, 2])
        lrstd = sb(work, "lrstd", [P, 2])
        junk = sb(work, "junk", [P, QR])
        lat = [sb(work, f"lat{i}", [P, A1N]) for i in range(4)]
        k1 = sb(work, "k1", [P, ROPE])
        k2 = sb(work, "k2", [P, ROPE])
        qlT0 = [sb(work, f"qlT0{i}", [P, P]) for i in range(2)]
        qlT1 = [sb(work, f"qlT1{i}", [QR - P, P]) for i in range(2)]
        kT = [sb(work, f"kT{i}", [P, S]) for i in range(2)]
        qtok = [sb(work, f"qtok{i}", [P, HC, P]) for i in range(2)]
        r1 = [sb(work, f"r1{i}", [P, HC, ROPE]) for i in range(2)]
        r2 = [sb(work, f"r2{i}", [P, HC, ROPE]) for i in range(2)]
        qT = [sb(work, f"qT{i}", [P, HC, P]) for i in range(2)]
        prob = [sb(work, f"prob{i}", [P, HC, S]) for i in range(2)]
        pT = [sb(work, f"pT{i}", [P, 2, HC * P]) for i in range(2)]
        nmax = [sb(work, f"nmax{i}", [P, HC]) for i in range(2)]
        psum_ = [sb(work, f"psum{i}", [P, HC]) for i in range(2)]
        rsum = [sb(work, f"rsum{i}", [P, HC]) for i in range(2)]
        oT = [sb(work, f"oT{i}", [P, H // 2, P]) for i in range(2)]
        MISC, QB, QTB, SB_, PTB, OB = 0, 1, 3, 4, 6, 3

        for n in idx_end + [("fold_vo", NC - 1), ("fold_q1", NC - 1), ("Wvo", NC - 1)]:
            need(sync, *n)
        load("rc", rc[:], a["rope_c"].rearrange("(j p) n -> p j n", p=P))
        load("rs", rs[:], a["rope_s"].rearrange("(j p) n -> p j n", p=P))
        load("wq_b", wq_b[:], a["q_norm"].partition_broadcast(P))
        load("wkv_b", wkv_b[:], a["kv_norm"].partition_broadcast(P))
        for e in (act, dve, pool, pe):
            for n in idx_end + [("fold_vo", NC - 1), ("fold_q1", NC - 1), ("Wvo", NC - 1)]:
                need(e, *n)
        xtok_view = a["x"].rearrange("(t p) n -> p t n", p=P)
        for q in range(4):
            load(("x", q), X[:, 4 * q:4 * q + 4, :], xtok_view[:, 4 * q:4 * q + 4, :])

        def pairs(ap, n):
            return ap.rearrange("p (h i two) -> p h i two", h=n, two=2)

        def latents(t):
            b, j, n = t // 2, t % 2, B + t // 2
            need(pe, "xT", n)
            need(pe, "a1w")
            if t >= 2:
                need(pe, "attn", "added", t - 2)
            if t >= 1:
                need(pe, "latT", t - 1)
            for k in range(KT):
                m = pe.matmul(PS[:, MISC, 0:A1N], XT[n % 2][:, k, j * P:(j + 1) * P], a1w[:, k, :],
                              start=(k == 0), stop=(k == KT - 1))
            sig(by_pe, m, "a1", t)
            if j == 1:
                done[("xT_used", n)] = done[("a1", t)]
                if n + 2 < 2 * B:
                    load_xT(n + 2)
            need(act, "a1", t)
            if t >= 1:
                need(act, "lat_q", t - 1)
                need(act, "lrstd", t - 1)
                need(act, "ssq2", t - 1)
            sig(by_act, act.activation(junk[:, 0:QR], PS[:, MISC, 0:QR], ACT.Square, scale=float(QR ** -0.5),
                                       accum_out=ssq[:, 0:1]), "ssq1", t)
            need(act, "ssq1", t)
            sig(by_act, act.activation(junk[:, 0:KVR], PS[:, MISC, QR:QR + KVR], ACT.Square,
                                       scale=float(KVR ** -0.5), accum_out=ssq[:, 1:2]), "ssq2", t)
            need(dve, "ssq2", t)
            sig(by_dve, dve.tensor_scalar(ssq[:], ssq[:], EPS, None, ALU.add), "ssq_eps", t)
            need(pool, "ssq_eps", t)
            need(pool, "minus_half")
            if t >= 1:
                need(pool, "lat_kv", t - 1)
            sig(by_pool, pool.tensor_tensor(lrstd[:], ssq[:], minus_half[:], ALU.pow), "lrstd", t)
            L = lat[t % 4]
            need(dve, "rc")
            need(dve, "rs")
            kp = PS[:, MISC, QR + KVR:A1N]
            sig(by_dve, dve.tensor_tensor(k1[:], kp, rc[:, j, :], ALU.mult), "k1", t)
            sig(by_dve, dve.tensor_tensor(pairs(k2[:], 1), pairs(kp, 1)[:, :, :, ::-1], pairs(rs[:, j, :], 1), ALU.mult),
                "k2", t)
            need(dve, "k2", t)
            if t >= 4:
                need(dve, "pv", NC * (2 * ((t - 4) // 2) + 2) - 1)
            sig(by_dve, dve.tensor_tensor(L[:, QR + KVR:A1N], k1[:], k2[:], ALU.add), "lat_pe", t)
            need(dve, "lrstd", t)
            need(dve, "wq_b")
            need(dve, "wkv_b")
            sig(by_dve, dve.scalar_tensor_tensor(L[:, 0:QR], PS[:, MISC, 0:QR], lrstd[:, 0:1], wq_b[:],
                                                 ALU.mult, ALU.mult), "lat_q", t)
            sig(by_dve, dve.scalar_tensor_tensor(L[:, QR:QR + KVR], PS[:, MISC, QR:QR + KVR], lrstd[:, 1:2],
                                                 wkv_b[:], ALU.mult, ALU.mult), "lat_kv", t)

        def latents_T(t):
            b, j = t // 2, t % 2
            L = lat[t % 4]
            need(pe, "lat_kv", t)
            need(pe, "ident")
            pe.transpose(PS[:, MISC, 0:P], L[:, 0:P], ident[:])
            pe.transpose(PS[:, MISC, P:2 * P], L[:, QR:A1N], ident[:])
            sig(by_pe, pe.transpose(PS[0:QR - P, MISC, 2 * P:3 * P], L[:, P:QR], ident[:]), "latT_ps", t)
            need(act, "latT_ps", t)
            if t >= 2:
                need(act, "qproj", NC * (t - 1) - 1)
            sig(by_act, act.activation(qlT0[t % 2][:], PS[:, MISC, 0:P], ACT.Copy), "qlT0", t)
            sig(by_act, act.activation(qlT1[t % 2][:], PS[0:QR - P, MISC, 2 * P:3 * P], ACT.Copy), "qlT1", t)
            if b >= 2:
                need(act, "scores", 2 * NC * (b - 1) - 1)
            sig(by_act, act.activation(kT[b % 2][:, j * P:(j + 1) * P], PS[:, MISC, P:2 * P], ACT.Copy), "latT", t)

        def q_project(i):
            t, c = divmod(i, NC)
            j = t % 2
            need(pe, "latT", t)
            need(pe, "Wq0_pe")
            need(pe, "Wq1_pe")
            if i >= 2:
                need(pe, "q_abs", i - 2)
                need(pe, "r2", i - 2)
            bank = PS[:, QB + i % 2, :]
            pe.matmul(bank, qlT0[t % 2][:], Wq0[:, c, :], start=True, stop=False)
            sig(by_pe, pe.matmul(bank, qlT1[t % 2][:], Wq1[:, c, :], start=False, stop=True), "qproj", i)
            need(dve, "qproj", i)
            if i >= 2:
                need(dve, "q_pe", i - 2)
            qp = pairs(bank[:, 256:512], HC)
            cb = pairs(rc[:, j, :], 1).broadcast_to([P, HC, ROPE // 2, 2])
            sb_ = pairs(rs[:, j, :], 1).broadcast_to([P, HC, ROPE // 2, 2])
            sig(by_dve, dve.tensor_tensor(r1[i % 2][:].rearrange("p h (i two) -> p h i two", two=2), qp, cb, ALU.mult),
                "r1", i)
            sig(by_dve, dve.tensor_tensor(r2[i % 2][:].rearrange("p h (i two) -> p h i two", two=2),
                                          qp[:, :, :, ::-1], sb_, ALU.mult), "r2", i)
            need(act, "r2", i)
            if i >= 2:
                need(act, "qtrans", i - 2)
            sig(by_act, act.activation(qtok[i % 2][:, :, 0:KVR],
                                       bank[:, 0:256].rearrange("p (h n) -> p h n", h=HC), ACT.Copy), "q_abs", i)
            need(pool, "r2", i)
            if i >= 2:
                need(pool, "qtrans", i - 2)
            sig(by_pool, pool.tensor_tensor(qtok[i % 2][:, :, KVR:P], r1[i % 2][:], r2[i % 2][:], ALU.add), "q_pe", i)

        def q_transpose(i):
            need(pe, "q_abs", i)
            need(pe, "q_pe", i)
            if i >= 1:
                need(pe, "qT", i - 1)
            if i >= 3:
                need(pe, "oT", i - 3)
            for h in range(HC):
                m = pe.transpose(PS[:, QTB, h * P:(h + 1) * P], qtok[i % 2][:, h, :], ident[:])
            sig(by_pe, m, "qtrans", i)
            need(dve, "qtrans", i)
            if i >= 2:
                need(dve, "scores", i - 2)
            sig(by_dve, dve.tensor_copy(qT[i % 2][:], PS[:, QTB, :].rearrange("p (h n) -> p h n", h=HC)), "qT", i)

        def scores(i):
            t, c = divmod(i, NC)
            b, j = divmod(t, 2)
            nk = P * (j + 1)
            need(pe, "qT", i)
            if i >= 1:
                need(pe, "masked", i - 1)
            bank = PS[:, SB_:SB_ + 2, :].rearrange("p a (h n) -> p (a h) n", h=2)
            for h in range(HC):
                m = pe.matmul(bank[:, h, 0:nk], qT[i % 2][:, h, :], kT[b % 2][:, 0:nk], start=True, stop=True)
            sig(by_pe, m, "scores", i)
            need(dve, "scores", i)
            if i >= 2:
                need(dve, "ptrans", i - 2)
            if j:
                need(dve, "mask1", b)
                mask = mask1[:, b, :]
            else:
                need(dve, "mask0")
                mask = mask0[:]
            for h in range(HC):
                ins = dve.tensor_tensor_reduce(prob[i % 2][:, h, 0:nk], bank[:, h, 0:nk], mask, -QSCALE, 3.0e38,
                                               ALU.add, ALU.min, nmax[i % 2][:, h:h + 1])
            sig(by_dve, ins, "masked", i)

        def exps(i):
            j = i // NC % 2
            nk = P * (j + 1)
            need(act, "masked", i)
            if i >= 2:
                need(act, "rsum", i - 2)
            for h in range(HC):
                p = prob[i % 2][:, h, 0:nk]
                ins = act.activation(p, p, ACT.Exp, bias=nmax[i % 2][:, h:h + 1], scale=-1.0,
                                     accum_out=psum_[i % 2][:, h:h + 1])
            sig(by_act, ins, "exp", i)
            need(dve, "exp", i)
            if i >= 2:
                need(dve, "prob", i - 2)
            sig(by_dve, dve.reciprocal(rsum[i % 2][:], psum_[i % 2][:]), "rsum", i)
            need(pool, "rsum", i)
            p = prob[i % 2][:, :, 0:nk]
            sig(by_pool, pool.tensor_tensor(p, p, rsum[i % 2][:].unsqueeze(2).broadcast_to([P, HC, nk]), ALU.mult),
                "prob", i)

        ORDER = (0, 2, 1, 3)

        def p_transpose(i):
            j = i // NC % 2
            need(pe, "prob", i)
            if i >= 1:
                need(pe, "pT", i - 1)
            for blk in range(j + 1):
                for s, h in enumerate(ORDER):
                    m = pe.transpose(PS[:, PTB + blk, s * P:(s + 1) * P],
                                     prob[i % 2][:, h, blk * P:(blk + 1) * P], ident[:])
            sig(by_pe, m, "ptrans", i)
            need(act, "ptrans", i)
            if i >= 2:
                need(act, "pv", i - 2)
            sig(by_act, act.activation(pT[i % 2][:, 0:j + 1, :], PS[:, PTB:PTB + j + 1, :], ACT.Copy), "pT", i)

        def attend(i):
            t, c = divmod(i, NC)
            b, j = divmod(t, 2)
            need(pe, "pT", i)
            if i >= 1:
                need(pe, "oT", i - 1)
            need(pe, "qT", min(i + 2, NT * NC - 1))
            for odd in range(2):
                for blk in range(j + 1):
                    m = pe.matmul(PS[KVR * odd:KVR * (odd + 1), OB, 0:2 * P],
                                  lat[(2 * b + blk) % 4][:, QR:QR + KVR],
                                  pT[i % 2][:, blk, 2 * P * odd:2 * P * (odd + 1)], start=(blk == 0), stop=(blk == j))
            sig(by_pe, m, "pv", i)
            need(dve, "pv", i)
            if t >= 2:
                need(dve, "oproj", t - 2)
            sig(by_dve, dve.tensor_copy(oT[t % 2][:, 2 * c:2 * c + 2, :],
                                        PS[:, OB, 0:2 * P].rearrange("p (a n) -> p a n", a=2)), "oT", i)

        def o_project(t):
            need(pe, "oT", NC * (t + 1) - 1)
            need(pe, "latT", min(t + 1, NT - 1))
            for q in range(H // 2):
                m = pe.matmul(PS[:, MISC, :], oT[t % 2][:, q, :], Wvo[:, q, :], start=(q == 0), stop=(q == H // 2 - 1))
            sig(by_pe, m, "oproj", t)
            layer_norm(t, PS[:, MISC, :], "attn", ("oproj", t), extra=("x", t // 4))

        latents(0)
        latents_T(0)
        N = NT * NC
        q_project(0)
        q_project(1)
        q_transpose(0)
        for i in range(N + 1):
            t, c = divmod(i, NC)
            if i < N:
                scores(i)
            if c == 1 and t >= 1:
                o_project(t - 1)
            if i >= 1:
                p_transpose(i - 1)
            if i + 2 < N:
                q_project(i + 2)
            if i + 1 < N:
                q_transpose(i + 1)
            if i >= 1:
                attend(i - 1)
            if i < N:
                exps(i)
            if c == 2 and t + 1 < NT:
                latents(t + 1)
            if c == 4 and t + 1 < NT:
                latents_T(t + 1)
        o_project(NT - 1)
        attn_end = [("oproj", NT - 1), ("attn", "normed", NT - 1), ("pT", N - 1), ("oT", N - 1), ("prob", N - 1)]
        work.close()
        attn.close()

        l1w = ExitStack()
        wqkv = sb(l1w, "wqkv", [P, KT, D + 2 * P])
        wo = sb(l1w, "wo", [P, KT, D])
        bo_b = sb(l1w, "bo_b", [P, D])
        Wf = sb(l1w, "Wf", [P, KT, D])
        ffn = ExitStack()
        sq = [sb(ffn, f"sq{i}", [P, D]) for i in range(2)]
        la = sb(ffn, "la", [R, D])
        lb = sb(ffn, "lb", [R, D])
        mag = sb(ffn, "mag", [P, D])
        crow = sb(ffn, "crow", [P, D])
        ones = sb(ffn, "ones", [P, P])
        Wg = sb(ffn, "Wg", [P, FM, KT, P])
        Wu = sb(ffn, "Wu", [P, FM, KT, P])
        Wd = sb(ffn, "Wd", [P, FM, D])
        nib = sb(ffn, "nib", [P, 512], I32)
        znib = sb(ffn, "znib", [P, 512], I32)
        zsh = sb(ffn, "zsh", [P, 512], I32)
        diff = [sb(ffn, f"diff{i}", [P, 512]) for i in range(2)]
        x1T = [sb(ffn, f"x1T{i}", [P, KT, QUARTER]) for i in range(2)]
        inter = sb(ffn, "inter", [P, FM, QUARTER])
        gate = [sb(ffn, f"gate{i}", [P, QUARTER]) for i in range(2)]
        y16 = [sb(ffn, f"y16{i}", [P, D], F16) for i in range(2)]

        load("nib_par", nib_par[:], a["nib_par"])
        order = [u for m in range(FM) for u in (m, FM + m)] + [2 * FM + m for m in range(FM)]

        def load_unit(n, before_scales=None):
            v, i = order[n], n % 2
            load(("qpack", n), qpack[i][:], a["qpack"][v])
            load(("zrep", n), zrep[i][:], a["zrep"][v].partition_broadcast(P))
            if before_scales:
                need(sync, *before_scales)
            load(("gsc", n), gsc[i][:], a["gsc"][v].partition_broadcast(P))

        load_unit(0)
        load_unit(1)
        for e in (sync, act, dve, pool, pe):
            for n in attn_end:
                need(e, *n)
        load("zsh", zsh[:], a["zsh"].partition_broadcast(P))

        def rows_of(ap):
            return ap.rearrange("(k p) n -> p k n", p=P)

        def load_layer1():
            load("la", la[:], a["lora_A"])
            load("lb", lb[:], a["lora_BT"])
            load("WfT", Wf[:], rows_of(a["ffnWT"]))
            load("mag", mag[:], a["mag"].partition_broadcast(P))
            load("wqkv", wqkv[:], rows_of(a["wqkv"]))
            load("wo", wo[:], rows_of(a["woT"]))
            load("bo_b", bo_b[:], a["bo"].partition_broadcast(P))

        def dequant(n):
            u, i = order[n], n % 2
            kind, m = divmod(u, FM)
            dst = Wd[:, m, :] if kind == 2 else (Wg, Wu)[kind][:, m, :, :].rearrange("p k n -> p (k n)")
            for w in ("qpack", "zrep", "gsc"):
                need(dve, w, n)
            need(dve, "nib_par")
            need(dve, "zsh")
            if n >= 1:
                need(dve, "diff", n - 1)
            sig(by_dve, dve.tensor_scalar(nib[:], qpack[i][:], nib_par[:, 0:1], nib_par[:, 1:2],
                                          ALU.bitwise_and, ALU.logical_shift_right), "nib", n)
            sig(by_dve, dve.tensor_tensor(znib[:], zrep[i][:], zsh[:], ALU.logical_shift_right), "zs", n)
            need(dve, "zs", n)
            sig(by_dve, dve.tensor_scalar(znib[:], znib[:], 15, None, ALU.bitwise_and), "znib", n)
            need(dve, "znib", n)
            if n >= 2:
                need(dve, "weight", n - 2)
            sig(by_dve, dve.scalar_tensor_tensor(diff[i][:], nib[:], 1.0, znib[:], ALU.subtract, ALU.subtract),
                "diff", n)
            need(pool, "diff", n)
            need(pool, "gsc", n)
            sig(by_pool, pool.tensor_tensor(dst, diff[i][:], gsc[i][:], ALU.mult), "weight", n)
            done[("unit", u)] = done[("weight", n)]
            if n + 2 < UNITS:
                need(sync, "diff", n)
                load_unit(n + 2, ("weight", n))

        XB, WB, GB, UB, DB = 0, 1, 2, 4, 6

        def adapt_steps():
            def product(k):
                if k == 0:
                    sig(by_pool, pool.memset(ones[:], 1.0), "ones")
                    need(pe, "la")
                    need(pe, "lb")
                else:
                    need(pe, "effW", k - 1)
                sig(by_pe, pe.matmul(PS[:, WB, :], la[:, k * P:(k + 1) * P], lb[:], start=True, stop=True), "BA", k)
                need(dve, "BA", k)
                need(dve, "WfT")
                sig(by_dve, dve.tensor_tensor(Wf[:, k, :], Wf[:, k, :], PS[:, WB, :], ALU.add), "effW", k)

            def square(k):
                if k == 0:
                    need(pe, "effW", KT - 1)
                    need(pe, "ones")
                need(act, "effW", k)
                if k >= 2:
                    need(act, "norm2", k - 2)
                sig(by_act, act.activation(sq[k % 2][:], Wf[:, k, :], ACT.Square), "effW2", k)

            def total(k):
                need(pe, "effW2", k)
                sig(by_pe, pe.matmul(PS[:, WB, :], ones[:], sq[k % 2][:], start=(k == 0), stop=(k == KT - 1)),
                    "norm2", k)

            def root():
                need(dve, "norm2", KT - 1)
                sig(by_dve, dve.tensor_copy(crow[:], PS[:, WB, :]), "crow")
                need(pool, "crow")
                need(pool, "mag")
                sig(by_pool, pool.tensor_tensor(crow[:], crow[:], minus_half[:, 0:1].broadcast_to([P, D]), ALU.pow),
                    "crow_r")
                need(pool, "crow_r")
                sig(by_pool, pool.tensor_tensor(crow[:], crow[:], mag[:], ALU.mult), "crow_m")

            def scale():
                need(dve, "crow_m")
                sig(by_dve, dve.tensor_tensor(Wf[:], Wf[:], crow[:].unsqueeze(1).broadcast_to([P, KT, D]), ALU.mult),
                    "Wf")
            steps = [lambda k=k: product(k) for k in range(KT)]
            steps += [lambda: square(0), lambda: square(1), lambda: total(0), lambda: square(2), lambda: total(1),
                      lambda: square(3), lambda: total(2), lambda: total(3), root, scale]
            return steps

        def x1_transpose(t):
            q = t // 4
            need(pe, "attn", "normed", t)
            if t >= 1:
                need(pe, "x1T", t - 1)
            for k in range(KT):
                m = pe.transpose(PS[:, XB, k * P:(k + 1) * P], X[:, t, k * P:(k + 1) * P], ident[:])
            sig(by_pe, m, "x1T_ps", t)
            need(act, "x1T_ps", t)
            if q >= 2:
                need(act, "gu", FM * (q - 1) - 1)
            sig(by_act, act.activation(x1T[q % 2][:, :, (t % 4) * P:(t % 4 + 1) * P],
                                       PS[:, XB, :].rearrange("p (k n) -> p k n", k=KT), ACT.Copy), "x1T", t)

        def gate_up(q, m):
            M = P if m < FM - 1 else FLAST
            s = q * FM + m
            need(pe, "unit", m)
            need(pe, "unit", FM + m)
            need(pe, "x1T", 4 * q + 3)
            if s >= 2:
                need(pe, "inter", s - 2)
            for W, bk in ((Wg, GB), (Wu, UB)):
                for k in range(KT):
                    ins = pe.matmul(PS[0:M, bk + s % 2, :], W[:, m, k, 0:M], x1T[q % 2][:, k, :],
                                    start=(k == 0), stop=(k == KT - 1))
            sig(by_pe, ins, "gu", s)
            need(act, "gu", s)
            if s >= 2:
                need(act, "inter", s - 2)
            sig(by_act, act.activation(gate[s % 2][0:M, :], PS[0:M, GB + s % 2, :], ACT.Silu), "silu", s)
            need(dve, "silu", s)
            if q:
                need(dve, "down", 4 * q - 1)
            sig(by_dve, dve.tensor_tensor(inter[0:M, m, :], gate[s % 2][0:M, :], PS[0:M, UB + s % 2, :], ALU.mult),
                "inter", s)

        def down(t):
            need(pe, "inter", FM * (t // 4 + 1) - 1)
            if t >= 2:
                need(pe, "y16", t - 2)
            for m in range(FM):
                M = P if m < FM - 1 else FLAST
                need(pe, "unit", 2 * FM + m)
                ins = pe.matmul(PS[:, DB + t % 2, :], inter[0:M, m, (t % 4) * P:(t % 4 + 1) * P], Wd[0:M, m, :],
                                start=(m == 0), stop=(m == FM - 1))
            sig(by_pe, ins, "down", t)
            need(act, "down", t)
            if t >= 2:
                need(act, "ffn", "added", t - 2)
            sig(by_act, act.activation(y16[t % 2][:], PS[:, DB + t % 2, :], ACT.Copy), "y16", t)
            layer_norm(t, y16[t % 2][:], "ffn", ("y16", t))

        for n in range(4):
            dequant(n)
        made = 4
        for t in range(4):
            x1_transpose(t)
        side = adapt_steps()
        for q in range(4):
            for m in range(FM):
                gate_up(q, m)
                for _ in range(3):
                    if made < UNITS:
                        dequant(made)
                        made += 1
                if q == 0 and m == FM - 1:
                    load_layer1()
                if q >= 1 and side:
                    side.pop(0)()
                if q < 3 and m >= 6 and m < 10:
                    x1_transpose(4 * (q + 1) + m - 6)
            for t in range(4 * q, 4 * q + 4):
                down(t)
        assert not side and made == UNITS
        ffn_end = [("ffn", "normed", NT - 1), ("down", NT - 1), ("weight", UNITS - 1), ("Wf",),
                   ("ffn", "rstd", NT - 1)]
        ffn.close()

        gqa = ExitStack()
        hpar = sb(gqa, "hpar", [P, 2])
        x2T = sb(gqa, "x2T", [P, KT, S])
        qhi = sb(gqa, "qhi", [P, G, S], F32R)
        qlo = sb(gqa, "qlo", [P, G, S], F32R)
        khi = sb(gqa, "khi", [P, 2, S], F32R)
        klo = sb(gqa, "klo", [P, 2, S], F32R)
        khr = sb(gqa, "khr", [P, S], F32R)
        klr = sb(gqa, "klr", [P, S])
        qs = [sb(gqa, f"qs{i}", [P, KVH // 2, G, S], F32R) for i in range(2)]
        ks = [sb(gqa, f"ks{i}", [P, KVH // 2, 2, S], F32R) for i in range(2)]
        v32 = [sb(gqa, f"v32{i}", [P, 2, KVH, 32]) for i in range(3)]
        gmax = [sb(gqa, f"gmax{i}", [P, 2, KVH // 2, G]) for i in range(2)]
        kones_f = sb(gqa, "kones_f", [P, 2, S])
        mT = sb(gqa, "mT", [KVH * G, P])
        mhi = [sb(gqa, f"mhi{i}", [KVH * G, P], F32R) for i in range(2)]
        mlo = [sb(gqa, f"mlo{i}", [KVH * G, P], F32R) for i in range(2)]
        gp = [sb(gqa, f"gp{i}", [P, 2, G * P]) for i in range(KVH)]
        yraw = [sb(gqa, f"yraw{i}", [P, G * P]) for i in range(2)]
        grs = sb(gqa, "grs", [P, G, 4])
        ytok = [sb(gqa, f"ytok{i}", [P, D]) for i in range(2)]
        yT = [sb(gqa, f"yT{i}", [P, KT, P]) for i in range(2)]
        x3T = [sb(gqa, f"x3T{i}", [P, KT, P]) for i in range(2)]
        for e in (sync, act, dve, pool, pe):
            for n in ffn_end:
                need(e, *n)
        load("hpar", hpar[:], a["hpar"])
        load("kones_f", kones_f[96:P], a["kones"])
        need(dve, "kones_f")
        for i in range(2):
            sig(by_dve, dve.tensor_copy(ks[i][96:P], kones_f[96:P].unsqueeze(1).broadcast_to([32, KVH // 2, 2, S])),
                "kones", i)
            sig(by_dve, dve.tensor_scalar(qs[i][96:P].rearrange("p h (a g) n -> p h a (g n)", a=2),
                                          kones_f[96:P].rearrange("p a n -> p (a n)").unsqueeze(1).unsqueeze(1)
                                          .broadcast_to([32, KVH // 2, 2, 2 * S]), 0.0, None, ALU.mult), "qs_zeros", i)
        for i in range(3):
            sig(by_pool, pool.memset(v32[i][:], 0.0), "v32_zeros", i)
            need(pool, "v32_zeros", i)
            sig(by_pool, pool.memset(v32[i][:, :, :, HD:HD + 1], 1.0), "v32_ones", i)

        TB2, PJ, GS, GT, GY, OUT = 0, 1, 2, 4, 6, 7
        mcount, pcount, ocount = [0], [0], [0]
        deferred = []

        def flush():
            while deferred:
                deferred.pop(0)()

        def misc_turn(eng, track, name, transposes_, evacuate, ready, before=()):
            c = mcount[0]
            mcount[0] += 1
            bank = PS[:, TB2, :]
            for n in ready:
                if n not in done:
                    flush()
                need(pe, *n)
            if c >= 1:
                if ("misc", c - 1) not in done:
                    flush()
                need(pe, "misc", c - 1)
            sig(by_pe, transposes_(bank), "misc_ps", c)

            def drain():
                need(eng, "misc_ps", c)
                for n in before:
                    if n in done:
                        need(eng, *n)
                sig(track, evacuate(bank), "misc", c)
                done[name] = done[("misc", c)]
            deferred.append(drain)

        def transpose_tile(name, t, src, ready, dst, before):
            def go(bank):
                for k in range(KT):
                    m = pe.transpose(bank[:, k * P:(k + 1) * P], src[:, k * P:(k + 1) * P], ident[:])
                return m
            misc_turn(act, by_act, (name, t), go,
                      lambda bank: act.activation(dst, bank.rearrange("p (k n) -> p k n", k=KT), ACT.Copy),
                      [ready], before)

        def bank1_turn():
            if pcount[0]:
                if ("bank1", pcount[0] - 1) not in done:
                    flush()
                need(pe, "bank1", pcount[0] - 1)
            pcount[0] += 1
            return pcount[0] - 1

        def split_stack(b, src_hi, src_lo, dst, kinds, name):
            for p2 in range(KVH // 2):
                for part, kind in enumerate(kinds):
                    src = (src_hi, src_lo)[kind]
                    load((name, "part"), dst[32 * part:32 * part + 32, p2].bitcast(F32),
                         src[32 * p2:32 * p2 + 32].bitcast(F32), group=(name, 4 * b + p2))

        def stacked(eng, name, b):
            for p2 in range(KVH // 2):
                need(eng, name, 4 * b + p2)

        def ready_x2T(b):
            if ("x2T", 2 * b + 1) not in done:
                flush()
            need(pe, "x2T", 2 * b + 1)
            need(pe, "wqkv")

        def qkv_q(b, g):
            turn = bank1_turn()
            ready_x2T(b)
            for k in range(KT):
                m = pe.matmul(PS[:, PJ, 0:S], wqkv[:, k, g * P:(g + 1) * P], x2T[:, k, :], start=(k == 0), stop=(k == KT - 1))
            sig(by_pe, m, "q_ps", b, g)

            def parts():
                need(act, "q_ps", b, g)
                if b >= 1:
                    stacked(act, "qs", b - 1)
                    stacked(dve, "qs", b - 1)
                sc = float(HD ** -0.5)
                sig(by_act, act.activation(qhi[:, g, :], PS[:, PJ, 0:S], ACT.Copy, scale=sc), "qhi", b, g)
                need(dve, "qhi", b, g)
                sig(by_dve, dve.scalar_tensor_tensor(qlo[:, g, :], PS[:, PJ, 0:S], sc, qhi[:, g, :].bitcast(F32),
                                                     ALU.mult, ALU.subtract), "qlo", b, g)
                done[("bank1", turn)] = done[("qlo", b, g)]
            deferred.append(parts)

        def qkv_k(b):
            turn = bank1_turn()
            ready_x2T(b)
            for k in range(KT):
                m = pe.matmul(PS[:, PJ, 0:S], wqkv[:, k, D:D + P], x2T[:, k, :], start=(k == 0), stop=(k == KT - 1))
            sig(by_pe, m, "k_ps", b)

            def parts():
                need(dve, "k_ps", b)
                need(dve, "hpar")
                if b >= 1:
                    stacked(dve, "ks", b - 1)
                    need(dve, "klo", b - 1)
                sig(by_dve, dve.tensor_copy(khr[:], PS[:, PJ, 0:S]), "khr", b)
                need(dve, "khr", b)
                sig(by_dve, dve.tensor_tensor(klr[:], PS[:, PJ, 0:S], khr[:].bitcast(F32), ALU.subtract), "klr", b)
                done[("bank1", turn)] = done[("klr", b)]
                need(dve, "klr", b)
                for p in range(2):
                    sig(by_dve, dve.tensor_scalar(khi[:, p, :], khr[:].bitcast(F32), hpar[:, p:p + 1], None, ALU.mult), "khi", b)
                    sig(by_dve, dve.tensor_scalar(klo[:, p, :], klr[:], hpar[:, p:p + 1], None, ALU.mult), "klo", b)
            deferred.append(parts)

        def qkv_v(b):
            turn = bank1_turn()
            for blk in range(2):
                for k in range(KT):
                    m = pe.matmul(PS[:, PJ, blk * P:(blk + 1) * P], x2T[:, k, blk * P:(blk + 1) * P],
                                  wqkv[:, k, D + P:D + 2 * P], start=(k == 0), stop=(k == KT - 1))
            sig(by_pe, m, "v_ps", b)

            def evacuate():
                need(act, "v_ps", b)
                need(act, "v32_ones", b % 3)
                if b >= 3:
                    need(act, "gpv", 2 * 2 * (b - 2) - 1)
                sig(by_act, act.activation(v32[b % 3][:, :, :, 0:HD],
                                           PS[:, PJ, 0:S].rearrange("p (b h d) -> p b h d", b=2, d=HD), ACT.Copy), "v32", b)
                done[("bank1", turn)] = done[("v32", b)]
            deferred.append(evacuate)

        def stack_free(b):
            if b >= 2:
                need(sync, "gst_blk", 2 * (16 * (b - 1) - 1) + 1)
            if b >= 1:
                need(sync, "gs", 2 * (16 * (b - 1) + 7) + 1)

        def stack_q(b):
            need(sync, "qhi", b, G - 1)
            need(sync, "qlo", b, G - 1)
            split_stack(b, qhi, qlo, qs[b % 2], (0, 0, 1), "qs")

        def stack_k(b):
            need(sync, "khi", b)
            need(sync, "klo", b)
            split_stack(b, khi, klo, ks[b % 2], (0, 1, 0), "ks")

        def row_maxima(i):
            t, r = divmod(i, 8)
            b, j = divmod(t, 2)
            p2, g0 = r // 2, 2 * (r % 2)
            need(pe, "qs", 4 * b + p2)
            need(pe, "ks", 4 * b + p2)
            if t >= 2:
                need(dve, "mT", t - 2)
            for g in (g0, g0 + 1):
                a_ = g % 2
                if i >= 1:
                    need(pe, "gmax", 2 * (i - 1) + a_)
                sig(by_pe, pe.matmul(PS[:, GS + a_, :], qs[b % 2][0:96, p2, g, j * P:(j + 1) * P],
                                     ks[b % 2][0:96, p2, :, :].rearrange("p a n -> p (a n)"), start=True, stop=True),
                    "gs", 2 * i + a_)
                need(dve, "gs", 2 * i + a_)
                sig(by_dve, dve.tensor_reduce(gmax[t % 2][:, :, p2, g],
                                              PS[:, GS + a_, :].rearrange("p (h n) -> p h n", h=2),
                                              AX.X, ALU.max, negate=True), "gmax", 2 * i + a_)

        def max_rows(t):
            b, j = divmod(t, 2)
            misc_turn(dve, by_dve, ("mT", t),
                      lambda bank: pe.transpose(bank[0:KVH * G, 0:P], gmax[t % 2][:].rearrange("p a h g -> p (a h g)"), ident[:]),
                      lambda bank: dve.tensor_copy(mT[:], bank[0:KVH * G, 0:P]),
                      [("gmax", 16 * t + 15)], [("mlo", t - 1), ("mhi", t - 1)])
            flush()
            need(dve, "mT", t)
            if t >= 2:
                need(dve, "mrow", t - 2)
            sig(by_dve, dve.tensor_copy(mhi[t % 2][:], mT[:]), "mhi", t)
            need(dve, "mhi", t)
            sig(by_dve, dve.tensor_tensor(mlo[t % 2][:], mT[:], mhi[t % 2][:].bitcast(F32), ALU.subtract), "mlo", t)
            if t >= 4:
                need(sync, "gst_blk", 2 * (8 * (t - 3) - 1) + 1)
            need(sync, "mlo", t)
            need(sync, "qs_zeros", b % 2)
            for part, m in enumerate((mhi, mlo)):
                load(("mrow", "part"), qs[b % 2][96 + 2 * part:98 + 2 * part, :, :, j * P:(j + 1) * P].bitcast(F32),
                     m[t % 2][:].bitcast(F32), group=("mrow", t))

        def transposed_scores(i):
            t, h = divmod(i, 8)
            b, j = divmod(t, 2)
            need(pe, "qs", 4 * b + h // 2)
            need(pe, "mrow", t)
            need(pe, "kones", b % 2)
            for blk in range(2):
                if i >= 1:
                    need(pe, "gexp", 2 * (i - 1) + blk)
                bank = PS[:, GT + blk, :]
                m = pe.matmul(bank, ks[b % 2][:, h // 2, h % 2, blk * P:(blk + 1) * P],
                              qs[b % 2][:, h // 2, :, j * P:(j + 1) * P], start=True, stop=True)
                sig(by_pe, m, "gst_blk", 2 * i + blk)
                need(act, "gst_blk", 2 * i + blk)
                if t >= 1:
                    need(act, "gpv", 2 * (t - 1) + h // 4)
                sig(by_act, act.activation(gp[h][:, blk, :], bank, ACT.Exp), "gexp", 2 * i + blk)

        def g_attend(t, u, blk):
            b, j = divmod(t, 2)
            need(pe, "gexp", 2 * (8 * t + 4 * u + 3) + 1)
            need(pe, "v32", b)
            if 2 * t + u >= 1:
                need(pe, "yraw", 2 * t + u - 1)
            for c in range(4):
                m = pe.matmul(PS[32 * c:32 * c + 32, GY, :], v32[b % 3][:, blk, 4 * u + c, :],
                              gp[4 * u + c][:, blk, :], start=(blk == 0), stop=(blk == 1))
            if blk == 1:
                sig(by_pe, m, "gpv", 2 * t + u)
                deferred.append(lambda: g_evacuate(t, u))

        def g_evacuate(t, u):
            need(act, "gpv", 2 * t + u)
            if t >= 1:
                need(act, "ytok", 2 * (t - 1) + u)
            sig(by_act, act.activation(yraw[u][:], PS[:, GY, :], ACT.Copy), "yraw", 2 * t + u)

        def g_normalise(t, u):
            def transposes(bank):
                for g in range(G):
                    m = pe.transpose(bank[:, g * P:(g + 1) * P], yraw[u][:, g * P:(g + 1) * P], ident[:])
                return m

            def divide(bank):
                y = bank.rearrange("p (g h d) -> p g h d", g=G, d=32)
                if 2 * t + u >= 1:
                    need(dve, "ytok", 2 * t + u - 1)
                sig(by_dve, dve.reciprocal(grs[:].unsqueeze(3), y[:, :, :, HD:HD + 1]), "grs", t, u)
                need(dve, "grs", t, u)
                dst = ytok[t % 2][:, u * 256:(u + 1) * 256].rearrange("p (h g d) -> p g h d", g=G, d=HD)
                for g in range(G):
                    m = dve.tensor_tensor(dst[:, g], y[:, g, :, 0:HD],
                                          grs[:, g].unsqueeze(2).broadcast_to([P, 4, HD]), ALU.mult)
                    if g < G - 1:
                        sig(by_dve, m, "ytok_part")
                return m
            misc_turn(dve, by_dve, ("ytok", 2 * t + u), transposes, divide, [("yraw", 2 * t + u)], [("yT", t - 2)])

        def add_bias(t):
            need(pool, "bo_b")
            need(pool, "x2T", t)
            sig(by_pool, pool.tensor_tensor(X[:, t, :], X[:, t, :], bo_b[:], ALU.add), "x_bo", t)

        def y_transpose(t):
            transpose_tile("yT", t, ytok[t % 2], ("ytok", 2 * t + 1), yT[t % 2][:], [("g_out", t - 2)])

        def product(t, part, xT, W, name, tag, extra=None, then=None):
            if part == 0:
                for n in (xT[0], W[0]) + ((("out_bank", ocount[0] - 1),) if ocount[0] else ()):
                    if n not in done:
                        flush()
                    need(pe, *n)
            for k in range(KT // 2 * part, KT // 2 * (part + 1)):
                m = pe.matmul(PS[:, OUT, :], xT[1][:, k, :], W[1][:, k, :], start=(k == 0), stop=(k == KT - 1))
            if part == 0:
                return
            sig(by_pe, m, name, t)
            turn = ocount[0]
            ocount[0] += 1

            def norm():
                layer_norm(t, PS[:, OUT, :], tag, (name, t), extra=extra)
                done[("out_bank", turn)] = done[(tag, "added", t)]
                if then:
                    then()
            deferred.append(norm)

        out_view = out.rearrange("(t p) n -> p t n", p=P)

        def g_output(t, part):
            product(t, part, (("yT", t), yT[t % 2]), (("wo",), wo), "g_out", "gqa", extra=("x_bo", t))

        def linear1(t):
            transpose_tile("x3T", t, X[:, t, :], ("gqa", "normed", t), x3T[t % 2][:], [("lin", t - 2)])

        def linear2(t, part):
            def store():
                need(sync, "lin_ln", "normed", t)
                load(("store", t), out_view[:, t, :], X[:, t, :])
            product(t, part, (("x3T", t), x3T[t % 2]), (("Wf",), Wf), "lin", "lin_ln", then=store)

        def x2_transpose(t):
            transpose_tile("x2T", t, X[:, t, :], ("ffn", "normed", t),
                           x2T[:, :, (t % 2) * P:(t % 2 + 1) * P], [("v_ps", t // 2 - 1), ("q_ps", t // 2 - 1, G - 1)])

        def stack(b):
            flush()
            stack_free(b)
            stack_k(b)
            stack_q(b)

        AHEAD = 10

        def tile_work(t, h):
            p = t - 1
            if h < 2:
                if h == 0 and p >= 1:
                    linear1(p - 1)
                if p >= 0:
                    g_attend(p, 1, h)
            if h == 2 and p >= 0:
                g_normalise(p, 1)
                add_bias(p)
            if h in (2, 3) and p >= 1:
                linear2(p - 1, h - 2)
            if h == 3 and p >= 0:
                y_transpose(p)
            if h in (4, 5):
                if t < NT:
                    g_attend(t, 0, h - 4)
                if p >= 0:
                    g_output(p, h - 4)
            if h == 6 and t < NT:
                g_normalise(t, 0)

        def sequence_work(b, step):
            if step in (1, 4):
                x2_transpose(2 * b + (step == 4))
            if step == 6:
                qkv_k(b)
            if step == 7:
                qkv_v(b)
            if step in (8, 9, 14, 15):
                qkv_q(b, (8, 9, 14, 15).index(step))

        for step in range(16):
            sequence_work(0, step)
        stack(0)
        for step in range(8):
            sequence_work(1, step)
        flush()
        for i in range(AHEAD):
            row_maxima(i)
            if i < 8:
                sequence_work(1, 8 + i)
            flush()
            if i % 8 == 7:
                max_rows(i // 8)
        for i in range(8 * NT):
            t, h = divmod(i, 8)
            b, step = divmod(i, 16)
            transposed_scores(i)
            if i + AHEAD < 8 * NT:
                row_maxima(i + AHEAD)
            tile_work(t, h)
            if step == 0 and b + 1 < B:
                stack(b + 1)
            if b + 2 < B:
                sequence_work(b + 2, step)
            flush()
            if i + AHEAD < 8 * NT and (i + AHEAD) % 8 == 7:
                max_rows((i + AHEAD) // 8)
        for h in range(6):
            tile_work(NT, h)
        flush()
        linear1(NT - 1)
        for part in range(2):
            linear2(NT - 1, part)
        flush()
        for t in range(NT):
            need(sync, "store", t)
        gqa.close()
        l1w.close()


def kernel(**inputs):
    import concourse.bacc as bacc
    from concourse.bass_utils import run_bass_kernel_spmd

    g = {k: np.asarray(v) for k, v in inputs.items()}
    f32 = np.float32
    arrays = {}
    x = g["L0_attn_hidden_states"].reshape(TOK, D)
    arrays["x"] = x
    arrays["xT"] = x.T
    arrays["wk_i"] = g["L0_attn_idx_wk_w"]
    arrays["ww_i"] = g["L0_attn_idx_weights_w"]
    arrays["wq_i"] = g["L0_attn_idx_wq_w"]
    arrays["a1w"] = np.concatenate([g["L0_attn_q_a_w"], g["L0_attn_kv_a_w"]], axis=1)
    qb = g["L0_attn_q_b_w"].reshape(QR, H, NOPE + ROPE)
    arrays["q_pe_w"] = qb[:, :, NOPE:].reshape(QR, H * ROPE)
    arrays["qnT"] = qb[:, :, :NOPE].transpose(2, 1, 0)
    kvb = g["L0_attn_kv_b_w"].reshape(KVR, H, NOPE + VD)
    arrays["wkT"] = kvb[:, :, :NOPE].transpose(2, 1, 0)
    arrays["wvT"] = kvb[:, :, NOPE:].transpose(2, 1, 0)
    arrays["o_w"] = g["L0_attn_o_w"]
    arrays["q_norm"] = g["L0_attn_q_a_norm_w"]
    arrays["kv_norm"] = g["L0_attn_kv_a_norm_w"]
    inv = (f32(1.0) / f32(10000.0) ** (np.arange(0, ROPE, 2, dtype=f32) / f32(ROPE))).astype(f32)
    ang = np.arange(S, dtype=f32)[:, None] * inv[None, :]
    arrays["rope_c"] = np.repeat(np.cos(ang), 2, axis=1).astype(f32)
    arrays["rope_s"] = np.stack([-np.sin(ang), np.sin(ang)], axis=2).reshape(S, ROPE).astype(f32)
    q, k = np.arange(S)[:, None], np.arange(S)[None, :]
    bf = mybir.dt.np(BF16)
    arrays["mask0"] = np.where(k <= q, 0.0, MASKED)[:P, :P].astype(bf)
    arrays["causal1"] = np.where(k <= q, 0.0, NOT_CAUSAL)[P:].astype(f32)
    arrays["ident"] = np.eye(P, dtype=f32)
    arrays["hpar"] = (np.arange(P)[:, None] // HD % 2 == np.arange(2)[None, :]).astype(f32)
    kones = ((np.arange(32)[:, None] < 4) & (np.arange(32)[:, None] % 2 == np.arange(2)[None, :])).astype(f32)
    arrays["kones"] = np.repeat(kones[:, :, None], S, axis=2)
    shift = 4 * (np.arange(P, dtype=np.int64) % 8)
    arrays["nib_par"] = np.stack([(15 << shift).astype(np.uint32).view(np.int32), shift.astype(np.int32)], axis=1)
    arrays["zsh"] = (4 * (np.arange(512) % 8)).astype(np.int32)

    def units(name, down):
        qw, zw, sc = (g[f"L0_ffn_{name}_{w}"] for w in ("qweight", "zeros", "scales"))
        qw, zw = np.repeat(qw, 8, axis=0), np.repeat(zw, 8, axis=1)
        if down:
            qw = np.pad(qw, ((0, FM * P - FI), (0, 0)))
            return qw.reshape(FM, P, D), zw, sc
        pad = ((0, 0), (0, FM * P - FI))
        qw, zw, sc = (np.pad(w, pad) for w in (qw, zw, sc))
        qw = qw.reshape(KT, P, FM, P).transpose(2, 1, 0, 3).reshape(FM, P, 512)
        zw, sc = (w.reshape(KT, FM, P).transpose(1, 0, 2).reshape(FM, 512) for w in (zw, sc))
        return qw, zw, sc
    parts = [units("gate", False), units("up", False), units("down", True)]
    for n, name in enumerate(("qpack", "zrep", "gsc")):
        arrays[name] = np.concatenate([p[n] for p in parts], axis=0)

    wq = g["L1_attn_Wq"].T.reshape(D, KVH, G, HD).transpose(0, 2, 1, 3).reshape(D, D)
    arrays["wqkv"] = np.concatenate([wq, g["L1_attn_Wk"].T, g["L1_attn_Wv"].T], axis=1)
    arrays["woT"] = g["L1_attn_Wo"].T
    arrays["bo"] = g["L1_attn_bo"]
    arrays["ffnWT"] = g["L1_ffn_W"].T
    arrays["lora_A"] = g["L1_ffn_lora_A"]
    arrays["lora_BT"] = g["L1_ffn_lora_B"].T
    arrays["mag"] = g["L1_ffn_magnitude"]

    nc = bacc.Bacc("TRN2", target_bir_lowering=False, num_devices=1)
    feeds, args = {}, {}
    for name, arr in arrays.items():
        arr = np.ascontiguousarray(arr)
        feeds["in_" + name] = arr
        args[name] = nc.dram_tensor("in_" + name, arr.shape, mybir.dt.from_np(arr.dtype), kind="ExternalInput").ap()
    out = nc.dram_tensor("out_x", (TOK, D), F32, kind="ExternalOutput").ap()
    build(nc, args, out)
    r = run_bass_kernel_spmd(nc, [feeds], core_ids=[0])
    return r.results[0]["out_x"].reshape(B, S, D)
```

```python
from contextlib import ExitStack

import numpy as np

import concourse.bass as bass
from concourse import mybir

F32 = mybir.dt.float32
F16 = mybir.dt.float16
BF16 = mybir.dt.bfloat16
I32 = mybir.dt.int32
F32R = mybir.dt.float32r
ALU = mybir.AluOpType
ACT = mybir.ActivationFunctionType
AX = mybir.AxisListType

P = 128
B, S, D = 8, 256, 512
TOK = B * S
NT = TOK // P
KT = D // P
H, NOPE, ROPE, VD = 32, 128, 64, 128
QR, KVR = 192, 64
IH, ID, TOPK = 16, 128, 128
A1N = QR + KVR + ROPE
HC = 4
NC = H // HC
QSCALE = float((NOPE + ROPE) ** -0.5)
FI = 1376
FM = -(-FI // P)
FLAST = FI - (FM - 1) * P
UNITS = 3 * FM
QUARTER = TOK // 4
KVH, G, HD = 8, 4, 16
R = 32
EPS = 1e-5

MASKED = -1.0e30
NOT_CAUSAL = -3.0e38
TAKEN = -3.4e38


class Track:

    def __init__(self, nc, ctx, name, step=1):
        self.sem, self.step, self.count = ctx.enter_context(nc.semaphore(name)), step, 0

    def add(self, ins):
        ins.then_inc(self.sem, self.step)
        self.count += self.step
        return self.count


def build(nc, a, out):
    ctx = ExitStack()
    pe, act, dve, pool, sync = nc.tensor, nc.scalar, nc.vector, nc.gpsimd, nc.sync
    done = {}
    waited = {}
    transfers = {}

    with ctx:
        by_pe, by_act = Track(nc, ctx, "by_pe"), Track(nc, ctx, "by_act")
        by_dve, by_pool = Track(nc, ctx, "by_dve"), Track(nc, ctx, "by_pool")

        def sig(track, ins, *name):
            done[name] = (track, track.add(ins))
            return name

        def need(eng, *name):
            track, value = done[name]
            key = (id(eng), id(track))
            if waited.get(key, 0) < value:
                eng.wait_ge(track.sem, value)
                waited[key] = value

        def load(name, dst, src, eng=sync, group=None):
            key = (name,) if isinstance(name, str) else name
            kind, *index = group or key
            slot = "_".join([kind] + [str(n % (NT if kind == "store" else 4)) for n in index])
            if slot not in transfers:
                transfers[slot] = Track(nc, ctx, "dma_" + slot, 16)
            done[group or key] = (transfers[slot], transfers[slot].add(eng.dma_start(dst, src)))

        def sb(stack, name, shape, dt=F32):
            return stack.enter_context(nc.sbuf_tensor(name, shape, dt))

        X = sb(ctx, "X", [P, NT, D])
        ident = sb(ctx, "ident", [P, P])
        PS = ctx.enter_context(nc.psum_tensor("PS", [P, 8, 512], F32))
        minus_half = sb(ctx, "minus_half", [P, 2])
        qpack = [sb(ctx, f"qpack{i}", [P, 512], I32) for i in range(2)]
        zrep = [sb(ctx, f"zrep{i}", [P, 512], I32) for i in range(2)]
        gsc = [sb(ctx, f"gsc{i}", [P, 512], F16) for i in range(2)]
        nib_par = sb(ctx, "nib_par", [P, 2], I32)
        zshift = sb(ctx, "zshift", [P, 8], I32)
        stat = sb(ctx, "stat", [P, 4, 6])
        mv = sb(ctx, "mv", [P, 4, 2])
        rstd = sb(ctx, "rstd", [P, 4, 1])

        load("ident", ident[:], a["ident"])
        sig(by_dve, dve.memset(minus_half[:], -0.5), "minus_half")

        ln_count = [0]

        def layer_norm(t, bank, tag, bank_ready, extra=None, y16=None):
            k = ln_count[0] % 4
            ln_count[0] += 1
            x = X[:, t, :]
            need(dve, *bank_ready)
            if extra is not None:
                need(dve, *extra)
            sig(by_dve, dve.tensor_tensor(x, x, bank, ALU.add), tag, "added", t)
            need(dve, tag, "added", t)
            if ln_count[0] > 4:
                need(dve, "ln_applied", ln_count[0] - 5)
            sig(by_dve, dve.bn_stats(stat[:, k, :], x), tag, "stats", t)
            need(dve, tag, "stats", t)
            sig(by_dve, dve.bn_aggr(mv[:, k, :], stat[:, k, :]), tag, "aggr", t)
            need(dve, tag, "aggr", t)
            sig(by_dve, dve.tensor_scalar(stat[:, k, 0:1], mv[:, k, 1:2], EPS, None, ALU.add), tag, "var", t)
            need(pool, tag, "var", t)
            need(pool, "minus_half")
            sig(by_pool, pool.tensor_tensor(rstd[:, k, :], stat[:, k, 0:1], minus_half[:, 0:1], ALU.pow),
                tag, "rstd", t)
            need(pool, tag, "rstd", t)
            sig(by_pool, pool.tensor_scalar(x, x, mv[:, k, 0:1], rstd[:, k, :], ALU.subtract, ALU.mult),
                tag, "normed", t)
            done[("ln_applied", ln_count[0] - 1)] = done[(tag, "normed", t)]

        attn = ExitStack()
        mask1 = sb(attn, "mask1", [P, B, S], BF16)
        mask0 = sb(attn, "mask0", [P, P], BF16)
        causal1 = sb(attn, "causal1", [P, S])
        accs = [sb(attn, f"acc{i}", [P, S]) for i in range(2)]
        top8 = sb(attn, "top8", [P, 8])
        rc = sb(attn, "rc", [P, 2, ROPE])
        rs = sb(attn, "rs", [P, 2, ROPE])
        qh0 = sb(attn, "qh0", [P, NT, P], F32R)
        ql0 = sb(attn, "ql0", [P, NT, P], F32R)
        q1s = sb(attn, "q1s", [P, NT, P], F32R)
        latk = sb(attn, "latk", [P, NT, P])
        kT = sb(attn, "kT", [P, B, P])
        kTh = sb(attn, "kTh", [P, NT, P], F32R)
        kTl = sb(attn, "kTl", [P, NT, P], F32R)
        Wh0, Wl0, Wh1, Wl1, Woh, Wol = [], [], [], [], [], []

        def folded_buffers(stack, i):
            for name, ws, shape in (("Wh0", Wh0, [P, 512]), ("Wl0", Wl0, [P, 512]), ("Wh1", Wh1, [P, 512]),
                                    ("Wl1", Wl1, [P, 512]), ("Woh", Woh, [P, 2, D]), ("Wol", Wol, [P, 2, D])):
                ws.append(sb(stack, f"{name}{i}", shape, F32R))
        folded_buffers(attn, 0)
        wt_qn = sb(attn, "wt_qn", [P, HC, 2 * P])
        wt_k = sb(attn, "wt_k", [P, HC, KVR])
        wt_v = sb(attn, "wt_v", [P, HC, KVR])
        wt_o = sb(attn, "wt_o", [P, HC, D])
        wt_pe = sb(attn, "wt_pe", [P, 2, HC * ROPE])

        def pairs(ap, n):
            return ap.rearrange("p (h i two) -> p h i two", h=n, two=2)

        idx = ExitStack()
        XT = [sb(idx, f"XT{i}", [P, KT, S]) for i in range(2)]
        a1w = sb(idx, "a1w", [P, KT, A1N])
        wq_b = sb(idx, "wq_b", [P, QR])
        wkv_b = sb(idx, "wkv_b", [P, KVR])
        ssq = sb(idx, "ssq", [P, 2])
        lrstd = sb(idx, "lrstd", [P, 2])
        junk = sb(idx, "junk", [P, QR])
        latq = sb(idx, "latq", [P, 2 * P])
        k1 = sb(idx, "k1", [P, ROPE])
        k2 = sb(idx, "k2", [P, ROPE])
        qtmp = sb(idx, "qtmp", [P, P], F32R)
        wk_i = sb(idx, "wk_i", [P, KT, ID])
        ww_i = sb(idx, "ww_i", [P, KT, IH])
        wq_i = sb(idx, "wq_i", [P, KT, IH * ID])
        ikT = [sb(idx, f"ikT{i}", [P, S]) for i in range(2)]
        iw = [sb(idx, f"iw{i}", [P, IH]) for i in range(2)]
        iqT = [sb(idx, f"iqT{i}", [P, 4 * P]) for i in range(2)]
        rel = [sb(idx, f"rel{i}", [P, 2 * S]) for i in range(3)]

        xT_view = a["xT"].rearrange("(k p) n -> p k n", p=P)

        def load_xT(b):
            if b >= 2:
                need(sync, "a1", 2 * (b - 2) + 1)
            load(("xT", b), XT[b % 2][:], xT_view[:, :, b * S:(b + 1) * S])

        load_xT(0)
        load("wk_i", wk_i[:], a["wk_i"].rearrange("(k p) n -> p k n", p=P))
        load("ww_i", ww_i[:], a["ww_i"].rearrange("(k p) n -> p k n", p=P))
        for g in range(4):
            load(("wq_i", g), wq_i[:, :, g * 512:(g + 1) * 512],
                 a["wq_i"].rearrange("(k p) n -> p k n", p=P)[:, :, g * 512:(g + 1) * 512])
        load("causal1", causal1[:], a["causal1"])
        load("mask0", mask0[:], a["mask0"])
        load("a1w", a1w[:], a["a1w"].rearrange("(k p) n -> p k n", p=P))
        load("rc", rc[:], a["rope_c"].rearrange("(j p) n -> p j n", p=P))
        load("rs", rs[:], a["rope_s"].rearrange("(j p) n -> p j n", p=P))
        load("wq_b", wq_b[:], a["q_norm"].partition_broadcast(P))
        load("wkv_b", wkv_b[:], a["kv_norm"].partition_broadcast(P))
        load_xT(1)

        def idx_keys(b):
            need(pe, "xT", b)
            need(pe, "wk_i")
            need(pe, "ww_i")
            if b >= 1:
                need(pe, "ikT", b - 1)
                need(pe, "iw", b - 1)
            for k in range(KT):
                m = pe.matmul(PS[:, 0, 0:S], wk_i[:, k, :], XT[b % 2][:, k, :], start=(k == 0), stop=(k == KT - 1))
            for k in range(KT):
                m = pe.matmul(PS[:, 0, S:S + IH], XT[b % 2][:, k, P:S], ww_i[:, k, :],
                              start=(k == 0), stop=(k == KT - 1))
            sig(by_pe, m, "idx_keys", b)
            need(dve, "idx_keys", b)
            if b >= 2:
                need(dve, "idx_scores", b - 2, 7)
            sig(by_dve, dve.tensor_copy(ikT[b % 2][:], PS[:, 0, 0:S]), "ikT", b)
            sig(by_dve, dve.tensor_scalar(iw[b % 2][:], PS[:, 0, S:S + IH], float(IH ** -0.5), None, ALU.mult),
                "iw", b)

        def idx_queries(b, g):
            need(pe, "wq_i", g)
            n = 4 * b + g
            if n >= 2:
                need(pe, "iqT", n - 2)
            for h in range(4):
                for k in range(KT):
                    m = pe.matmul(PS[:, 1 + n % 2, h * P:(h + 1) * P],
                                  wq_i[:, k, (4 * g + h) * ID:(4 * g + h + 1) * ID], XT[b % 2][:, k, P:S],
                                  start=(k == 0), stop=(k == KT - 1))
            sig(by_pe, m, "idx_q", n)
            need(act, "idx_q", n)
            if n >= 2:
                need(act, "idx_scores", (n - 2) // 4, 2 * ((n - 2) % 4) + 1)
            sig(by_act, act.activation(iqT[n % 2][:], PS[:, 1 + n % 2, :], ACT.Copy), "iqT", n)

        def idx_scores(b, g):
            n = 4 * b + g
            need(pe, "iqT", n)
            need(pe, "ikT", b)
            for pr in range(2):
                u = 8 * b + 2 * g + pr
                if u >= 4:
                    need(pe, "relu", u - 4)
                for h in range(2):
                    m = pe.matmul(PS[:, 3 + u % 4, h * S:(h + 1) * S],
                                  iqT[n % 2][:, (2 * pr + h) * P:(2 * pr + h + 1) * P], ikT[b % 2][:],
                                  start=True, stop=True)
                sig(by_pe, m, "idx_scores", b, 2 * g + pr)
                need(act, "idx_scores", b, 2 * g + pr)
                if u >= 3:
                    need(act, "idx_sum", u - 3)
                sig(by_act, act.activation(rel[u % 3][:], PS[:, 3 + u % 4, :], ACT.Relu), "relu", u)
                need(dve, "relu", u)
                for h in range(2):
                    head = 4 * g + 2 * pr + h
                    acc, w = accs[b % 2][:], iw[b % 2][:, head:head + 1]
                    r = rel[u % 3][:, h * S:(h + 1) * S]
                    if head == 0:
                        need(dve, "iw", b)
                        ins = dve.tensor_scalar(acc, r, w, None, ALU.mult)
                    else:
                        need(dve, "idx_acc", b, head - 1)
                        ins = dve.scalar_tensor_tensor(acc, r, w, acc, ALU.mult, ALU.add)
                    sig(by_dve, ins, "idx_acc", b, head)
                done[("idx_sum", u)] = done[("idx_acc", b, 4 * g + 2 * pr + 1)]

        def idx_topk_parts(b):
            acc = accs[b % 2][:]

            def scale():
                need(dve, "idx_acc", b, IH - 1)
                need(dve, "causal1")
                sig(by_dve, dve.scalar_tensor_tensor(acc, acc, float(ID ** -0.5), causal1[:], ALU.mult, ALU.add),
                    "taken", b, -1)

            def round_(r):
                need(dve, "taken", b, r - 1)
                sig(by_dve, dve.max(top8[:], acc), "top8", b, r)
                need(dve, "top8", b, r)
                sig(by_dve, dve.match_replace(acc, top8[:], acc, TAKEN), "taken", b, r)

            def finish():
                need(dve, "taken", b, TOPK // 8 - 1)
                sig(by_dve, dve.tensor_scalar(mask1[:, b, :], acc, (TAKEN + NOT_CAUSAL) / 2, MASKED,
                                              ALU.is_gt, ALU.mult), "mask1", b)
            return [scale] + [lambda r=r: round_(r) for r in range(TOPK // 8)] + [finish]

        LB = 7

        def latents(t):
            b, j = divmod(t, 2)
            need(pe, "xT", b)
            need(pe, "a1w")
            if t >= 1:
                need(pe, "latT", t - 1)
            for k in range(KT):
                m = pe.matmul(PS[:, LB, 0:A1N], XT[b % 2][:, k, j * P:(j + 1) * P], a1w[:, k, :],
                              start=(k == 0), stop=(k == KT - 1))
            sig(by_pe, m, "a1", t)
            need(act, "a1", t)
            if t >= 1:
                need(act, "lat_q", t - 1)
                need(act, "lrstd", t - 1)
                need(act, "ssq2", t - 1)
            sig(by_act, act.activation(junk[:, 0:QR], PS[:, LB, 0:QR], ACT.Square, scale=float(QR ** -0.5),
                                       accum_out=ssq[:, 0:1]), "ssq1", t)
            need(act, "ssq1", t)
            sig(by_act, act.activation(junk[:, 0:KVR], PS[:, LB, QR:QR + KVR], ACT.Square,
                                       scale=float(KVR ** -0.5), accum_out=ssq[:, 1:2]), "ssq2", t)
            need(dve, "ssq2", t)
            sig(by_dve, dve.tensor_scalar(ssq[:], ssq[:], EPS, None, ALU.add), "ssq_eps", t)
            need(pool, "ssq_eps", t)
            need(pool, "minus_half")
            if t >= 1:
                need(pool, "lat_kv", t - 1)
            sig(by_pool, pool.tensor_tensor(lrstd[:], ssq[:], minus_half[:], ALU.pow), "lrstd", t)
            need(dve, "rc")
            need(dve, "rs")
            if t >= 1:
                need(dve, "latT_ps", t - 1)
            kp = PS[:, LB, QR + KVR:A1N]
            sig(by_dve, dve.tensor_tensor(k1[:], kp, rc[:, j, :], ALU.mult), "k1", t)
            sig(by_dve, dve.tensor_tensor(pairs(k2[:], 1), pairs(kp, 1)[:, :, :, ::-1], pairs(rs[:, j, :], 1), ALU.mult),
                "k2", t)
            need(dve, "k2", t)
            sig(by_dve, dve.tensor_tensor(latk[:, t, KVR:P], k1[:], k2[:], ALU.add), "lat_pe", t)
            need(dve, "lrstd", t)
            need(dve, "wq_b")
            need(dve, "wkv_b")
            for dst, src in ((0, 0), (QR, P)):
                sig(by_dve, dve.scalar_tensor_tensor(latq[:, dst:dst + QR - src], PS[:, LB, src:QR], lrstd[:, 0:1],
                                                     wq_b[:, src:QR], ALU.mult, ALU.mult), "lat_q", t)
            sig(by_dve, dve.scalar_tensor_tensor(latk[:, t, 0:KVR], PS[:, LB, QR:QR + KVR], lrstd[:, 1:2],
                                                 wkv_b[:], ALU.mult, ALU.mult), "lat_kv", t)

        def latents_T(t):
            bank = PS[:, LB, :]
            half = QR - P
            need(pe, "lat_kv", t)
            need(pe, "ident")
            pe.transpose(bank[:, 0:P], latq[:, 0:P], ident[:])
            pe.transpose(bank[:, P:2 * P], latk[:, t, :], ident[:])
            sig(by_pe, pe.transpose(bank[:, 2 * P:3 * P], latq[:, P:2 * P], ident[:]), "latT_ps", t)
            need(act, "latT_ps", t)
            sig(by_act, act.activation(qh0[:, t, :], bank[:, 0:P], ACT.Copy), "qh0", t)
            sig(by_act, act.activation(q1s[0:half, t, :], bank[0:half, 2 * P:3 * P], ACT.Copy), "q1_hi", t)
            if t % 2 == 0:
                sig(by_act, act.activation(kT[:, t // 2, :], bank[:, P:2 * P], ACT.Copy), "kT_whole", t)
            sig(by_act, act.activation(kTh[:, t, :], bank[:, P:2 * P], ACT.Copy), "kT", t)
            need(dve, "kT", t)
            if t >= 1:
                need(dve, "latT", t - 1)
            sig(by_dve, dve.tensor_copy(qtmp[half:P], bank[half:P, 2 * P:3 * P]), "qtmp", t)
            sig(by_dve, dve.tensor_tensor(ql0[:, t, :], bank[:, 0:P], qh0[:, t, :].bitcast(F32), ALU.subtract), "ql0", t)
            sig(by_dve, dve.tensor_tensor(kTl[:, t, :], bank[:, P:2 * P], kTh[:, t, :].bitcast(F32), ALU.subtract), "kTl", t)
            need(dve, "qtmp", t)
            sig(by_dve, dve.tensor_tensor(q1s[half:P, t, :], bank[half:P, 2 * P:3 * P], qtmp[half:P].bitcast(F32),
                                          ALU.subtract), "latT", t)

        MISC, QB, QTB, SB_, PTB, OB = 0, 1, 3, 4, 6, 7
        misc_reader = [[("ikT", B - 1), ("iw", B - 1)]]

        def misc_bank():
            for n in misc_reader[0]:
                need(pe, *n)

        def fold_load(c):
            if c >= 1:
                need(sync, "fold_pe", c - 1, 1)
                need(sync, "fold_vo", c - 1, 1)
            hs = slice(HC * c, HC * (c + 1))
            load(("wt", "part"), wt_qn[:], a["qnT"][:, hs, :], group=("wt_q", c))
            load(("wt", "part"), wt_k[:], a["wkT"][:, hs, :], group=("wt_q", c))
            load(("wt", "part"), wt_pe[:], a["q_pe_w"][:, :, c * HC * ROPE:(c + 1) * HC * ROPE].rearrange("a p n -> p a n"),
                 group=("wt_q", c))
            load(("wt", "part"), wt_v[:], a["wvT"][:, hs, :], group=("wt_o", c))
            load(("wt", "part"), wt_o[:], a["o_w"].rearrange("(h p) n -> p h n", p=P)[:, hs, :], group=("wt_o", c))

        def two_parts(name, c, k, hi, lo, src, ready):
            need(act, *ready)
            if c >= 2:
                for e in (act, dve):
                    need(e, "qproj", (c - 1) * NT - 1)
                    need(e, "oproj", (c - 1) * NT - 1)
            sig(by_act, act.activation(hi, src, ACT.Copy), name + "_hi", c, k)
            need(dve, name + "_hi", c, k)
            sig(by_dve, dve.tensor_tensor(lo, src, hi.bitcast(F32), ALU.subtract), name, c, k)

        def fold_q(c, k):
            need(pe, "wt_q", c)
            misc_bank()
            for h in range(HC):
                m = pe.matmul(PS[:, MISC, h * KVR:(h + 1) * KVR], wt_qn[:, h, k * P:(k + 1) * P], wt_k[:, h, :],
                              start=True, stop=True)
            sig(by_pe, m, "fold_qk", c, k)
            hi, lo = ((Wh0, Wl0), (Wh1, Wl1))[k]
            two_parts("fold_q", c, k, hi[c % 2][:, 0:256], lo[c % 2][:, 0:256], PS[:, MISC, 0:256], ("fold_qk", c, k))
            misc_reader[0] = [("fold_q", c, k)]

        def fold_pe(c):
            for k in range(2):
                hi, lo = ((Wh0, Wl0), (Wh1, Wl1))[k]
                two_parts("fold_pe", c, k, hi[c % 2][:, 256:512], lo[c % 2][:, 256:512], wt_pe[:, k, :], ("wt_q", c))

        def fold_o(c, p):
            need(pe, "wt_o", c)
            misc_bank()
            for h in range(2):
                m = pe.matmul(PS[h * KVR:(h + 1) * KVR, MISC, :], wt_v[:, 2 * p + h, :], wt_o[:, 2 * p + h, :],
                              start=True, stop=True)
            sig(by_pe, m, "fold_vo", c, p)
            two_parts("fold_o", c, p, Woh[c % 2][:, p, :], Wol[c % 2][:, p, :], PS[:, MISC, :], ("fold_vo", c, p))
            misc_reader[0] = [("fold_o", c, p)]

        pending = []

        def topk_steps(n):
            for _ in range(n):
                if pending:
                    pending.pop(0)()

        for b in range(B):
            idx_keys(b)
            idx_queries(b, 0)
            for g in range(4):
                if g < 3:
                    idx_queries(b, g + 1)
                idx_scores(b, g)
                if b == B - 1:
                    (lambda: fold_q(0, 0), lambda: fold_q(0, 1), lambda: fold_o(0, 0), lambda: fold_o(0, 1))[g]()
                topk_steps(3)
                (latents, latents_T)[g % 2](2 * b + g // 2)
                topk_steps(2)
            pending = idx_topk_parts(b)
            if b + 2 < B:
                load_xT(b + 2)
            if b == 0:
                fold_load(0)
        fold_pe(0)
        idx_end = [("idx_scores", B - 1, 7), ("a1", NT - 1), ("relu", 8 * B - 1), ("latT", NT - 1), ("idx_acc", B - 1, IH - 1),
                   ("lrstd", NT - 1)]
        idx.close()

        work = ExitStack()
        folded_buffers(work, 1)
        qtok = [sb(work, f"qtok{i}", [P, HC, P]) for i in range(2)]
        r1 = [sb(work, f"r1{i}", [P, HC, ROPE]) for i in range(2)]
        r2 = [sb(work, f"r2{i}", [P, HC, ROPE]) for i in range(2)]
        qT = sb(work, "qT", [P, HC, P])
        qTh = sb(work, "qTh", [P, HC, P], F32R)
        qTl = sb(work, "qTl", [P, HC, P], F32R)
        prob = [sb(work, f"prob{i}", [P, HC, S]) for i in range(3)]
        pT = [sb(work, f"pT{i}", [P, 2, HC * P]) for i in range(2)]
        nmax = [sb(work, f"nmax{i}", [P, HC]) for i in range(3)]
        psum_ = [sb(work, f"psum{i}", [P, HC]) for i in range(3)]
        rsum = [sb(work, f"rsum{i}", [P, HC]) for i in range(3)]
        oTh = [sb(work, f"oTh{i}", [P, 2, P], F32R) for i in range(2)]
        oTl = [sb(work, f"oTl{i}", [P, 2, P], F32R) for i in range(2)]

        for e in (sync, act, dve, pool, pe):
            for n in idx_end:
                need(e, *n)
        xtok_view = a["x"].rearrange("(t p) n -> p t n", p=P)
        for q in range(4):
            load(("x", q), X[:, 4 * q:4 * q + 4, :], xtok_view[:, 4 * q:4 * q + 4, :])

        def q_project(i):
            c, t = divmod(i, NT)
            j, w = t % 2, c % 2
            need(pe, "latT", t)
            need(pe, "fold_q", c, 1)
            need(pe, "fold_pe", c, 1)
            if i >= 2:
                need(pe, "q_abs", i - 2)
                need(pe, "r2", i - 2)
            bank = PS[:, QB + i % 2, :]
            terms = ((qh0, Wh0), (qh0, Wl0), (ql0, Wh0), (q1s, Wh1), (q1s, Wl1))
            for n, (q, W) in enumerate(terms):
                m = pe.matmul(bank, q[:, t, :], W[w][:], start=(n == 0), stop=(n == len(terms) - 1))
            sig(by_pe, m, "qproj", i)
            need(dve, "qproj", i)
            if i >= 2:
                need(dve, "q_pe", i - 2)
            qp = pairs(bank[:, 256:512], HC)
            cb = pairs(rc[:, j, :], 1).broadcast_to([P, HC, ROPE // 2, 2])
            sb_ = pairs(rs[:, j, :], 1).broadcast_to([P, HC, ROPE // 2, 2])
            sig(by_dve, dve.tensor_tensor(r1[i % 2][:].rearrange("p h (i two) -> p h i two", two=2), qp, cb, ALU.mult),
                "r1", i)
            sig(by_dve, dve.tensor_tensor(r2[i % 2][:].rearrange("p h (i two) -> p h i two", two=2),
                                          qp[:, :, :, ::-1], sb_, ALU.mult), "r2", i)
            need(pool, "r2", i)
            if i >= 2:
                need(pool, "qtrans", i - 2)
            sig(by_pool, pool.tensor_tensor(qtok[i % 2][:, :, KVR:P], r1[i % 2][:], r2[i % 2][:], ALU.add), "q_pe", i)

        def q_latent(i):
            need(act, "r2", i)
            if i >= 2:
                need(act, "qtrans", i - 2)
            sig(by_act, act.activation(qtok[i % 2][:, :, 0:KVR],
                                       PS[:, QB + i % 2, 0:256].rearrange("p (h n) -> p h n", h=HC), ACT.Copy), "q_abs", i)

        def q_transpose(i):
            need(pe, "q_abs", i)
            need(pe, "q_pe", i)
            if i >= 1:
                need(pe, "qT", i - 1)
            for h in range(HC):
                m = pe.transpose(PS[:, QTB, h * P:(h + 1) * P], qtok[i % 2][:, h, :], ident[:])
            sig(by_pe, m, "qtrans", i)
            bank = PS[:, QTB, :].rearrange("p (h n) -> p h n", h=HC)
            if i % 2:
                need(act, "qtrans", i)
                if i >= 2:
                    need(act, "scores", i - 2)
                sig(by_act, act.activation(qTh[:], bank, ACT.Copy), "qTh", i)
                need(dve, "qTh", i)
                sig(by_dve, dve.tensor_tensor(qTl[:], bank, qTh[:].bitcast(F32), ALU.subtract), "qT", i)
            else:
                need(dve, "qtrans", i)
                if i >= 2:
                    need(dve, "scores", i - 2)
                sig(by_dve, dve.tensor_copy(qT[:], bank), "qT", i)

        def scores(i):
            t = i % NT
            b, j = divmod(t, 2)
            nk = P * (j + 1)
            need(pe, "qT", i)
            if i >= 1:
                need(pe, "masked", i - 1)
            bank = PS[:, SB_:SB_ + 2, :].rearrange("p a (h n) -> p (a h) n", h=2)
            kh, kl = (k[:, 2 * b:2 * b + 2, :].rearrange("p a n -> p (a n)") for k in (kTh, kTl))
            terms = ((qTh, kh), (qTh, kl), (qTl, kh)) if j else ((qT, kT[:, b, :]),)
            for h in range(HC):
                for n, (q, k) in enumerate(terms):
                    m = pe.matmul(bank[:, h, 0:nk], q[:, h, :], k, start=(n == 0), stop=(n == len(terms) - 1))
            sig(by_pe, m, "scores", i)
            need(dve, "scores", i)
            if i >= 3:
                need(dve, "ptrans", i - 3)
            if j:
                need(dve, "mask1", b)
                mask = mask1[:, b, :]
            else:
                need(dve, "mask0")
                mask = mask0[:]
            for h in range(HC):
                ins = dve.tensor_tensor_reduce(prob[i % 3][:, h, 0:nk], bank[:, h, 0:nk], mask, -QSCALE, 3.0e38,
                                               ALU.add, ALU.min, nmax[i % 3][:, h:h + 1])
            sig(by_dve, ins, "masked", i)

        def exps(i):
            nk = P * (i % 2 + 1)
            need(act, "masked", i)
            if i >= 3:
                need(act, "rsum", i - 3)
            for h in range(HC):
                p = prob[i % 3][:, h, 0:nk]
                ins = act.activation(p, p, ACT.Exp, bias=nmax[i % 3][:, h:h + 1], scale=-1.0,
                                     accum_out=psum_[i % 3][:, h:h + 1])
            sig(by_act, ins, "exp", i)

        def divide(i):
            nk = P * (i % 2 + 1)
            need(dve, "exp", i)
            if i >= 3:
                need(dve, "prob", i - 3)
            sig(by_dve, dve.reciprocal(rsum[i % 3][:], psum_[i % 3][:]), "rsum", i)
            need(pool, "rsum", i)
            p = prob[i % 3][:, :, 0:nk]
            sig(by_pool, pool.tensor_tensor(p, p, rsum[i % 3][:].unsqueeze(2).broadcast_to([P, HC, nk]), ALU.mult),
                "prob", i)

        ORDER = (0, 2, 1, 3)

        def p_transpose(i):
            j = i % 2
            need(pe, "prob", i)
            if i >= 1:
                need(pe, "pT", i - 1)
            for blk in range(j + 1):
                if blk == 1:
                    need(pe, "oT", i - 1)
                for s, h in enumerate(ORDER):
                    m = pe.transpose(PS[:, PTB + blk, s * P:(s + 1) * P],
                                     prob[i % 3][:, h, blk * P:(blk + 1) * P], ident[:])
            sig(by_pe, m, "ptrans", i)
            need(act, "ptrans", i)
            if i >= 2:
                need(act, "pv", i - 2)
            sig(by_act, act.activation(pT[i % 2][:, 0:j + 1, :], PS[:, PTB:PTB + j + 1, :], ACT.Copy), "pT", i)

        def attend(i):
            t = i % NT
            b, j = divmod(t, 2)
            need(pe, "pT", i)
            if i >= 1:
                need(pe, "oT", i - 1)
            for blk in range(j + 1):
                for odd in range(2):
                    m = pe.matmul(PS[KVR * odd:KVR * (odd + 1), OB, 0:2 * P], latk[:, 2 * b + blk, 0:KVR],
                                  pT[i % 2][:, blk, 2 * P * odd:2 * P * (odd + 1)], start=(blk == 0), stop=(blk == j))
            sig(by_pe, m, "pv", i)

        def attend_parts(i):
            need(act, "pv", i)
            if i >= 2:
                need(act, "oproj", i - 2)
                need(dve, "oproj", i - 2)
            bank = PS[:, OB, 0:2 * P].rearrange("p (a n) -> p a n", a=2)
            sig(by_act, act.activation(oTh[i % 2][:], bank, ACT.Copy), "oTh", i)
            need(dve, "oTh", i)
            sig(by_dve, dve.tensor_tensor(oTl[i % 2][:], bank, oTh[i % 2][:].bitcast(F32), ALU.subtract), "oT", i)

        def o_project(i):
            c, t = divmod(i, NT)
            w = c % 2
            need(pe, "oT", i)
            need(pe, "fold_o", c, 1)
            misc_bank()
            terms = [(o, W, q) for q in range(2) for o, W in ((oTh, Woh), (oTh, Wol), (oTl, Woh))]
            for n, (o, W, q) in enumerate(terms):
                m = pe.matmul(PS[:, MISC, :], o[i % 2][:, q, :], W[w][:, q, :], start=(n == 0), stop=(n == len(terms) - 1))
            sig(by_pe, m, "oproj", i)
            if c == NC - 1:
                layer_norm(t, PS[:, MISC, :], "attn", ("oproj", i), extra=("acc", c - 1, t))
                misc_reader[0] = [("attn", "added", t)]
            else:
                need(dve, "oproj", i)
                need(dve, *(("acc", c - 1, t) if c else ("x", t // 4)))
                sig(by_dve, dve.tensor_tensor(X[:, t, :], X[:, t, :], PS[:, MISC, :], ALU.add), "acc", c, t)
                misc_reader[0] = [("acc", c, t)]

        N = NT * NC
        for i in range(2):
            q_project(i)
            q_latent(i)
        q_transpose(0)
        fold_load(1)
        for i in range(N + 4):
            c, t = divmod(i, NT)
            if i < N:
                scores(i)
                topk_steps(2)
            if c + 1 < NC:
                if t in (3, 5):
                    fold_q(c + 1, t // 4)
                if t == 7:
                    fold_pe(c + 1)
                if t in (9, 11):
                    fold_o(c + 1, t // 10)
                if t == 12 and c + 2 < NC:
                    fold_load(c + 2)
            if 1 <= i <= N:
                divide(i - 1)
            if 2 <= i < N + 2:
                p_transpose(i - 2)
            if i + 1 < N:
                q_transpose(i + 1)
            if i + 2 < N:
                q_project(i + 2)
                q_latent(i + 2)
            if 3 <= i < N + 3:
                o_project(i - 3)
            if i < N:
                exps(i)
            if 2 <= i < N + 2:
                attend(i - 2)
                attend_parts(i - 2)
        attn_end = [("oproj", N - 1), ("attn", "normed", NT - 1), ("pT", N - 1), ("oTh", N - 1), ("oT", N - 1), ("prob", N - 1)]
        work.close()
        attn.close()

        l1w = ExitStack()
        wqkv = sb(l1w, "wqkv", [P, KT, D + 2 * P])
        wo = sb(l1w, "wo", [P, KT, D])
        bo_b = sb(l1w, "bo_b", [P, D])
        Wf = sb(l1w, "Wf", [P, KT, D])
        ffn = ExitStack()
        sq = [sb(ffn, f"sq{i}", [P, D]) for i in range(2)]
        la = sb(ffn, "la", [R, D])
        lb = sb(ffn, "lb", [R, D])
        mag = sb(ffn, "mag", [P, D])
        crow = sb(ffn, "crow", [P, D])
        ones = sb(ffn, "ones", [P, P])
        Wg = sb(ffn, "Wg", [P, FM, KT, P])
        Wu = sb(ffn, "Wu", [P, FM, KT, P])
        Wd = sb(ffn, "Wd", [P, FM, D])
        nib = sb(ffn, "nib", [P, 512], I32)
        znib = sb(ffn, "znib", [P, 512], I32)
        zsh = sb(ffn, "zsh", [P, 512], I32)
        diff = [sb(ffn, f"diff{i}", [P, 512]) for i in range(2)]
        x1T = [sb(ffn, f"x1T{i}", [P, KT, QUARTER]) for i in range(2)]
        inter = sb(ffn, "inter", [P, FM, QUARTER])
        gate = [sb(ffn, f"gate{i}", [P, QUARTER]) for i in range(2)]
        y16 = [sb(ffn, f"y16{i}", [P, D], F16) for i in range(2)]

        load("nib_par", nib_par[:], a["nib_par"])
        order = [u for m in range(FM) for u in (m, FM + m)] + [2 * FM + m for m in range(FM)]

        def load_unit(n, before_scales=None):
            v, i = order[n], n % 2
            load(("qpack", n), qpack[i][:], a["qpack"][v])
            load(("zrep", n), zrep[i][:], a["zrep"][v].partition_broadcast(P))
            if before_scales:
                need(sync, *before_scales)
            load(("gsc", n), gsc[i][:], a["gsc"][v].partition_broadcast(P))

        load_unit(0)
        load_unit(1)
        for e in (sync, act, dve, pool, pe):
            for n in attn_end:
                need(e, *n)
        load("zsh", zsh[:], a["zsh"].partition_broadcast(P))

        def rows_of(ap):
            return ap.rearrange("(k p) n -> p k n", p=P)

        def load_layer1():
            load("la", la[:], a["lora_A"])
            load("lb", lb[:], a["lora_BT"])
            load("WfT", Wf[:], rows_of(a["ffnWT"]))
            load("mag", mag[:], a["mag"].partition_broadcast(P))
            load("wqkv", wqkv[:], rows_of(a["wqkv"]))
            load("wo", wo[:], rows_of(a["woT"]))
            load("bo_b", bo_b[:], a["bo"].partition_broadcast(P))

        def dequant(n):
            u, i = order[n], n % 2
            kind, m = divmod(u, FM)
            dst = Wd[:, m, :] if kind == 2 else (Wg, Wu)[kind][:, m, :, :].rearrange("p k n -> p (k n)")
            for w in ("qpack", "zrep", "gsc"):
                need(dve, w, n)
            need(dve, "nib_par")
            need(dve, "zsh")
            if n >= 1:
                need(dve, "diff", n - 1)
            sig(by_dve, dve.tensor_scalar(nib[:], qpack[i][:], nib_par[:, 0:1], nib_par[:, 1:2],
                                          ALU.bitwise_and, ALU.logical_shift_right), "nib", n)
            sig(by_dve, dve.tensor_tensor(znib[:], zrep[i][:], zsh[:], ALU.logical_shift_right), "zs", n)
            need(dve, "zs", n)
            sig(by_dve, dve.tensor_scalar(znib[:], znib[:], 15, None, ALU.bitwise_and), "znib", n)
            need(dve, "znib", n)
            if n >= 2:
                need(dve, "weight", n - 2)
            sig(by_dve, dve.scalar_tensor_tensor(diff[i][:], nib[:], 1.0, znib[:], ALU.subtract, ALU.subtract),
                "diff", n)
            need(pool, "diff", n)
            need(pool, "gsc", n)
            sig(by_pool, pool.tensor_tensor(dst, diff[i][:], gsc[i][:], ALU.mult), "weight", n)
            done[("unit", u)] = done[("weight", n)]
            if n + 2 < UNITS:
                need(sync, "diff", n)
                load_unit(n + 2, ("weight", n))

        XB, WB, GB, UB, DB = 0, 1, 2, 4, 6

        ROOTS = 8

        def adapt_steps():
            def product(k):
                if k == 0:
                    sig(by_pool, pool.memset(ones[:], 1.0), "ones")
                    need(pe, "la")
                    need(pe, "lb")
                else:
                    need(pe, "effW", k - 1)
                sig(by_pe, pe.matmul(PS[:, WB, :], la[:, k * P:(k + 1) * P], lb[:], start=True, stop=True), "BA", k)
                need(dve, "BA", k)
                need(dve, "WfT")
                sig(by_dve, dve.tensor_tensor(Wf[:, k, :], Wf[:, k, :], PS[:, WB, :], ALU.add), "effW", k)

            def square(k):
                if k == 0:
                    need(pe, "effW", KT - 1)
                    need(pe, "ones")
                need(act, "effW", k)
                if k >= 2:
                    need(act, "norm2", k - 2)
                sig(by_act, act.activation(sq[k % 2][:], Wf[:, k, :], ACT.Square), "effW2", k)

            def total(k):
                need(pe, "effW2", k)
                sig(by_pe, pe.matmul(PS[:, WB, :], ones[:], sq[k % 2][:], start=(k == 0), stop=(k == KT - 1)),
                    "norm2", k)

            def root(r):
                if r == 0:
                    need(dve, "norm2", KT - 1)
                    sig(by_dve, dve.tensor_copy(crow[:], PS[:, WB, :]), "crow")
                need(pool, "crow")
                n = D // ROOTS
                part = crow[:, r * n:(r + 1) * n]
                sig(by_pool, pool.tensor_tensor(part, part, minus_half[:, 0:1].broadcast_to([P, n]), ALU.pow),
                    "crow_r")

            def magnitudes():
                need(pool, "crow_r")
                need(pool, "mag")
                sig(by_pool, pool.tensor_tensor(crow[:], crow[:], mag[:], ALU.mult), "crow_m")

            def scale():
                need(dve, "crow_m")
                sig(by_dve, dve.tensor_tensor(Wf[:], Wf[:], crow[:].unsqueeze(1).broadcast_to([P, KT, D]), ALU.mult),
                    "Wf")
            steps = [lambda k=k: product(k) for k in range(KT)]
            steps += [lambda: square(0), lambda: square(1), lambda: total(0), lambda: square(2), lambda: total(1),
                      lambda: square(3), lambda: total(2), lambda: total(3)]
            steps += [lambda r=r: root(r) for r in range(ROOTS)]
            steps += [magnitudes, lambda: None, scale]
            return steps

        def x1_transpose(t):
            q = t // 4
            need(pe, "attn", "normed", t)
            if t >= 1:
                need(pe, "x1T", t - 1)
            for k in range(KT):
                m = pe.transpose(PS[:, XB, k * P:(k + 1) * P], X[:, t, k * P:(k + 1) * P], ident[:])
            sig(by_pe, m, "x1T_ps", t)
            need(act, "x1T_ps", t)
            if q >= 2:
                need(act, "gu", FM * (q - 1) - 1)
            sig(by_act, act.activation(x1T[q % 2][:, :, (t % 4) * P:(t % 4 + 1) * P],
                                       PS[:, XB, :].rearrange("p (k n) -> p k n", k=KT), ACT.Copy), "x1T", t)

        def gate_up(q, m):
            M = P if m < FM - 1 else FLAST
            s = q * FM + m
            need(pe, "unit", m)
            need(pe, "unit", FM + m)
            need(pe, "x1T", 4 * q + 3)
            if s >= 2:
                need(pe, "inter", s - 2)
            for W, bk in ((Wg, GB), (Wu, UB)):
                for k in range(KT):
                    ins = pe.matmul(PS[0:M, bk + s % 2, :], W[:, m, k, 0:M], x1T[q % 2][:, k, :],
                                    start=(k == 0), stop=(k == KT - 1))
            sig(by_pe, ins, "gu", s)
            need(act, "gu", s)
            if s >= 2:
                need(act, "inter", s - 2)
            sig(by_act, act.activation(gate[s % 2][0:M, :], PS[0:M, GB + s % 2, :], ACT.Silu), "silu", s)
            need(dve, "silu", s)
            if q:
                need(dve, "down", 4 * q - 1)
            sig(by_dve, dve.tensor_tensor(inter[0:M, m, :], gate[s % 2][0:M, :], PS[0:M, UB + s % 2, :], ALU.mult),
                "inter", s)

        def down(t):
            need(pe, "inter", FM * (t // 4 + 1) - 1)
            if t >= 2:
                need(pe, "y16", t - 2)
            for m in range(FM):
                M = P if m < FM - 1 else FLAST
                need(pe, "unit", 2 * FM + m)
                ins = pe.matmul(PS[:, DB + t % 2, :], inter[0:M, m, (t % 4) * P:(t % 4 + 1) * P], Wd[0:M, m, :],
                                start=(m == 0), stop=(m == FM - 1))
            sig(by_pe, ins, "down", t)
            need(act, "down", t)
            if t >= 2:
                need(act, "ffn", "added", t - 2)
            sig(by_act, act.activation(y16[t % 2][:], PS[:, DB + t % 2, :], ACT.Copy), "y16", t)
            layer_norm(t, y16[t % 2][:], "ffn", ("y16", t))

        for n in range(4):
            dequant(n)
        made = 4
        for t in range(4):
            x1_transpose(t)
        side = adapt_steps()
        for q in range(4):
            for m in range(FM):
                gate_up(q, m)
                for _ in range(3):
                    if made < UNITS:
                        dequant(made)
                        made += 1
                if q == 0 and m == FM - 1:
                    load_layer1()
                if q >= 1 and side:
                    side.pop(0)()
                if q < 3 and m >= 6 and m < 10:
                    x1_transpose(4 * (q + 1) + m - 6)
            for t in range(4 * q, 4 * q + 4):
                down(t)
        assert not side and made == UNITS
        ffn_end = [("ffn", "normed", NT - 1), ("down", NT - 1), ("weight", UNITS - 1), ("Wf",),
                   ("ffn", "rstd", NT - 1)]
        ffn.close()

        gqa = ExitStack()
        hpar = sb(gqa, "hpar", [P, 2])
        x2T = sb(gqa, "x2T", [P, KT, S])
        qhi = sb(gqa, "qhi", [P, G, S], F32R)
        qlo = sb(gqa, "qlo", [P, G, S], F32R)
        khi = sb(gqa, "khi", [P, 2, S], F32R)
        klo = sb(gqa, "klo", [P, 2, S], F32R)
        khr = sb(gqa, "khr", [P, S], F32R)
        klr = sb(gqa, "klr", [P, S])
        qs = [sb(gqa, f"qs{i}", [P, KVH // 2, G, S], F32R) for i in range(2)]
        ks = [sb(gqa, f"ks{i}", [P, KVH // 2, 2, S], F32R) for i in range(2)]
        v32 = [sb(gqa, f"v32{i}", [P, 2, KVH, 32]) for i in range(3)]
        gmax = [sb(gqa, f"gmax{i}", [P, 2, KVH // 2, G]) for i in range(2)]
        kones_f = sb(gqa, "kones_f", [P, 2, S])
        mT = sb(gqa, "mT", [KVH * G, P])
        mhi = [sb(gqa, f"mhi{i}", [KVH * G, P], F32R) for i in range(2)]
        mlo = [sb(gqa, f"mlo{i}", [KVH * G, P], F32R) for i in range(2)]
        gp = [sb(gqa, f"gp{i}", [P, 2, G * P]) for i in range(KVH)]
        yraw = [sb(gqa, f"yraw{i}", [P, G * P]) for i in range(2)]
        grs = sb(gqa, "grs", [P, G, 4])
        ytok = [sb(gqa, f"ytok{i}", [P, D]) for i in range(2)]
        yT = [sb(gqa, f"yT{i}", [P, KT, P]) for i in range(2)]
        x3T = [sb(gqa, f"x3T{i}", [P, KT, P]) for i in range(2)]
        for e in (sync, act, dve, pool, pe):
            for n in ffn_end:
                need(e, *n)
        load("hpar", hpar[:], a["hpar"])
        load("kones_f", kones_f[96:P], a["kones"])
        need(dve, "kones_f")
        for i in range(2):
            sig(by_dve, dve.tensor_copy(ks[i][96:P], kones_f[96:P].unsqueeze(1).broadcast_to([32, KVH // 2, 2, S])),
                "kones", i)
            sig(by_dve, dve.tensor_scalar(qs[i][96:P].rearrange("p h (a g) n -> p h a (g n)", a=2),
                                          kones_f[96:P].rearrange("p a n -> p (a n)").unsqueeze(1).unsqueeze(1)
                                          .broadcast_to([32, KVH // 2, 2, 2 * S]), 0.0, None, ALU.mult), "qs_zeros", i)
        for i in range(3):
            sig(by_pool, pool.memset(v32[i][:], 0.0), "v32_zeros", i)
            need(pool, "v32_zeros", i)
            sig(by_pool, pool.memset(v32[i][:, :, :, HD:HD + 1], 1.0), "v32_ones", i)

        TB2, PJ, GS, GT, GY, OUT = 0, 1, 2, 4, 6, 7
        mcount, pcount, ocount = [0], [0], [0]
        deferred = []

        def flush():
            while deferred:
                deferred.pop(0)()

        def misc_turn(eng, track, name, transposes_, evacuate, ready, before=()):
            c = mcount[0]
            mcount[0] += 1
            bank = PS[:, TB2, :]
            for n in ready:
                if n not in done:
                    flush()
                need(pe, *n)
            if c >= 1:
                if ("misc", c - 1) not in done:
                    flush()
                need(pe, "misc", c - 1)
            sig(by_pe, transposes_(bank), "misc_ps", c)

            def drain():
                need(eng, "misc_ps", c)
                for n in before:
                    if n in done:
                        need(eng, *n)
                sig(track, evacuate(bank), "misc", c)
                done[name] = done[("misc", c)]
            deferred.append(drain)

        def transpose_tile(name, t, src, ready, dst, before):
            def go(bank):
                for k in range(KT):
                    m = pe.transpose(bank[:, k * P:(k + 1) * P], src[:, k * P:(k + 1) * P], ident[:])
                return m
            misc_turn(act, by_act, (name, t), go,
                      lambda bank: act.activation(dst, bank.rearrange("p (k n) -> p k n", k=KT), ACT.Copy),
                      [ready], before)

        def bank1_turn():
            if pcount[0]:
                if ("bank1", pcount[0] - 1) not in done:
                    flush()
                need(pe, "bank1", pcount[0] - 1)
            pcount[0] += 1
            return pcount[0] - 1

        def split_stack(b, src_hi, src_lo, dst, kinds, name):
            for p2 in range(KVH // 2):
                for part, kind in enumerate(kinds):
                    src = (src_hi, src_lo)[kind]
                    load((name, "part"), dst[32 * part:32 * part + 32, p2].bitcast(F32),
                         src[32 * p2:32 * p2 + 32].bitcast(F32), group=(name, 4 * b + p2))

        def stacked(eng, name, b):
            for p2 in range(KVH // 2):
                need(eng, name, 4 * b + p2)

        def ready_x2T(b):
            if ("x2T", 2 * b + 1) not in done:
                flush()
            need(pe, "x2T", 2 * b + 1)
            need(pe, "wqkv")

        def qkv_q(b, g):
            turn = bank1_turn()
            ready_x2T(b)
            for k in range(KT):
                m = pe.matmul(PS[:, PJ, 0:S], wqkv[:, k, g * P:(g + 1) * P], x2T[:, k, :], start=(k == 0), stop=(k == KT - 1))
            sig(by_pe, m, "q_ps", b, g)

            def parts():
                need(act, "q_ps", b, g)
                if b >= 1:
                    stacked(act, "qs", b - 1)
                    stacked(dve, "qs", b - 1)
                sc = float(HD ** -0.5)
                sig(by_act, act.activation(qhi[:, g, :], PS[:, PJ, 0:S], ACT.Copy, scale=sc), "qhi", b, g)
                need(dve, "qhi", b, g)
                sig(by_dve, dve.scalar_tensor_tensor(qlo[:, g, :], PS[:, PJ, 0:S], sc, qhi[:, g, :].bitcast(F32),
                                                     ALU.mult, ALU.subtract), "qlo", b, g)
                done[("bank1", turn)] = done[("qlo", b, g)]
            deferred.append(parts)

        def qkv_k(b):
            turn = bank1_turn()
            ready_x2T(b)
            for k in range(KT):
                m = pe.matmul(PS[:, PJ, 0:S], wqkv[:, k, D:D + P], x2T[:, k, :], start=(k == 0), stop=(k == KT - 1))
            sig(by_pe, m, "k_ps", b)

            def parts():
                need(dve, "k_ps", b)
                need(dve, "hpar")
                if b >= 1:
                    stacked(dve, "ks", b - 1)
                    need(dve, "klo", b - 1)
                sig(by_dve, dve.tensor_copy(khr[:], PS[:, PJ, 0:S]), "khr", b)
                need(dve, "khr", b)
                sig(by_dve, dve.tensor_tensor(klr[:], PS[:, PJ, 0:S], khr[:].bitcast(F32), ALU.subtract), "klr", b)
                done[("bank1", turn)] = done[("klr", b)]
                need(dve, "klr", b)
                for p in range(2):
                    sig(by_dve, dve.tensor_scalar(khi[:, p, :], khr[:].bitcast(F32), hpar[:, p:p + 1], None, ALU.mult), "khi", b)
                    sig(by_dve, dve.tensor_scalar(klo[:, p, :], klr[:], hpar[:, p:p + 1], None, ALU.mult), "klo", b)
            deferred.append(parts)

        def qkv_v(b):
            turn = bank1_turn()
            for blk in range(2):
                for k in range(KT):
                    m = pe.matmul(PS[:, PJ, blk * P:(blk + 1) * P], x2T[:, k, blk * P:(blk + 1) * P],
                                  wqkv[:, k, D + P:D + 2 * P], start=(k == 0), stop=(k == KT - 1))
            sig(by_pe, m, "v_ps", b)

            def evacuate():
                need(act, "v_ps", b)
                need(act, "v32_ones", b % 3)
                if b >= 3:
                    need(act, "gpv", 2 * 2 * (b - 2) - 1)
                sig(by_act, act.activation(v32[b % 3][:, :, :, 0:HD],
                                           PS[:, PJ, 0:S].rearrange("p (b h d) -> p b h d", b=2, d=HD), ACT.Copy), "v32", b)
                done[("bank1", turn)] = done[("v32", b)]
            deferred.append(evacuate)

        def stack_free(b):
            if b >= 2:
                need(sync, "gst_blk", 2 * (16 * (b - 1) - 1) + 1)
            if b >= 1:
                need(sync, "gs", 2 * (16 * (b - 1) + 7) + 1)

        def stack_q(b):
            need(sync, "qhi", b, G - 1)
            need(sync, "qlo", b, G - 1)
            split_stack(b, qhi, qlo, qs[b % 2], (0, 0, 1), "qs")

        def stack_k(b):
            need(sync, "khi", b)
            need(sync, "klo", b)
            split_stack(b, khi, klo, ks[b % 2], (0, 1, 0), "ks")

        def row_maxima(i):
            t, r = divmod(i, 8)
            b, j = divmod(t, 2)
            p2, g0 = r // 2, 2 * (r % 2)
            need(pe, "qs", 4 * b + p2)
            need(pe, "ks", 4 * b + p2)
            if t >= 2:
                need(dve, "mT", t - 2)
            for g in (g0, g0 + 1):
                a_ = g % 2
                if i >= 1:
                    need(pe, "gmax", 2 * (i - 1) + a_)
                sig(by_pe, pe.matmul(PS[:, GS + a_, :], qs[b % 2][0:96, p2, g, j * P:(j + 1) * P],
                                     ks[b % 2][0:96, p2, :, :].rearrange("p a n -> p (a n)"), start=True, stop=True),
                    "gs", 2 * i + a_)
                need(dve, "gs", 2 * i + a_)
                sig(by_dve, dve.tensor_reduce(gmax[t % 2][:, :, p2, g],
                                              PS[:, GS + a_, :].rearrange("p (h n) -> p h n", h=2),
                                              AX.X, ALU.max, negate=True), "gmax", 2 * i + a_)

        def max_rows(t):
            b, j = divmod(t, 2)
            misc_turn(dve, by_dve, ("mT", t),
                      lambda bank: pe.transpose(bank[0:KVH * G, 0:P], gmax[t % 2][:].rearrange("p a h g -> p (a h g)"), ident[:]),
                      lambda bank: dve.tensor_copy(mT[:], bank[0:KVH * G, 0:P]),
                      [("gmax", 16 * t + 15)], [("mlo", t - 1), ("mhi", t - 1)])
            flush()
            need(dve, "mT", t)
            if t >= 2:
                need(dve, "mrow", t - 2)
            sig(by_dve, dve.tensor_copy(mhi[t % 2][:], mT[:]), "mhi", t)
            need(dve, "mhi", t)
            sig(by_dve, dve.tensor_tensor(mlo[t % 2][:], mT[:], mhi[t % 2][:].bitcast(F32), ALU.subtract), "mlo", t)
            if t >= 4:
                need(sync, "gst_blk", 2 * (8 * (t - 3) - 1) + 1)
            need(sync, "mlo", t)
            need(sync, "qs_zeros", b % 2)
            for part, m in enumerate((mhi, mlo)):
                load(("mrow", "part"), qs[b % 2][96 + 2 * part:98 + 2 * part, :, :, j * P:(j + 1) * P].bitcast(F32),
                     m[t % 2][:].bitcast(F32), group=("mrow", t))

        def transposed_scores(i):
            t, h = divmod(i, 8)
            b, j = divmod(t, 2)
            need(pe, "qs", 4 * b + h // 2)
            need(pe, "mrow", t)
            need(pe, "kones", b % 2)
            for blk in range(2):
                if i >= 1:
                    need(pe, "gexp", 2 * (i - 1) + blk)
                bank = PS[:, GT + blk, :]
                m = pe.matmul(bank, ks[b % 2][:, h // 2, h % 2, blk * P:(blk + 1) * P],
                              qs[b % 2][:, h // 2, :, j * P:(j + 1) * P], start=True, stop=True)
                sig(by_pe, m, "gst_blk", 2 * i + blk)
                need(act, "gst_blk", 2 * i + blk)
                if t >= 1:
                    need(act, "gpv", 2 * (t - 1) + h // 4)
                sig(by_act, act.activation(gp[h][:, blk, :], bank, ACT.Exp), "gexp", 2 * i + blk)

        def g_attend(t, u, blk):
            b, j = divmod(t, 2)
            need(pe, "gexp", 2 * (8 * t + 4 * u + 3) + 1)
            need(pe, "v32", b)
            if 2 * t + u >= 1:
                need(pe, "yraw", 2 * t + u - 1)
            for c in range(4):
                m = pe.matmul(PS[32 * c:32 * c + 32, GY, :], v32[b % 3][:, blk, 4 * u + c, :],
                              gp[4 * u + c][:, blk, :], start=(blk == 0), stop=(blk == 1))
            if blk == 1:
                sig(by_pe, m, "gpv", 2 * t + u)
                deferred.append(lambda: g_evacuate(t, u))

        def g_evacuate(t, u):
            need(act, "gpv", 2 * t + u)
            if t >= 1:
                need(act, "ytok", 2 * (t - 1) + u)
            sig(by_act, act.activation(yraw[u][:], PS[:, GY, :], ACT.Copy), "yraw", 2 * t + u)

        def g_normalise(t, u):
            def transposes(bank):
                for g in range(G):
                    m = pe.transpose(bank[:, g * P:(g + 1) * P], yraw[u][:, g * P:(g + 1) * P], ident[:])
                return m

            def divide(bank):
                y = bank.rearrange("p (g h d) -> p g h d", g=G, d=32)
                if 2 * t + u >= 1:
                    need(dve, "ytok", 2 * t + u - 1)
                sig(by_dve, dve.reciprocal(grs[:].unsqueeze(3), y[:, :, :, HD:HD + 1]), "grs", t, u)
                need(dve, "grs", t, u)
                dst = ytok[t % 2][:, u * 256:(u + 1) * 256].rearrange("p (h g d) -> p g h d", g=G, d=HD)
                for g in range(G):
                    m = dve.tensor_tensor(dst[:, g], y[:, g, :, 0:HD],
                                          grs[:, g].unsqueeze(2).broadcast_to([P, 4, HD]), ALU.mult)
                    if g < G - 1:
                        sig(by_dve, m, "ytok_part")
                return m
            misc_turn(dve, by_dve, ("ytok", 2 * t + u), transposes, divide, [("yraw", 2 * t + u)], [("yT", t - 2)])

        def add_bias(t):
            need(pool, "bo_b")
            need(pool, "x2T", t)
            sig(by_pool, pool.tensor_tensor(X[:, t, :], X[:, t, :], bo_b[:], ALU.add), "x_bo", t)

        def y_transpose(t):
            transpose_tile("yT", t, ytok[t % 2], ("ytok", 2 * t + 1), yT[t % 2][:], [("g_out", t - 2)])

        def product(t, part, xT, W, name, tag, extra=None, then=None):
            if part == 0:
                for n in (xT[0], W[0]) + ((("out_bank", ocount[0] - 1),) if ocount[0] else ()):
                    if n not in done:
                        flush()
                    need(pe, *n)
            for k in range(KT // 2 * part, KT // 2 * (part + 1)):
                m = pe.matmul(PS[:, OUT, :], xT[1][:, k, :], W[1][:, k, :], start=(k == 0), stop=(k == KT - 1))
            if part == 0:
                return
            sig(by_pe, m, name, t)
            turn = ocount[0]
            ocount[0] += 1

            def norm():
                layer_norm(t, PS[:, OUT, :], tag, (name, t), extra=extra)
                done[("out_bank", turn)] = done[(tag, "added", t)]
                if then:
                    then()
            deferred.append(norm)

        out_view = out.rearrange("(t p) n -> p t n", p=P)

        def g_output(t, part):
            product(t, part, (("yT", t), yT[t % 2]), (("wo",), wo), "g_out", "gqa", extra=("x_bo", t))

        def linear1(t):
            transpose_tile("x3T", t, X[:, t, :], ("gqa", "normed", t), x3T[t % 2][:], [("lin", t - 2)])

        def linear2(t, part):
            def store():
                need(sync, "lin_ln", "normed", t)
                load(("store", t), out_view[:, t, :], X[:, t, :])
            product(t, part, (("x3T", t), x3T[t % 2]), (("Wf",), Wf), "lin", "lin_ln", then=store)

        def x2_transpose(t):
            transpose_tile("x2T", t, X[:, t, :], ("ffn", "normed", t),
                           x2T[:, :, (t % 2) * P:(t % 2 + 1) * P], [("v_ps", t // 2 - 1), ("q_ps", t // 2 - 1, G - 1)])

        def stack(b):
            flush()
            stack_free(b)
            stack_k(b)
            stack_q(b)

        AHEAD = 10

        def tile_work(t, h):
            p = t - 1
            if h < 2:
                if h == 0 and p >= 1:
                    linear1(p - 1)
                if p >= 0:
                    g_attend(p, 1, h)
            if h == 2 and p >= 0:
                g_normalise(p, 1)
                add_bias(p)
            if h in (2, 3) and p >= 1:
                linear2(p - 1, h - 2)
            if h == 3 and p >= 0:
                y_transpose(p)
            if h in (4, 5):
                if t < NT:
                    g_attend(t, 0, h - 4)
                if p >= 0:
                    g_output(p, h - 4)
            if h == 6 and t < NT:
                g_normalise(t, 0)

        def sequence_work(b, step):
            if step in (1, 4):
                x2_transpose(2 * b + (step == 4))
            if step == 6:
                qkv_k(b)
            if step == 7:
                qkv_v(b)
            if step in (8, 9, 14, 15):
                qkv_q(b, (8, 9, 14, 15).index(step))

        for step in range(16):
            sequence_work(0, step)
        stack(0)
        for step in range(8):
            sequence_work(1, step)
        flush()
        for i in range(AHEAD):
            row_maxima(i)
            if i < 8:
                sequence_work(1, 8 + i)
            flush()
            if i % 8 == 7:
                max_rows(i // 8)
        for i in range(8 * NT):
            t, h = divmod(i, 8)
            b, step = divmod(i, 16)
            transposed_scores(i)
            if i + AHEAD < 8 * NT:
                row_maxima(i + AHEAD)
            tile_work(t, h)
            if step == 0 and b + 1 < B:
                stack(b + 1)
            if b + 2 < B:
                sequence_work(b + 2, step)
            flush()
            if i + AHEAD < 8 * NT and (i + AHEAD) % 8 == 7:
                max_rows((i + AHEAD) // 8)
        for h in range(6):
            tile_work(NT, h)
        flush()
        linear1(NT - 1)
        for part in range(2):
            linear2(NT - 1, part)
        flush()
        for t in range(NT):
            need(sync, "store", t)
        gqa.close()
        l1w.close()


def kernel(**inputs):
    import concourse.bacc as bacc
    from concourse.bass_utils import run_bass_kernel_spmd

    g = {k: np.asarray(v) for k, v in inputs.items()}
    f32 = np.float32
    arrays = {}
    x = g["L0_attn_hidden_states"].reshape(TOK, D)
    arrays["x"] = x
    arrays["xT"] = x.T
    arrays["wk_i"] = g["L0_attn_idx_wk_w"]
    arrays["ww_i"] = g["L0_attn_idx_weights_w"]
    arrays["wq_i"] = g["L0_attn_idx_wq_w"]
    arrays["a1w"] = np.concatenate([g["L0_attn_q_a_w"], g["L0_attn_kv_a_w"]], axis=1)
    qb = g["L0_attn_q_b_w"].reshape(QR, H, NOPE + ROPE)
    dup = np.concatenate([np.arange(QR), np.arange(P, QR)])
    arrays["q_pe_w"] = qb[dup, :, NOPE:].reshape(2, P, H * ROPE)
    arrays["qnT"] = qb[dup, :, :NOPE].transpose(2, 1, 0)
    kvb = g["L0_attn_kv_b_w"].reshape(KVR, H, NOPE + VD)
    arrays["wkT"] = kvb[:, :, :NOPE].transpose(2, 1, 0)
    arrays["wvT"] = kvb[:, :, NOPE:].transpose(2, 1, 0)
    arrays["o_w"] = g["L0_attn_o_w"]
    arrays["q_norm"] = g["L0_attn_q_a_norm_w"]
    arrays["kv_norm"] = g["L0_attn_kv_a_norm_w"]
    inv = (f32(1.0) / f32(10000.0) ** (np.arange(0, ROPE, 2, dtype=f32) / f32(ROPE))).astype(f32)
    ang = np.arange(S, dtype=f32)[:, None] * inv[None, :]
    arrays["rope_c"] = np.repeat(np.cos(ang), 2, axis=1).astype(f32)
    arrays["rope_s"] = np.stack([-np.sin(ang), np.sin(ang)], axis=2).reshape(S, ROPE).astype(f32)
    q, k = np.arange(S)[:, None], np.arange(S)[None, :]
    bf = mybir.dt.np(BF16)
    arrays["mask0"] = np.where(k <= q, 0.0, MASKED)[:P, :P].astype(bf)
    arrays["causal1"] = np.where(k <= q, 0.0, NOT_CAUSAL)[P:].astype(f32)
    arrays["ident"] = np.eye(P, dtype=f32)
    arrays["hpar"] = (np.arange(P)[:, None] // HD % 2 == np.arange(2)[None, :]).astype(f32)
    kones = ((np.arange(32)[:, None] < 4) & (np.arange(32)[:, None] % 2 == np.arange(2)[None, :])).astype(f32)
    arrays["kones"] = np.repeat(kones[:, :, None], S, axis=2)
    shift = 4 * (np.arange(P, dtype=np.int64) % 8)
    arrays["nib_par"] = np.stack([(15 << shift).astype(np.uint32).view(np.int32), shift.astype(np.int32)], axis=1)
    arrays["zsh"] = (4 * (np.arange(512) % 8)).astype(np.int32)

    def units(name, down):
        qw, zw, sc = (g[f"L0_ffn_{name}_{w}"] for w in ("qweight", "zeros", "scales"))
        qw, zw = np.repeat(qw, 8, axis=0), np.repeat(zw, 8, axis=1)
        if down:
            qw = np.pad(qw, ((0, FM * P - FI), (0, 0)))
            return qw.reshape(FM, P, D), zw, sc
        pad = ((0, 0), (0, FM * P - FI))
        qw, zw, sc = (np.pad(w, pad) for w in (qw, zw, sc))
        qw = qw.reshape(KT, P, FM, P).transpose(2, 1, 0, 3).reshape(FM, P, 512)
        zw, sc = (w.reshape(KT, FM, P).transpose(1, 0, 2).reshape(FM, 512) for w in (zw, sc))
        return qw, zw, sc
    parts = [units("gate", False), units("up", False), units("down", True)]
    for n, name in enumerate(("qpack", "zrep", "gsc")):
        arrays[name] = np.concatenate([p[n] for p in parts], axis=0)

    wq = g["L1_attn_Wq"].T.reshape(D, KVH, G, HD).transpose(0, 2, 1, 3).reshape(D, D)
    arrays["wqkv"] = np.concatenate([wq, g["L1_attn_Wk"].T, g["L1_attn_Wv"].T], axis=1)
    arrays["woT"] = g["L1_attn_Wo"].T
    arrays["bo"] = g["L1_attn_bo"]
    arrays["ffnWT"] = g["L1_ffn_W"].T
    arrays["lora_A"] = g["L1_ffn_lora_A"]
    arrays["lora_BT"] = g["L1_ffn_lora_B"].T
    arrays["mag"] = g["L1_ffn_magnitude"]

    nc = bacc.Bacc("TRN2", target_bir_lowering=False, num_devices=1)
    feeds, args = {}, {}
    for name, arr in arrays.items():
        arr = np.ascontiguousarray(arr)
        feeds["in_" + name] = arr
        args[name] = nc.dram_tensor("in_" + name, arr.shape, mybir.dt.from_np(arr.dtype), kind="ExternalInput").ap()
    out = nc.dram_tensor("out_x", (TOK, D), F32, kind="ExternalOutput").ap()
    build(nc, args, out)
    r = run_bass_kernel_spmd(nc, [feeds], core_ids=[0])
    return r.results[0]["out_x"].reshape(B, S, D)
```

```python
from contextlib import ExitStack

import numpy as np

import concourse.bass as bass
from concourse import mybir

F32 = mybir.dt.float32
F16 = mybir.dt.float16
BF16 = mybir.dt.bfloat16
I32 = mybir.dt.int32
F32R = mybir.dt.float32r
ALU = mybir.AluOpType
ACT = mybir.ActivationFunctionType
AX = mybir.AxisListType

P = 128
B, S, D = 8, 256, 512
TOK = B * S
NT = TOK // P
KT = D // P
H, NOPE, ROPE, VD = 32, 128, 64, 128
QR, KVR = 192, 64
IH, ID, TOPK = 16, 128, 128
A1N = QR + KVR + ROPE
HC = 4
NC = H // HC
QSCALE = float((NOPE + ROPE) ** -0.5)
FI = 1376
FM = -(-FI // P)
FLAST = FI - (FM - 1) * P
UNITS = 3 * FM
QUARTER = TOK // 4
KVH, G, HD = 8, 4, 16
R = 32
EPS = 1e-5

MASKED = -1.0e30
NOT_CAUSAL = -3.0e38
TAKEN = -3.4e38


class Track:

    def __init__(self, nc, ctx, name, step=1):
        self.sem, self.step, self.count = ctx.enter_context(nc.semaphore(name)), step, 0

    def add(self, ins):
        ins.then_inc(self.sem, self.step)
        self.count += self.step
        return self.count


def build(nc, a, out):
    ctx = ExitStack()
    pe, act, dve, pool, sync = nc.tensor, nc.scalar, nc.vector, nc.gpsimd, nc.sync
    done = {}
    waited = {}
    transfers = {}

    with ctx:
        by_pe, by_act = Track(nc, ctx, "by_pe"), Track(nc, ctx, "by_act")
        by_dve, by_pool = Track(nc, ctx, "by_dve"), Track(nc, ctx, "by_pool")

        def sig(track, ins, *name):
            done[name] = (track, track.add(ins))
            return name

        def need(eng, *name):
            track, value = done[name]
            key = (id(eng), id(track))
            if waited.get(key, 0) < value:
                eng.wait_ge(track.sem, value)
                waited[key] = value

        def load(name, dst, src, eng=sync, group=None):
            key = (name,) if isinstance(name, str) else name
            kind, *index = group or key
            slot = "_".join([kind] + [str(n % (NT if kind == "store" else 4)) for n in index])
            if slot not in transfers:
                transfers[slot] = Track(nc, ctx, "dma_" + slot, 16)
            done[group or key] = (transfers[slot], transfers[slot].add(eng.dma_start(dst, src)))

        def sb(stack, name, shape, dt=F32):
            return stack.enter_context(nc.sbuf_tensor(name, shape, dt))

        X = sb(ctx, "X", [P, NT, D])
        ident = sb(ctx, "ident", [P, P])
        PS = ctx.enter_context(nc.psum_tensor("PS", [P, 8, 512], F32))
        minus_half = sb(ctx, "minus_half", [P, 2])
        RING = 3
        qpack = [sb(ctx, f"qpack{i}", [P, 512], I32) for i in range(RING)]
        zrep = [sb(ctx, f"zrep{i}", [P, 512], F16) for i in range(RING)]
        gsc = [sb(ctx, f"gsc{i}", [P, 512], F16) for i in range(RING)]
        nib_par = sb(ctx, "nib_par", [P, 2], I32)
        stat = sb(ctx, "stat", [P, 4, 6])
        mv = sb(ctx, "mv", [P, 4, 2])
        rstd = sb(ctx, "rstd", [P, 4, 1])

        load("ident", ident[:], a["ident"])
        sig(by_dve, dve.memset(minus_half[:], -0.5), "minus_half")

        ln_count = [0]

        def layer_norm(t, bank, tag, bank_ready, extra=None, later=None):
            k = ln_count[0] % 4
            ln_count[0] += 1
            x = X[:, t, :]
            need(dve, *bank_ready)
            if extra is not None:
                need(dve, *extra)
            sig(by_dve, dve.tensor_tensor(x, x, bank, ALU.add), tag, "added", t)
            need(dve, tag, "added", t)
            if ln_count[0] > 4:
                need(dve, "ln_applied", ln_count[0] - 5)
            sig(by_dve, dve.bn_stats(stat[:, k, :], x), tag, "stats", t)
            need(dve, tag, "stats", t)
            sig(by_dve, dve.bn_aggr(mv[:, k, :], stat[:, k, :]), tag, "aggr", t)
            need(dve, tag, "aggr", t)
            sig(by_dve, dve.tensor_scalar(stat[:, k, 0:1], mv[:, k, 1:2], EPS, None, ALU.add), tag, "var", t)
            need(pool, tag, "var", t)
            need(pool, "minus_half")
            sig(by_pool, pool.tensor_tensor(rstd[:, k, :], stat[:, k, 0:1], minus_half[:, 0:1], ALU.pow),
                tag, "rstd", t)
            n = ln_count[0] - 1

            def normalise(eng=pool, track=by_pool):
                need(eng, tag, "rstd", t)
                sig(track, eng.tensor_scalar(x, x, mv[:, k, 0:1], rstd[:, k, :], ALU.subtract, ALU.mult),
                    tag, "normed", t)
                done[("ln_applied", n)] = done[(tag, "normed", t)]
            if later is None:
                normalise()
            else:
                later.append(lambda: normalise(dve, by_dve))

        attn = ExitStack()
        mask1 = sb(attn, "mask1", [P, B, S], BF16)
        mask0 = sb(attn, "mask0", [P, P], BF16)
        causal1 = sb(attn, "causal1", [P, S])
        accs = [sb(attn, f"acc{i}", [P, S]) for i in range(2)]
        top8 = sb(attn, "top8", [P, 8])
        rc = sb(attn, "rc", [P, 2, ROPE])
        rs = sb(attn, "rs", [P, 2, ROPE])
        qh0 = sb(attn, "qh0", [P, NT, P], F32R)
        ql0 = sb(attn, "ql0", [P, NT, P], F32R)
        q1s = sb(attn, "q1s", [P, NT, P], F32R)
        latk = sb(attn, "latk", [P, NT, P])
        kT = sb(attn, "kT", [P, B, P])
        kTh = sb(attn, "kTh", [P, NT, P], F32R)
        kTl = sb(attn, "kTl", [P, NT, P], F32R)
        Wh0, Wl0, Wh1, Wl1, Woh, Wol = [], [], [], [], [], []

        def folded_buffers(stack, i):
            for name, ws, shape in (("Wh0", Wh0, [P, 512]), ("Wl0", Wl0, [P, 512]), ("Wh1", Wh1, [P, 512]),
                                    ("Wl1", Wl1, [P, 512]), ("Woh", Woh, [P, 2, D]), ("Wol", Wol, [P, 2, D])):
                ws.append(sb(stack, f"{name}{i}", shape, F32R))
        folded_buffers(attn, 0)
        wt_qn = sb(attn, "wt_qn", [P, HC, 2 * P])
        wt_k = sb(attn, "wt_k", [P, HC, KVR])
        wt_v = sb(attn, "wt_v", [P, HC, KVR])
        wt_o = sb(attn, "wt_o", [P, HC, D])
        wt_pe = sb(attn, "wt_pe", [P, 2, HC * ROPE])

        def pairs(ap, n):
            return ap.rearrange("p (h i two) -> p h i two", h=n, two=2)

        idx = ExitStack()
        XT = [sb(idx, f"XT{i}", [P, KT, S]) for i in range(2)]
        a1w = sb(idx, "a1w", [P, KT, A1N])
        wq_b = sb(idx, "wq_b", [P, QR])
        wkv_b = sb(idx, "wkv_b", [P, KVR])
        ssq = sb(idx, "ssq", [P, 2])
        lrstd = sb(idx, "lrstd", [P, 2])
        junk = sb(idx, "junk", [P, QR])
        latq = sb(idx, "latq", [P, 2 * P])
        k1 = sb(idx, "k1", [P, ROPE])
        k2 = sb(idx, "k2", [P, ROPE])
        qtmp = sb(idx, "qtmp", [P, P], F32R)
        wk_i = sb(idx, "wk_i", [P, KT, ID])
        ww_i = sb(idx, "ww_i", [P, KT, IH])
        wq_i = sb(idx, "wq_i", [P, KT, IH * ID])
        ikT = [sb(idx, f"ikT{i}", [P, S]) for i in range(2)]
        iw = [sb(idx, f"iw{i}", [P, IH]) for i in range(2)]
        iqT = [sb(idx, f"iqT{i}", [P, 4 * P]) for i in range(2)]
        rel = [sb(idx, f"rel{i}", [P, 2 * S]) for i in range(3)]

        zraw = sb(idx, "zraw", [UNITS, 512], I32)
        zsh = sb(idx, "zsh", [UNITS, 512], I32)
        z16 = sb(idx, "z16", [UNITS, 512], F16)
        zeros_dram = nc.dram_tensor("zeros", (UNITS, 512), F16, kind="Internal").ap()

        def unpack_zeros():
            load("zraw", zraw[:], a["zrep"])
            load("zsh", zsh[:], a["zsh"].partition_broadcast(UNITS))
            need(dve, "zraw")
            need(dve, "zsh")
            sig(by_dve, dve.tensor_tensor(zraw[:], zraw[:], zsh[:], ALU.logical_shift_right), "zs")
            need(dve, "zs")
            sig(by_dve, dve.tensor_scalar(zraw[:], zraw[:], 15, None, ALU.bitwise_and), "znib")
            need(dve, "znib")
            sig(by_dve, dve.tensor_scalar(z16[:], zraw[:], 1.0, None, ALU.add), "z16")
            need(sync, "z16")
            load("zeros", zeros_dram, z16[:])

        xT_view = a["xT"].rearrange("(k p) n -> p k n", p=P)

        def load_xT(b):
            if b >= 2:
                need(sync, "a1", 2 * (b - 2) + 1)
            load(("xT", b), XT[b % 2][:], xT_view[:, :, b * S:(b + 1) * S])

        load_xT(0)
        load("wk_i", wk_i[:], a["wk_i"].rearrange("(k p) n -> p k n", p=P))
        load("ww_i", ww_i[:], a["ww_i"].rearrange("(k p) n -> p k n", p=P))
        for g in range(4):
            load(("wq_i", g), wq_i[:, :, g * 512:(g + 1) * 512],
                 a["wq_i"].rearrange("(k p) n -> p k n", p=P)[:, :, g * 512:(g + 1) * 512])
        load("causal1", causal1[:], a["causal1"])
        load("mask0", mask0[:], a["mask0"])
        load("a1w", a1w[:], a["a1w"].rearrange("(k p) n -> p k n", p=P))
        load("rc", rc[:], a["rope_c"].rearrange("(j p) n -> p j n", p=P))
        load("rs", rs[:], a["rope_s"].rearrange("(j p) n -> p j n", p=P))
        load("wq_b", wq_b[:], a["q_norm"].partition_broadcast(P))
        load("wkv_b", wkv_b[:], a["kv_norm"].partition_broadcast(P))
        load_xT(1)

        def idx_keys(b):
            need(pe, "xT", b)
            need(pe, "wk_i")
            need(pe, "ww_i")
            if b >= 1:
                need(pe, "ikT", b - 1)
                need(pe, "iw", b - 1)
            for k in range(KT):
                m = pe.matmul(PS[:, 0, 0:S], wk_i[:, k, :], XT[b % 2][:, k, :], start=(k == 0), stop=(k == KT - 1))
            for k in range(KT):
                m = pe.matmul(PS[:, 0, S:S + IH], XT[b % 2][:, k, P:S], ww_i[:, k, :],
                              start=(k == 0), stop=(k == KT - 1))
            sig(by_pe, m, "idx_keys", b)
            need(dve, "idx_keys", b)
            if b >= 2:
                need(dve, "idx_scores", b - 2, 7)
            sig(by_dve, dve.tensor_copy(ikT[b % 2][:], PS[:, 0, 0:S]), "ikT", b)
            sig(by_dve, dve.tensor_scalar(iw[b % 2][:], PS[:, 0, S:S + IH], float(IH ** -0.5), None, ALU.mult),
                "iw", b)

        def idx_queries(b, g):
            need(pe, "wq_i", g)
            n = 4 * b + g
            if n >= 2:
                need(pe, "iqT", n - 2)
            for h in range(4):
                for k in range(KT):
                    m = pe.matmul(PS[:, 1 + n % 2, h * P:(h + 1) * P],
                                  wq_i[:, k, (4 * g + h) * ID:(4 * g + h + 1) * ID], XT[b % 2][:, k, P:S],
                                  start=(k == 0), stop=(k == KT - 1))
            sig(by_pe, m, "idx_q", n)
            need(act, "idx_q", n)
            if n >= 2:
                need(act, "idx_scores", (n - 2) // 4, 2 * ((n - 2) % 4) + 1)
            sig(by_act, act.activation(iqT[n % 2][:], PS[:, 1 + n % 2, :], ACT.Copy), "iqT", n)

        def idx_scores(b, g):
            n = 4 * b + g
            need(pe, "iqT", n)
            need(pe, "ikT", b)
            for pr in range(2):
                u = 8 * b + 2 * g + pr
                if u >= 4:
                    need(pe, "relu", u - 4)
                for h in range(2):
                    m = pe.matmul(PS[:, 3 + u % 4, h * S:(h + 1) * S],
                                  iqT[n % 2][:, (2 * pr + h) * P:(2 * pr + h + 1) * P], ikT[b % 2][:],
                                  start=True, stop=True)
                sig(by_pe, m, "idx_scores", b, 2 * g + pr)
                need(act, "idx_scores", b, 2 * g + pr)
                if u >= 3:
                    need(act, "idx_sum", u - 3)
                sig(by_act, act.activation(rel[u % 3][:], PS[:, 3 + u % 4, :], ACT.Relu), "relu", u)
                need(dve, "relu", u)
                for h in range(2):
                    head = 4 * g + 2 * pr + h
                    acc, w = accs[b % 2][:], iw[b % 2][:, head:head + 1]
                    r = rel[u % 3][:, h * S:(h + 1) * S]
                    if head == 0:
                        need(dve, "iw", b)
                        ins = dve.tensor_scalar(acc, r, w, None, ALU.mult)
                    else:
                        need(dve, "idx_acc", b, head - 1)
                        ins = dve.scalar_tensor_tensor(acc, r, w, acc, ALU.mult, ALU.add)
                    sig(by_dve, ins, "idx_acc", b, head)
                done[("idx_sum", u)] = done[("idx_acc", b, 4 * g + 2 * pr + 1)]

        def idx_topk_parts(b):
            acc = accs[b % 2][:]

            def scale():
                need(dve, "idx_acc", b, IH - 1)
                need(dve, "causal1")
                sig(by_dve, dve.scalar_tensor_tensor(acc, acc, float(ID ** -0.5), causal1[:], ALU.mult, ALU.add),
                    "taken", b, -1)

            def round_(r):
                need(dve, "taken", b, r - 1)
                sig(by_dve, dve.max(top8[:], acc), "top8", b, r)
                need(dve, "top8", b, r)
                sig(by_dve, dve.match_replace(acc, top8[:], acc, TAKEN), "taken", b, r)

            def finish():
                need(dve, "taken", b, TOPK // 8 - 1)
                sig(by_dve, dve.tensor_scalar(mask1[:, b, :], acc, (TAKEN + NOT_CAUSAL) / 2, MASKED,
                                              ALU.is_gt, ALU.mult), "mask1", b)
            return [scale] + [lambda r=r: round_(r) for r in range(TOPK // 8)] + [finish]

        LB = 7

        def latents(t):
            b, j = divmod(t, 2)
            need(pe, "xT", b)
            need(pe, "a1w")
            if t >= 1:
                need(pe, "latT", t - 1)
            for k in range(KT):
                m = pe.matmul(PS[:, LB, 0:A1N], XT[b % 2][:, k, j * P:(j + 1) * P], a1w[:, k, :],
                              start=(k == 0), stop=(k == KT - 1))
            sig(by_pe, m, "a1", t)
            need(act, "a1", t)
            if t >= 1:
                need(act, "lat_q", t - 1)
                need(act, "lrstd", t - 1)
                need(act, "ssq2", t - 1)
            sig(by_act, act.activation(junk[:, 0:QR], PS[:, LB, 0:QR], ACT.Square, scale=float(QR ** -0.5),
                                       accum_out=ssq[:, 0:1]), "ssq1", t)
            need(act, "ssq1", t)
            sig(by_act, act.activation(junk[:, 0:KVR], PS[:, LB, QR:QR + KVR], ACT.Square,
                                       scale=float(KVR ** -0.5), accum_out=ssq[:, 1:2]), "ssq2", t)
            need(dve, "ssq2", t)
            sig(by_dve, dve.tensor_scalar(ssq[:], ssq[:], EPS, None, ALU.add), "ssq_eps", t)
            need(pool, "ssq_eps", t)
            need(pool, "minus_half")
            if t >= 1:
                need(pool, "lat_kv", t - 1)
            sig(by_pool, pool.tensor_tensor(lrstd[:], ssq[:], minus_half[:], ALU.pow), "lrstd", t)
            need(dve, "rc")
            need(dve, "rs")
            if t >= 1:
                need(dve, "latT_ps", t - 1)
            kp = PS[:, LB, QR + KVR:A1N]
            sig(by_dve, dve.tensor_tensor(k1[:], kp, rc[:, j, :], ALU.mult), "k1", t)
            sig(by_dve, dve.tensor_tensor(pairs(k2[:], 1), pairs(kp, 1)[:, :, :, ::-1], pairs(rs[:, j, :], 1), ALU.mult),
                "k2", t)
            need(dve, "k2", t)
            sig(by_dve, dve.tensor_tensor(latk[:, t, KVR:P], k1[:], k2[:], ALU.add), "lat_pe", t)
            need(dve, "lrstd", t)
            need(dve, "wq_b")
            need(dve, "wkv_b")
            for dst, src in ((0, 0), (QR, P)):
                sig(by_dve, dve.scalar_tensor_tensor(latq[:, dst:dst + QR - src], PS[:, LB, src:QR], lrstd[:, 0:1],
                                                     wq_b[:, src:QR], ALU.mult, ALU.mult), "lat_q", t)
            sig(by_dve, dve.scalar_tensor_tensor(latk[:, t, 0:KVR], PS[:, LB, QR:QR + KVR], lrstd[:, 1:2],
                                                 wkv_b[:], ALU.mult, ALU.mult), "lat_kv", t)

        def latents_T(t):
            bank = PS[:, LB, :]
            half = QR - P
            need(pe, "lat_kv", t)
            need(pe, "ident")
            pe.transpose(bank[:, 0:P], latq[:, 0:P], ident[:])
            pe.transpose(bank[:, P:2 * P], latk[:, t, :], ident[:])
            sig(by_pe, pe.transpose(bank[:, 2 * P:3 * P], latq[:, P:2 * P], ident[:]), "latT_ps", t)
            need(act, "latT_ps", t)
            sig(by_act, act.activation(qh0[:, t, :], bank[:, 0:P], ACT.Copy), "qh0", t)
            sig(by_act, act.activation(q1s[0:half, t, :], bank[0:half, 2 * P:3 * P], ACT.Copy), "q1_hi", t)
            if t % 2 == 0:
                sig(by_act, act.activation(kT[:, t // 2, :], bank[:, P:2 * P], ACT.Copy), "kT_whole", t)
            sig(by_act, act.activation(kTh[:, t, :], bank[:, P:2 * P], ACT.Copy), "kT", t)
            need(dve, "kT", t)
            if t >= 1:
                need(dve, "latT", t - 1)
            sig(by_dve, dve.tensor_copy(qtmp[half:P], bank[half:P, 2 * P:3 * P]), "qtmp", t)
            sig(by_dve, dve.tensor_tensor(ql0[:, t, :], bank[:, 0:P], qh0[:, t, :].bitcast(F32), ALU.subtract), "ql0", t)
            sig(by_dve, dve.tensor_tensor(kTl[:, t, :], bank[:, P:2 * P], kTh[:, t, :].bitcast(F32), ALU.subtract), "kTl", t)
            need(dve, "qtmp", t)
            sig(by_dve, dve.tensor_tensor(q1s[half:P, t, :], bank[half:P, 2 * P:3 * P], qtmp[half:P].bitcast(F32),
                                          ALU.subtract), "latT", t)

        MISC, QB, QTB, SB_, PTB, OB = 0, 1, 3, 4, 6, 7
        misc_reader = [[("ikT", B - 1), ("iw", B - 1)]]

        def misc_bank():
            for n in misc_reader[0]:
                need(pe, *n)

        def fold_load(c):
            if c >= 1:
                need(sync, "fold_pe", c - 1, 1)
                need(sync, "fold_vo", c - 1, 1)
            hs = slice(HC * c, HC * (c + 1))
            load(("wt", "part"), wt_qn[:], a["qnT"][:, hs, :], group=("wt_q", c))
            load(("wt", "part"), wt_k[:], a["wkT"][:, hs, :], group=("wt_q", c))
            load(("wt", "part"), wt_pe[:], a["q_pe_w"][:, :, c * HC * ROPE:(c + 1) * HC * ROPE].rearrange("a p n -> p a n"),
                 group=("wt_q", c))
            load(("wt", "part"), wt_v[:], a["wvT"][:, hs, :], group=("wt_o", c))
            load(("wt", "part"), wt_o[:], a["o_w"].rearrange("(h p) n -> p h n", p=P)[:, hs, :], group=("wt_o", c))

        def two_parts(name, c, k, hi, lo, src, ready):
            need(act, *ready)
            if c >= 2:
                for e in (act, dve):
                    need(e, "qproj", (c - 1) * NT - 1)
                    need(e, "oproj", (c - 1) * NT - 1)
            sig(by_act, act.activation(hi, src, ACT.Copy), name + "_hi", c, k)
            need(dve, name + "_hi", c, k)
            sig(by_dve, dve.tensor_tensor(lo, src, hi.bitcast(F32), ALU.subtract), name, c, k)

        def fold_q(c, k):
            need(pe, "wt_q", c)
            misc_bank()
            for h in range(HC):
                m = pe.matmul(PS[:, MISC, h * KVR:(h + 1) * KVR], wt_qn[:, h, k * P:(k + 1) * P], wt_k[:, h, :],
                              start=True, stop=True)
            sig(by_pe, m, "fold_qk", c, k)
            hi, lo = ((Wh0, Wl0), (Wh1, Wl1))[k]
            two_parts("fold_q", c, k, hi[c % 2][:, 0:256], lo[c % 2][:, 0:256], PS[:, MISC, 0:256], ("fold_qk", c, k))
            misc_reader[0] = [("fold_q", c, k)]

        def fold_pe(c):
            for k in range(2):
                hi, lo = ((Wh0, Wl0), (Wh1, Wl1))[k]
                two_parts("fold_pe", c, k, hi[c % 2][:, 256:512], lo[c % 2][:, 256:512], wt_pe[:, k, :], ("wt_q", c))

        def fold_o(c, p):
            need(pe, "wt_o", c)
            misc_bank()
            for h in range(2):
                m = pe.matmul(PS[h * KVR:(h + 1) * KVR, MISC, :], wt_v[:, 2 * p + h, :], wt_o[:, 2 * p + h, :],
                              start=True, stop=True)
            sig(by_pe, m, "fold_vo", c, p)
            two_parts("fold_o", c, p, Woh[c % 2][:, p, :], Wol[c % 2][:, p, :], PS[:, MISC, :], ("fold_vo", c, p))
            misc_reader[0] = [("fold_o", c, p)]

        pending = []

        def topk_steps(n):
            for _ in range(n):
                if pending:
                    pending.pop(0)()

        for b in range(B):
            idx_keys(b)
            idx_queries(b, 0)
            for g in range(4):
                if g < 3:
                    idx_queries(b, g + 1)
                if g % 2 == 0 and 2 * b + g // 2 >= 1:
                    latents_T(2 * b + g // 2 - 1)
                idx_scores(b, g)
                if b == B - 1:
                    (lambda: fold_q(0, 0), lambda: fold_q(0, 1), lambda: fold_o(0, 0), lambda: fold_o(0, 1))[g]()
                topk_steps(3)
                if g % 2 == 0:
                    latents(2 * b + g // 2)
                topk_steps(2)
            pending = idx_topk_parts(b)
            if b + 2 < B:
                load_xT(b + 2)
            if b == 0:
                fold_load(0)
                unpack_zeros()
        latents_T(NT - 1)
        fold_pe(0)
        idx_end = [("idx_scores", B - 1, 7), ("a1", NT - 1), ("relu", 8 * B - 1), ("latT", NT - 1), ("idx_acc", B - 1, IH - 1),
                   ("lrstd", NT - 1), ("zeros",)]
        idx.close()

        work = ExitStack()
        folded_buffers(work, 1)
        qtok = [sb(work, f"qtok{i}", [P, HC, P]) for i in range(2)]
        r1 = [sb(work, f"r1{i}", [P, HC, ROPE]) for i in range(2)]
        r2 = [sb(work, f"r2{i}", [P, HC, ROPE]) for i in range(2)]
        qT = sb(work, "qT", [P, HC, P])
        qTh = sb(work, "qTh", [P, HC, P], F32R)
        qTl = sb(work, "qTl", [P, HC, P], F32R)
        prob = [sb(work, f"prob{i}", [P, HC, S]) for i in range(3)]
        pT = [sb(work, f"pT{i}", [P, 2, HC * P]) for i in range(2)]
        nmax = [sb(work, f"nmax{i}", [P, HC]) for i in range(3)]
        psum_ = [sb(work, f"psum{i}", [P, HC]) for i in range(3)]
        rsum = [sb(work, f"rsum{i}", [P, HC]) for i in range(3)]
        oTh = [sb(work, f"oTh{i}", [P, 2, P], F32R) for i in range(2)]
        oTl = [sb(work, f"oTl{i}", [P, 2, P], F32R) for i in range(2)]

        for e in (sync, act, dve, pool, pe):
            for n in idx_end:
                need(e, *n)
        xtok_view = a["x"].rearrange("(t p) n -> p t n", p=P)
        for q in range(4):
            load(("x", q), X[:, 4 * q:4 * q + 4, :], xtok_view[:, 4 * q:4 * q + 4, :])

        def q_project(i):
            c, t = divmod(i, NT)
            j, w = t % 2, c % 2
            need(pe, "latT", t)
            need(pe, "fold_q", c, 1)
            need(pe, "fold_pe", c, 1)
            if i >= 2:
                need(pe, "q_abs", i - 2)
                need(pe, "r2", i - 2)
            bank = PS[:, QB + i % 2, :]
            terms = ((qh0, Wh0), (qh0, Wl0), (ql0, Wh0), (q1s, Wh1), (q1s, Wl1))
            for n, (q, W) in enumerate(terms):
                m = pe.matmul(bank, q[:, t, :], W[w][:], start=(n == 0), stop=(n == len(terms) - 1))
            sig(by_pe, m, "qproj", i)
            need(dve, "qproj", i)
            if i >= 2:
                need(dve, "q_pe", i - 2)
            qp = pairs(bank[:, 256:512], HC)
            cb = pairs(rc[:, j, :], 1).broadcast_to([P, HC, ROPE // 2, 2])
            sb_ = pairs(rs[:, j, :], 1).broadcast_to([P, HC, ROPE // 2, 2])
            sig(by_dve, dve.tensor_tensor(r1[i % 2][:].rearrange("p h (i two) -> p h i two", two=2), qp, cb, ALU.mult),
                "r1", i)
            sig(by_dve, dve.tensor_tensor(r2[i % 2][:].rearrange("p h (i two) -> p h i two", two=2),
                                          qp[:, :, :, ::-1], sb_, ALU.mult), "r2", i)
            need(pool, "r2", i)
            if i >= 2:
                need(pool, "qtrans", i - 2)
            sig(by_pool, pool.tensor_tensor(qtok[i % 2][:, :, KVR:P], r1[i % 2][:], r2[i % 2][:], ALU.add), "q_pe", i)

        def q_latent(i):
            need(act, "r2", i)
            if i >= 2:
                need(act, "qtrans", i - 2)
            sig(by_act, act.activation(qtok[i % 2][:, :, 0:KVR],
                                       PS[:, QB + i % 2, 0:256].rearrange("p (h n) -> p h n", h=HC), ACT.Copy), "q_abs", i)

        def q_transpose(i):
            need(pe, "q_abs", i)
            need(pe, "q_pe", i)
            if i >= 1:
                need(pe, "qT", i - 1)
            for h in range(HC):
                m = pe.transpose(PS[:, QTB, h * P:(h + 1) * P], qtok[i % 2][:, h, :], ident[:])
            sig(by_pe, m, "qtrans", i)
            bank = PS[:, QTB, :].rearrange("p (h n) -> p h n", h=HC)
            if i % 2:
                need(act, "qtrans", i)
                if i >= 2:
                    need(act, "scores", i - 2)
                sig(by_act, act.activation(qTh[:], bank, ACT.Copy), "qTh", i)
                need(dve, "qTh", i)
                sig(by_dve, dve.tensor_tensor(qTl[:], bank, qTh[:].bitcast(F32), ALU.subtract), "qT", i)
            else:
                need(dve, "qtrans", i)
                if i >= 2:
                    need(dve, "scores", i - 2)
                sig(by_dve, dve.tensor_copy(qT[:], bank), "qT", i)

        def scores(i):
            t = i % NT
            b, j = divmod(t, 2)
            nk = P * (j + 1)
            need(pe, "qT", i)
            if i >= 1:
                need(pe, "masked", i - 1)
            bank = PS[:, SB_:SB_ + 2, :].rearrange("p a (h n) -> p (a h) n", h=2)
            kh, kl = (k[:, 2 * b:2 * b + 2, :].rearrange("p a n -> p (a n)") for k in (kTh, kTl))
            terms = ((qTh, kh), (qTh, kl), (qTl, kh)) if j else ((qT, kT[:, b, :]),)
            for h in range(HC):
                for n, (q, k) in enumerate(terms):
                    m = pe.matmul(bank[:, h, 0:nk], q[:, h, :], k, start=(n == 0), stop=(n == len(terms) - 1))
            sig(by_pe, m, "scores", i)
            need(dve, "scores", i)
            if i >= 3:
                need(dve, "ptrans", i - 3)
            if j:
                need(dve, "mask1", b)
                mask = mask1[:, b, :]
            else:
                need(dve, "mask0")
                mask = mask0[:]
            for h in range(HC):
                ins = dve.tensor_tensor_reduce(prob[i % 3][:, h, 0:nk], bank[:, h, 0:nk], mask, -QSCALE, 3.0e38,
                                               ALU.add, ALU.min, nmax[i % 3][:, h:h + 1])
            sig(by_dve, ins, "masked", i)

        def exps(i):
            nk = P * (i % 2 + 1)
            need(act, "masked", i)
            if i >= 3:
                need(act, "rsum", i - 3)
            for h in range(HC):
                p = prob[i % 3][:, h, 0:nk]
                ins = act.activation(p, p, ACT.Exp, bias=nmax[i % 3][:, h:h + 1], scale=-1.0,
                                     accum_out=psum_[i % 3][:, h:h + 1])
            sig(by_act, ins, "exp", i)

        def divide(i):
            nk = P * (i % 2 + 1)
            need(dve, "exp", i)
            if i >= 3:
                need(dve, "prob", i - 3)
            sig(by_dve, dve.reciprocal(rsum[i % 3][:], psum_[i % 3][:]), "rsum", i)
            need(pool, "rsum", i)
            p = prob[i % 3][:, :, 0:nk]
            sig(by_pool, pool.tensor_tensor(p, p, rsum[i % 3][:].unsqueeze(2).broadcast_to([P, HC, nk]), ALU.mult),
                "prob", i)

        ORDER = (0, 2, 1, 3)

        def p_transpose(i):
            j = i % 2
            need(pe, "prob", i)
            if i >= 1:
                need(pe, "pT", i - 1)
            for blk in range(j + 1):
                if blk == 1:
                    need(pe, "oT", i - 1)
                for s, h in enumerate(ORDER):
                    m = pe.transpose(PS[:, PTB + blk, s * P:(s + 1) * P],
                                     prob[i % 3][:, h, blk * P:(blk + 1) * P], ident[:])
            sig(by_pe, m, "ptrans", i)
            need(act, "ptrans", i)
            if i >= 2:
                need(act, "pv", i - 2)
            sig(by_act, act.activation(pT[i % 2][:, 0:j + 1, :], PS[:, PTB:PTB + j + 1, :], ACT.Copy), "pT", i)

        def attend(i):
            t = i % NT
            b, j = divmod(t, 2)
            need(pe, "pT", i)
            if i >= 1:
                need(pe, "oT", i - 1)
            for blk in range(j + 1):
                for odd in range(2):
                    m = pe.matmul(PS[KVR * odd:KVR * (odd + 1), OB, 0:2 * P], latk[:, 2 * b + blk, 0:KVR],
                                  pT[i % 2][:, blk, 2 * P * odd:2 * P * (odd + 1)], start=(blk == 0), stop=(blk == j))
            sig(by_pe, m, "pv", i)

        def attend_parts(i):
            need(act, "pv", i)
            if i >= 2:
                need(act, "oproj", i - 2)
                need(dve, "oproj", i - 2)
            bank = PS[:, OB, 0:2 * P].rearrange("p (a n) -> p a n", a=2)
            sig(by_act, act.activation(oTh[i % 2][:], bank, ACT.Copy), "oTh", i)
            need(dve, "oTh", i)
            sig(by_dve, dve.tensor_tensor(oTl[i % 2][:], bank, oTh[i % 2][:].bitcast(F32), ALU.subtract), "oT", i)

        def o_project(i):
            c, t = divmod(i, NT)
            w = c % 2
            need(pe, "oT", i)
            need(pe, "fold_o", c, 1)
            misc_bank()
            terms = [(o, W, q) for q in range(2) for o, W in ((oTh, Woh), (oTh, Wol), (oTl, Woh))]
            for n, (o, W, q) in enumerate(terms):
                m = pe.matmul(PS[:, MISC, :], o[i % 2][:, q, :], W[w][:, q, :], start=(n == 0), stop=(n == len(terms) - 1))
            sig(by_pe, m, "oproj", i)
            if c == NC - 1:
                layer_norm(t, PS[:, MISC, :], "attn", ("oproj", i), extra=("acc", c - 1, t), later=norm_later)
                misc_reader[0] = [("attn", "added", t)]
            else:
                need(dve, "oproj", i)
                need(dve, *(("acc", c - 1, t) if c else ("x", t // 4)))
                sig(by_dve, dve.tensor_tensor(X[:, t, :], X[:, t, :], PS[:, MISC, :], ALU.add), "acc", c, t)
                misc_reader[0] = [("acc", c, t)]

        N = NT * NC
        norm_later = []
        for i in range(2):
            q_project(i)
            q_latent(i)
        q_transpose(0)
        fold_load(1)
        for i in range(N + 4):
            c, t = divmod(i, NT)
            if i < N:
                scores(i)
                topk_steps(2)
            if c + 1 < NC:
                if t in (3, 5):
                    fold_q(c + 1, t // 4)
                if t == 7:
                    fold_pe(c + 1)
                if t in (9, 11):
                    fold_o(c + 1, t // 10)
                if t == 12 and c + 2 < NC:
                    fold_load(c + 2)
            if 1 <= i <= N:
                divide(i - 1)
            while norm_later:
                norm_later.pop(0)()
            if 2 <= i < N + 2:
                p_transpose(i - 2)
            if i + 1 < N:
                q_transpose(i + 1)
            if i + 2 < N:
                q_project(i + 2)
                q_latent(i + 2)
            if 3 <= i < N + 3:
                o_project(i - 3)
            if i < N:
                exps(i)
            if 2 <= i < N + 2:
                attend(i - 2)
                attend_parts(i - 2)
        assert not norm_later
        attn_end = [("oproj", N - 1), ("attn", "normed", NT - 1), ("pT", N - 1), ("oTh", N - 1), ("oT", N - 1), ("prob", N - 1)]
        work.close()
        attn.close()

        l1w = ExitStack()
        wo = sb(l1w, "wo", [P, KT, D])
        bo_b = sb(l1w, "bo_b", [P, D])
        Wf = sb(l1w, "Wf", [P, KT, D])
        ffn = ExitStack()
        sq = sb(ffn, "sq", [P, KT, D])
        la = sb(ffn, "la", [R, D])
        lb = sb(ffn, "lb", [R, D])
        mag = sb(ffn, "mag", [P, KT])
        ccol = sb(ffn, "ccol", [P, KT])
        cdiag = sb(ffn, "cdiag", [P, KT, P])
        ones = sb(ffn, "ones", [P, P])
        ints = sb(ffn, "ints", [P, 2 * FM, 512], F16)
        scales = sb(ffn, "scales", [P, 2 * FM, 512], F16)
        dints = sb(ffn, "dints", [P, 512], F16)
        Wd = sb(ffn, "Wd", [P, FM, D])
        nib = sb(ffn, "nib", [P, 512], I32)
        wtmp = [sb(ffn, f"wtmp{i}", [P, 512]) for i in range(2)]
        SLOTS = 3
        whi = [sb(ffn, f"whi{i}", [P, KT, P], F32R) for i in range(SLOTS)]
        wlo = [sb(ffn, f"wlo{i}", [P, KT, P], F32R) for i in range(SLOTS)]
        x1h = sb(ffn, "x1h", [P, KT, QUARTER], F32R)
        x1l = sb(ffn, "x1l", [P, KT, QUARTER], F32R)
        inter = sb(ffn, "inter", [P, FM, QUARTER])
        gate = [sb(ffn, f"gate{i}", [P, QUARTER]) for i in range(2)]
        y16 = [sb(ffn, f"y16{i}", [P, D], F16) for i in range(2)]

        load("nib_par", nib_par[:], a["nib_par"])
        order = [u for m in range(FM) for u in (m, FM + m)] + [2 * FM + m for m in range(FM)]

        def scale_group(m):
            return (m + 1).bit_length() - 1

        def load_unit(n, before_scales=None):
            v, i = order[n], n % RING
            load(("qpack", n), qpack[i][:], a["qpack"][v])
            load(("zrep", n), zrep[i][:], zeros_dram[v].partition_broadcast(P))
            if v >= 2 * FM:
                if before_scales:
                    need(sync, *before_scales)
                load(("gsc", n), gsc[i][:], a["gsc"][v].partition_broadcast(P))

        need(sync, "zeros")
        for n in range(RING):
            load_unit(n)
        for e in (sync, act, dve, pool, pe):
            for n in attn_end:
                need(e, *n)

        def load_scales(n):
            if n < 2 * FM:
                load(("scale", "part"), scales[:, order[n], :], a["gsc"][order[n]].partition_broadcast(P),
                     group=("scale", scale_group(n // 2)))

        for n in range(3):
            load_scales(n)

        def rows_of(ap):
            return ap.rearrange("(k p) n -> p k n", p=P)

        def load_layer1():
            load("la", la[:], a["lora_A"])
            load("lb", lb[:], a["lora_BT"])
            load("WfT", Wf[:], rows_of(a["ffnWT"]))
            load("mag", mag[:], a["mag"])
            load("wo", wo[:], rows_of(a["woT"]))
            load("bo_b", bo_b[:], a["bo"].partition_broadcast(P))

        def dequant(n):
            u, i = order[n], n % RING
            kind, m = divmod(u, FM)
            for w in ("qpack", "zrep"):
                need(dve, w, n)
            need(dve, "nib_par")
            if n >= 1:
                need(dve, "diff", n - 1)
            sig(by_dve, dve.tensor_scalar(nib[:], qpack[i][:], nib_par[:, 0:1], nib_par[:, 1:2],
                                          ALU.bitwise_and, ALU.logical_shift_right), "nib", n)
            need(dve, "nib", n)
            if kind == 2 and m:
                need(dve, "weight", n - 1)
            dst = dints[:] if kind == 2 else ints[:, u, :]
            sig(by_dve, dve.tensor_tensor(dst, nib[:], zrep[i][:], ALU.subtract), "diff", n)
            done[("unit", u)] = done[("diff", n)]
            if kind == 2:
                need(pool, "diff", n)
                need(pool, "gsc", n)
                sig(by_pool, pool.tensor_tensor(Wd[:, m, :], dints[:], gsc[i][:], ALU.mult), "weight", n)
                done[("unit", u)] = done[("weight", n)]
            load_scales(n + 3)
            if n + RING < UNITS:
                need(sync, "diff", n)
                load_unit(n + RING, ("weight", n) if kind == 2 else None)

        def weight(v):
            s, kind = divmod(v, 2)
            m = s % FM
            u = kind * FM + m
            need(pool, "unit", u)
            need(pool, "scale", scale_group(m))
            if v >= 2:
                need(pool, "wlo", v - 2)
            sig(by_pool, pool.tensor_tensor(wtmp[v % 2][:], ints[:, u, :], scales[:, u, :], ALU.mult), "wtmp", v)
            for e in (act, dve):
                if v >= SLOTS:
                    need(e, "gu", v - SLOTS)
            need(act, "wtmp", v)
            t = wtmp[v % 2][:].rearrange("p (k n) -> p k n", k=KT)
            sig(by_act, act.activation(whi[v % SLOTS][:], t, ACT.Copy), "whi", v)
            need(dve, "whi", v)
            sig(by_dve, dve.tensor_tensor(wlo[v % SLOTS][:], t, whi[v % SLOTS][:].bitcast(F32), ALU.subtract), "wlo", v)

        XB, WB, GB, UB, DB = 0, 1, 2, 4, 6

        def adapt_steps():
            def product(k):
                if k == 0:
                    sig(by_pool, pool.memset(ones[:], 1.0), "ones")
                    need(pe, "la")
                    need(pe, "lb")
                    need(pe, "x1T", 7)
                else:
                    need(pe, "effW", k - 1)
                sig(by_pe, pe.matmul(PS[:, WB, :], la[:, k * P:(k + 1) * P], lb[:], start=True, stop=True), "BA", k)
                need(dve, "BA", k)
                need(dve, "WfT")
                sig(by_dve, dve.tensor_tensor(Wf[:, k, :], Wf[:, k, :], PS[:, WB, :], ALU.add), "effW", k)

            def square(k):
                need(act, "effW", k)
                sig(by_act, act.activation(sq[:, k, :], Wf[:, k, :], ACT.Square), "effW2", k)

            def total():
                need(pe, "effW", KT - 1)
                need(pe, "effW2", KT - 1)
                need(pe, "ones")
                for j in range(KT):
                    for k in range(KT):
                        m = pe.matmul(PS[:, WB, j:j + 1], sq[:, k, j * P:(j + 1) * P], ones[:, 0:1],
                                      start=(k == 0), stop=(k == KT - 1))
                sig(by_pe, m, "norm2")

            def root():
                need(dve, "norm2")
                sig(by_dve, dve.tensor_copy(ccol[:], PS[:, WB, 0:KT]), "ccol")
                need(pool, "ccol")
                need(pool, "mag")
                sig(by_pool, pool.tensor_tensor(ccol[:], ccol[:], minus_half[:, 0:1].broadcast_to([P, KT]), ALU.pow),
                    "ccol_r")
                need(pool, "ccol_r")
                sig(by_pool, pool.tensor_tensor(ccol[:], ccol[:], mag[:], ALU.mult), "ccol_m")

            def spread():
                need(dve, "ccol_m")
                for j in range(KT):
                    sig(by_dve, dve.tensor_scalar(cdiag[:, j, :], ident[:], ccol[:, j:j + 1], None, ALU.mult), "cdiag")
                need(pe, "cdiag")
                need(pe, "ccol")
                for j in range(KT):
                    m = pe.matmul(PS[:, WB, j * P:(j + 1) * P], ones[:], cdiag[:, j, :], start=True, stop=True)
                sig(by_pe, m, "crow")

            def scale():
                need(dve, "crow")
                sig(by_dve, dve.tensor_tensor(Wf[:], Wf[:], PS[:, WB, :].unsqueeze(1).broadcast_to([P, KT, D]), ALU.mult),
                    "Wf")
            steps = [lambda k=k: product(k) for k in range(KT)]
            steps += [lambda k=k: square(k) for k in range(KT)]
            return steps + [total, root, spread, scale]

        def x1_transpose(t):
            q = t // 4
            need(pe, "attn", "normed", t)
            if t >= 2:
                need(pe, "x1T", t - 2)
            if ("Wf",) in done and t % 2:
                need(pe, "Wf")
            for k in range(KT):
                m = pe.transpose(PS[:, XB + t % 2, k * P:(k + 1) * P], X[:, t, k * P:(k + 1) * P], ident[:])
            sig(by_pe, m, "x1T_ps", t)
            need(act, "x1T_ps", t)
            if q >= 1:
                need(act, "gu", 2 * FM * q - 1)
            bank = PS[:, XB + t % 2, :].rearrange("p (k n) -> p k n", k=KT)
            cols = slice((t % 4) * P, (t % 4 + 1) * P)
            sig(by_act, act.activation(x1h[:, :, cols], bank, ACT.Copy), "x1h", t)
            need(dve, "x1h", t)
            sig(by_dve, dve.tensor_tensor(x1l[:, :, cols], bank, x1h[:, :, cols].bitcast(F32), ALU.subtract), "x1T", t)

        def gate_up(q, m):
            s = q * FM + m
            need(pe, "x1T", 4 * q + 3)
            if s >= 2:
                need(pe, "inter", s - 2)
            for kind, bk in ((0, GB), (1, UB)):
                v = 2 * s + kind
                need(pe, "wlo", v)
                hi, lo = whi[v % SLOTS], wlo[v % SLOTS]
                for k in range(KT):
                    for n, (w, x) in enumerate(((hi, x1h), (lo, x1h), (hi, x1l))):
                        ins = pe.matmul(PS[:, bk + s % 2, :], w[:, k, :], x[:, k, :],
                                        start=(k == 0 and n == 0), stop=(k == KT - 1 and n == 2))
                sig(by_pe, ins, "gu", v)
                if kind == 0:
                    need(act, "gu", v)
                    if s >= 2:
                        need(act, "inter", s - 2)
                    sig(by_act, act.activation(gate[s % 2][:], PS[:, GB + s % 2, :], ACT.Silu), "silu", s)
                    if v + SLOTS < 8 * FM:
                        weight(v + SLOTS)
            need(dve, "silu", s)
            need(dve, "gu", 2 * s + 1)
            if q:
                need(dve, "down", 4 * q - 1)
            sig(by_dve, dve.tensor_tensor(inter[:, m, :], gate[s % 2][:], PS[:, UB + s % 2, :], ALU.mult), "inter", s)
            if v + SLOTS < 8 * FM:
                weight(v + SLOTS)

        def down(t):
            need(pe, "inter", FM * (t // 4 + 1) - 1)
            if t >= 2:
                need(pe, "y16", t - 2)
            for m in range(FM):
                M = P if m < FM - 1 else FLAST
                need(pe, "unit", 2 * FM + m)
                ins = pe.matmul(PS[:, DB + t % 2, :], inter[0:M, m, (t % 4) * P:(t % 4 + 1) * P], Wd[0:M, m, :],
                                start=(m == 0), stop=(m == FM - 1))
            sig(by_pe, ins, "down", t)
            need(act, "down", t)
            if t >= 2:
                need(act, "ffn", "added", t - 2)
            sig(by_act, act.activation(y16[t % 2][:], PS[:, DB + t % 2, :], ACT.Copy), "y16", t)
            layer_norm(t, y16[t % 2][:], "ffn", ("y16", t))

        for n in range(5):
            dequant(n)
            if n < SLOTS:
                weight(n)
            if n == 1:
                for t in range(4):
                    x1_transpose(t)
        made = 5
        side = adapt_steps()
        for q in range(4):
            for m in range(FM):
                for _ in range(3):
                    if made < UNITS:
                        dequant(made)
                        made += 1
                gate_up(q, m)
                if q == 0 and m == FM - 1:
                    load_layer1()
                if q == 1:
                    for _ in range(2 if m == 2 else 1):
                        side.pop(0)()
            for t in range(4 * q, 4 * q + 4):
                if t + 4 < NT:
                    x1_transpose(t + 4)
                down(t)
        assert not side and made == UNITS
        ffn_end = [("ffn", "normed", NT - 1), ("down", NT - 1), ("weight", UNITS - 1), ("Wf",),
                   ("ffn", "rstd", NT - 1)]
        ffn.close()

        gqa = ExitStack()
        hpar = sb(gqa, "hpar", [P, 2])
        x2T = sb(gqa, "x2T", [P, KT, S])
        wqkv = sb(gqa, "wqkv", [P, KT, D + 2 * P])
        qhi = sb(gqa, "qhi", [P, G, S], F32R)
        qlo = sb(gqa, "qlo", [P, G, S], F32R)
        khi = sb(gqa, "khi", [P, 2, S], F32R)
        klo = sb(gqa, "klo", [P, 2, S], F32R)
        khr = sb(gqa, "khr", [P, S], F32R)
        klr = sb(gqa, "klr", [P, S])
        qs = [sb(gqa, f"qs{i}", [P, KVH // 2, G, S], F32R) for i in range(2)]
        ks = [sb(gqa, f"ks{i}", [P, KVH // 2, 2, S], F32R) for i in range(2)]
        v32 = [sb(gqa, f"v32{i}", [P, 2, KVH, 32]) for i in range(3)]
        gmax = [sb(gqa, f"gmax{i}", [P, 2, KVH // 2, G]) for i in range(2)]
        kones_f = sb(gqa, "kones_f", [P, 2, S])
        mT = sb(gqa, "mT", [KVH * G, P])
        mhi = [sb(gqa, f"mhi{i}", [KVH * G, P], F32R) for i in range(2)]
        mlo = [sb(gqa, f"mlo{i}", [KVH * G, P], F32R) for i in range(2)]
        gp = [sb(gqa, f"gp{i}", [P, 2, G * P]) for i in range(KVH)]
        yraw = [sb(gqa, f"yraw{i}", [P, G * P]) for i in range(2)]
        grs = sb(gqa, "grs", [P, G, 4])
        ytok = [sb(gqa, f"ytok{i}", [P, D]) for i in range(2)]
        yT = [sb(gqa, f"yT{i}", [P, KT, P]) for i in range(2)]
        x3T = [sb(gqa, f"x3T{i}", [P, KT, P]) for i in range(2)]
        for e in (sync, act, dve, pool, pe):
            for n in ffn_end:
                need(e, *n)
        load("wqkv", wqkv[:], a["wqkv"].rearrange("(k p) n -> p k n", p=P))
        load("hpar", hpar[:], a["hpar"])
        load("kones_f", kones_f[96:P], a["kones"])
        need(dve, "kones_f")
        for i in range(2):
            sig(by_dve, dve.tensor_copy(ks[i][96:P], kones_f[96:P].unsqueeze(1).broadcast_to([32, KVH // 2, 2, S])),
                "kones", i)
            sig(by_dve, dve.tensor_scalar(qs[i][96:P].rearrange("p h (a g) n -> p h a (g n)", a=2),
                                          kones_f[96:P].rearrange("p a n -> p (a n)").unsqueeze(1).unsqueeze(1)
                                          .broadcast_to([32, KVH // 2, 2, 2 * S]), 0.0, None, ALU.mult), "qs_zeros", i)
        for i in range(3):
            sig(by_pool, pool.memset(v32[i][:], 0.0), "v32_zeros", i)
            need(pool, "v32_zeros", i)
            sig(by_pool, pool.memset(v32[i][:, :, :, HD:HD + 1], 1.0), "v32_ones", i)

        TB2, PJ, GS, GT, GY, OUT = 0, 1, 2, 4, 6, 7
        mcount, pcount, ocount = [0], [0], [0]
        deferred = []

        def flush():
            while deferred:
                deferred.pop(0)()

        def misc_turn(eng, track, name, transposes_, evacuate, ready, before=()):
            c = mcount[0]
            mcount[0] += 1
            bank = PS[:, TB2, :]
            for n in ready:
                if n not in done:
                    flush()
                need(pe, *n)
            if c >= 1:
                if ("misc", c - 1) not in done:
                    flush()
                need(pe, "misc", c - 1)
            sig(by_pe, transposes_(bank), "misc_ps", c)

            def drain():
                need(eng, "misc_ps", c)
                for n in before:
                    if n in done:
                        need(eng, *n)
                sig(track, evacuate(bank), "misc", c)
                done[name] = done[("misc", c)]
            deferred.append(drain)

        def transpose_tile(name, t, src, ready, dst, before):
            def go(bank):
                for k in range(KT):
                    m = pe.transpose(bank[:, k * P:(k + 1) * P], src[:, k * P:(k + 1) * P], ident[:])
                return m
            misc_turn(act, by_act, (name, t), go,
                      lambda bank: act.activation(dst, bank.rearrange("p (k n) -> p k n", k=KT), ACT.Copy),
                      [ready], before)

        starting = [True]

        def bank1_turn():
            turn = pcount[0]
            pcount[0] += 1
            for c in (turn - 2,) if starting[0] else (turn - 2, turn - 1):
                if c >= 0:
                    if ("bank1", c) not in done:
                        flush()
                    need(pe, "bank1", c)
            return turn, PS[:, GY if starting[0] and turn % 2 else PJ, :]

        def split_stack(b, src_hi, src_lo, dst, kinds, name):
            for p2 in range(KVH // 2):
                for part, kind in enumerate(kinds):
                    src = (src_hi, src_lo)[kind]
                    load((name, "part"), dst[32 * part:32 * part + 32, p2].bitcast(F32),
                         src[32 * p2:32 * p2 + 32].bitcast(F32), group=(name, 4 * b + p2))

        def stacked(eng, name, b):
            for p2 in range(KVH // 2):
                need(eng, name, 4 * b + p2)

        def ready_x2T(b):
            if ("x2T", 2 * b + 1) not in done:
                flush()
            need(pe, "x2T", 2 * b + 1)
            need(pe, "wqkv")

        def qkv_q(b, g):
            turn, bank = bank1_turn()
            ready_x2T(b)
            for k in range(KT):
                m = pe.matmul(bank[:, 0:S], wqkv[:, k, g * P:(g + 1) * P], x2T[:, k, :], start=(k == 0), stop=(k == KT - 1))
            sig(by_pe, m, "q_ps", b, g)

            def parts():
                need(act, "q_ps", b, g)
                if b >= 1:
                    stacked(act, "qs", b - 1)
                    stacked(dve, "qs", b - 1)
                sc = float(HD ** -0.5)
                sig(by_act, act.activation(qhi[:, g, :], bank[:, 0:S], ACT.Copy, scale=sc), "qhi", b, g)
                need(dve, "qhi", b, g)
                sig(by_dve, dve.scalar_tensor_tensor(qlo[:, g, :], bank[:, 0:S], sc, qhi[:, g, :].bitcast(F32),
                                                     ALU.mult, ALU.subtract), "qlo", b, g)
                done[("bank1", turn)] = done[("qlo", b, g)]
            deferred.append(parts)

        def qkv_k(b):
            turn, bank = bank1_turn()
            ready_x2T(b)
            for k in range(KT):
                m = pe.matmul(bank[:, 0:S], wqkv[:, k, D:D + P], x2T[:, k, :], start=(k == 0), stop=(k == KT - 1))
            sig(by_pe, m, "k_ps", b)

            def parts():
                need(dve, "k_ps", b)
                need(dve, "hpar")
                if b >= 1:
                    stacked(dve, "ks", b - 1)
                    need(dve, "klo", b - 1)
                sig(by_dve, dve.tensor_copy(khr[:], bank[:, 0:S]), "khr", b)
                need(dve, "khr", b)
                sig(by_dve, dve.tensor_tensor(klr[:], bank[:, 0:S], khr[:].bitcast(F32), ALU.subtract), "klr", b)
                done[("bank1", turn)] = done[("klr", b)]
                need(dve, "klr", b)
                for p in range(2):
                    sig(by_dve, dve.tensor_scalar(khi[:, p, :], khr[:].bitcast(F32), hpar[:, p:p + 1], None, ALU.mult), "khi", b)
                    sig(by_dve, dve.tensor_scalar(klo[:, p, :], klr[:], hpar[:, p:p + 1], None, ALU.mult), "klo", b)
            deferred.append(parts)

        def qkv_v(b):
            turn, bank = bank1_turn()
            for blk in range(2):
                for k in range(KT):
                    m = pe.matmul(bank[:, blk * P:(blk + 1) * P], x2T[:, k, blk * P:(blk + 1) * P],
                                  wqkv[:, k, D + P:D + 2 * P], start=(k == 0), stop=(k == KT - 1))
            sig(by_pe, m, "v_ps", b)

            def evacuate():
                need(act, "v_ps", b)
                need(act, "v32_ones", b % 3)
                if b >= 3:
                    need(act, "gpv", 2 * 2 * (b - 2) - 1)
                sig(by_act, act.activation(v32[b % 3][:, :, :, 0:HD],
                                           bank[:, 0:S].rearrange("p (b h d) -> p b h d", b=2, d=HD), ACT.Copy), "v32", b)
                done[("bank1", turn)] = done[("v32", b)]
            deferred.append(evacuate)

        def stack_free(b):
            if b >= 2:
                need(sync, "gst_blk", 2 * (16 * (b - 1) - 1) + 1)
            if b >= 1:
                need(sync, "gs", 2 * (16 * (b - 1) + 7) + 1)

        def stack_q(b):
            need(sync, "qhi", b, G - 1)
            need(sync, "qlo", b, G - 1)
            split_stack(b, qhi, qlo, qs[b % 2], (0, 0, 1), "qs")

        def stack_k(b):
            need(sync, "khi", b)
            need(sync, "klo", b)
            split_stack(b, khi, klo, ks[b % 2], (0, 1, 0), "ks")

        def row_maxima(i):
            t, r = divmod(i, 8)
            b, j = divmod(t, 2)
            p2, g0 = r // 2, 2 * (r % 2)
            need(pe, "qs", 4 * b + p2)
            need(pe, "ks", 4 * b + p2)
            if t >= 2:
                need(dve, "mT", t - 2)
            for g in (g0, g0 + 1):
                a_ = g % 2
                if i >= 1:
                    need(pe, "gmax", 2 * (i - 1) + a_)
                sig(by_pe, pe.matmul(PS[:, GS + a_, :], qs[b % 2][0:96, p2, g, j * P:(j + 1) * P],
                                     ks[b % 2][0:96, p2, :, :].rearrange("p a n -> p (a n)"), start=True, stop=True),
                    "gs", 2 * i + a_)
                need(dve, "gs", 2 * i + a_)
                sig(by_dve, dve.tensor_reduce(gmax[t % 2][:, :, p2, g],
                                              PS[:, GS + a_, :].rearrange("p (h n) -> p h n", h=2),
                                              AX.X, ALU.max, negate=True), "gmax", 2 * i + a_)

        def max_rows(t):
            b, j = divmod(t, 2)
            misc_turn(dve, by_dve, ("mT", t),
                      lambda bank: pe.transpose(bank[0:KVH * G, 0:P], gmax[t % 2][:].rearrange("p a h g -> p (a h g)"), ident[:]),
                      lambda bank: dve.tensor_copy(mT[:], bank[0:KVH * G, 0:P]),
                      [("gmax", 16 * t + 15)], [("mlo", t - 1), ("mhi", t - 1)])
            flush()
            need(dve, "mT", t)
            if t >= 2:
                need(dve, "mrow", t - 2)
            sig(by_dve, dve.tensor_copy(mhi[t % 2][:], mT[:]), "mhi", t)
            need(dve, "mhi", t)
            sig(by_dve, dve.tensor_tensor(mlo[t % 2][:], mT[:], mhi[t % 2][:].bitcast(F32), ALU.subtract), "mlo", t)
            if t >= 4:
                need(sync, "gst_blk", 2 * (8 * (t - 3) - 1) + 1)
            need(sync, "mlo", t)
            need(sync, "qs_zeros", b % 2)
            for part, m in enumerate((mhi, mlo)):
                load(("mrow", "part"), qs[b % 2][96 + 2 * part:98 + 2 * part, :, :, j * P:(j + 1) * P].bitcast(F32),
                     m[t % 2][:].bitcast(F32), group=("mrow", t))

        def transposed_scores(i):
            t, h = divmod(i, 8)
            b, j = divmod(t, 2)
            need(pe, "qs", 4 * b + h // 2)
            need(pe, "mrow", t)
            need(pe, "kones", b % 2)
            for blk in range(2):
                if i >= 1:
                    need(pe, "gexp", 2 * (i - 1) + blk)
                bank = PS[:, GT + blk, :]
                m = pe.matmul(bank, ks[b % 2][:, h // 2, h % 2, blk * P:(blk + 1) * P],
                              qs[b % 2][:, h // 2, :, j * P:(j + 1) * P], start=True, stop=True)
                sig(by_pe, m, "gst_blk", 2 * i + blk)
                need(act, "gst_blk", 2 * i + blk)
                if t >= 1:
                    need(act, "gpv", 2 * (t - 1) + h // 4)
                sig(by_act, act.activation(gp[h][:, blk, :], bank, ACT.Exp), "gexp", 2 * i + blk)

        def g_attend(t, u, blk):
            b, j = divmod(t, 2)
            need(pe, "gexp", 2 * (8 * t + 4 * u + 3) + 1)
            need(pe, "v32", b)
            if 2 * t + u >= 1:
                need(pe, "yraw", 2 * t + u - 1)
            for c in range(4):
                m = pe.matmul(PS[32 * c:32 * c + 32, GY, :], v32[b % 3][:, blk, 4 * u + c, :],
                              gp[4 * u + c][:, blk, :], start=(blk == 0), stop=(blk == 1))
            if blk == 1:
                sig(by_pe, m, "gpv", 2 * t + u)
                deferred.append(lambda: g_evacuate(t, u))

        def g_evacuate(t, u):
            need(act, "gpv", 2 * t + u)
            if t >= 1:
                need(act, "ytok", 2 * (t - 1) + u)
            sig(by_act, act.activation(yraw[u][:], PS[:, GY, :], ACT.Copy), "yraw", 2 * t + u)

        def g_normalise(t, u):
            def transposes(bank):
                for g in range(G):
                    m = pe.transpose(bank[:, g * P:(g + 1) * P], yraw[u][:, g * P:(g + 1) * P], ident[:])
                return m

            def divide(bank):
                y = bank.rearrange("p (g h d) -> p g h d", g=G, d=32)
                if 2 * t + u >= 1:
                    need(dve, "ytok", 2 * t + u - 1)
                sig(by_dve, dve.reciprocal(grs[:].unsqueeze(3), y[:, :, :, HD:HD + 1]), "grs", t, u)
                need(dve, "grs", t, u)
                dst = ytok[t % 2][:, u * 256:(u + 1) * 256].rearrange("p (h g d) -> p g h d", g=G, d=HD)
                for g in range(G):
                    m = dve.tensor_tensor(dst[:, g], y[:, g, :, 0:HD],
                                          grs[:, g].unsqueeze(2).broadcast_to([P, 4, HD]), ALU.mult)
                    if g < G - 1:
                        sig(by_dve, m, "ytok_part")
                return m
            misc_turn(dve, by_dve, ("ytok", 2 * t + u), transposes, divide, [("yraw", 2 * t + u)], [("yT", t - 2)])

        def add_bias(t):
            need(pool, "bo_b")
            need(pool, "x2T", t)
            sig(by_pool, pool.tensor_tensor(X[:, t, :], X[:, t, :], bo_b[:], ALU.add), "x_bo", t)

        def y_transpose(t):
            transpose_tile("yT", t, ytok[t % 2], ("ytok", 2 * t + 1), yT[t % 2][:], [("g_out", t - 2)])

        def product(t, part, xT, W, name, tag, extra=None, then=None):
            if part == 0:
                for n in (xT[0], W[0]) + ((("out_bank", ocount[0] - 1),) if ocount[0] else ()):
                    if n not in done:
                        flush()
                    need(pe, *n)
            for k in range(KT // 2 * part, KT // 2 * (part + 1)):
                m = pe.matmul(PS[:, OUT, :], xT[1][:, k, :], W[1][:, k, :], start=(k == 0), stop=(k == KT - 1))
            if part == 0:
                return
            sig(by_pe, m, name, t)
            turn = ocount[0]
            ocount[0] += 1

            def norm():
                layer_norm(t, PS[:, OUT, :], tag, (name, t), extra=extra)
                done[("out_bank", turn)] = done[(tag, "added", t)]
                if then:
                    then()
            deferred.append(norm)

        out_view = out.rearrange("(t p) n -> p t n", p=P)

        def g_output(t, part):
            product(t, part, (("yT", t), yT[t % 2]), (("wo",), wo), "g_out", "gqa", extra=("x_bo", t))

        def linear1(t):
            transpose_tile("x3T", t, X[:, t, :], ("gqa", "normed", t), x3T[t % 2][:], [("lin", t - 2)])

        def linear2(t, part):
            def store():
                need(sync, "lin_ln", "normed", t)
                load(("store", t), out_view[:, t, :], X[:, t, :])
            product(t, part, (("x3T", t), x3T[t % 2]), (("Wf",), Wf), "lin", "lin_ln", then=store)

        def x2_transpose(t):
            transpose_tile("x2T", t, X[:, t, :], ("ffn", "normed", t),
                           x2T[:, :, (t % 2) * P:(t % 2 + 1) * P], [("v_ps", t // 2 - 1), ("q_ps", t // 2 - 1, G - 1)])

        def stack(b):
            flush()
            stack_free(b)
            stack_k(b)
            stack_q(b)

        AHEAD = 10

        def tile_work(t, h):
            p = t - 1
            if h < 2:
                if h == 0 and p >= 1:
                    linear1(p - 1)
                if p >= 0:
                    g_attend(p, 1, h)
            if h == 2 and p >= 0:
                g_normalise(p, 1)
                add_bias(p)
            if h in (2, 3) and p >= 1:
                linear2(p - 1, h - 2)
            if h == 3 and p >= 0:
                y_transpose(p)
            if h in (4, 5):
                if t < NT:
                    g_attend(t, 0, h - 4)
                if p >= 0:
                    g_output(p, h - 4)
            if h == 6 and t < NT:
                g_normalise(t, 0)

        def sequence_work(b, step):
            if step in (1, 4):
                x2_transpose(2 * b + (step == 4))
            if step == 6:
                qkv_k(b)
            if step == 7:
                qkv_v(b)
            if step in (8, 9, 14, 15):
                qkv_q(b, (8, 9, 14, 15).index(step))

        for step in range(16):
            sequence_work(0, step)
        stack(0)
        for step in range(8):
            sequence_work(1, step)
        flush()
        for i in range(AHEAD):
            row_maxima(i)
            if i < 8:
                sequence_work(1, 8 + i)
            flush()
            if i % 8 == 7:
                max_rows(i // 8)
        starting[0] = False
        for c in (pcount[0] - 2, pcount[0] - 1):
            need(pe, "bank1", c)
        for i in range(8 * NT):
            t, h = divmod(i, 8)
            b, step = divmod(i, 16)
            transposed_scores(i)
            if i + AHEAD < 8 * NT:
                row_maxima(i + AHEAD)
            tile_work(t, h)
            if step == 0 and b + 1 < B:
                stack(b + 1)
            if b + 2 < B:
                sequence_work(b + 2, step)
            flush()
            if i + AHEAD < 8 * NT and (i + AHEAD) % 8 == 7:
                max_rows((i + AHEAD) // 8)
        for h in range(6):
            tile_work(NT, h)
        flush()
        linear1(NT - 1)
        for part in range(2):
            linear2(NT - 1, part)
        flush()
        for t in range(NT):
            need(sync, "store", t)
        gqa.close()
        l1w.close()


def kernel(**inputs):
    import concourse.bacc as bacc
    from concourse.bass_utils import run_bass_kernel_spmd

    g = {k: np.asarray(v) for k, v in inputs.items()}
    f32 = np.float32
    arrays = {}
    x = g["L0_attn_hidden_states"].reshape(TOK, D)
    arrays["x"] = x
    arrays["xT"] = x.T
    arrays["wk_i"] = g["L0_attn_idx_wk_w"]
    arrays["ww_i"] = g["L0_attn_idx_weights_w"]
    arrays["wq_i"] = g["L0_attn_idx_wq_w"]
    arrays["a1w"] = np.concatenate([g["L0_attn_q_a_w"], g["L0_attn_kv_a_w"]], axis=1)
    qb = g["L0_attn_q_b_w"].reshape(QR, H, NOPE + ROPE)
    dup = np.concatenate([np.arange(QR), np.arange(P, QR)])
    arrays["q_pe_w"] = qb[dup, :, NOPE:].reshape(2, P, H * ROPE)
    arrays["qnT"] = qb[dup, :, :NOPE].transpose(2, 1, 0)
    kvb = g["L0_attn_kv_b_w"].reshape(KVR, H, NOPE + VD)
    arrays["wkT"] = kvb[:, :, :NOPE].transpose(2, 1, 0)
    arrays["wvT"] = kvb[:, :, NOPE:].transpose(2, 1, 0)
    arrays["o_w"] = g["L0_attn_o_w"]
    arrays["q_norm"] = g["L0_attn_q_a_norm_w"]
    arrays["kv_norm"] = g["L0_attn_kv_a_norm_w"]
    inv = (f32(1.0) / f32(10000.0) ** (np.arange(0, ROPE, 2, dtype=f32) / f32(ROPE))).astype(f32)
    ang = np.arange(S, dtype=f32)[:, None] * inv[None, :]
    arrays["rope_c"] = np.repeat(np.cos(ang), 2, axis=1).astype(f32)
    arrays["rope_s"] = np.stack([-np.sin(ang), np.sin(ang)], axis=2).reshape(S, ROPE).astype(f32)
    q, k = np.arange(S)[:, None], np.arange(S)[None, :]
    bf = mybir.dt.np(BF16)
    arrays["mask0"] = np.where(k <= q, 0.0, MASKED)[:P, :P].astype(bf)
    arrays["causal1"] = np.where(k <= q, 0.0, NOT_CAUSAL)[P:].astype(f32)
    arrays["ident"] = np.eye(P, dtype=f32)
    arrays["hpar"] = (np.arange(P)[:, None] // HD % 2 == np.arange(2)[None, :]).astype(f32)
    kones = ((np.arange(32)[:, None] < 4) & (np.arange(32)[:, None] % 2 == np.arange(2)[None, :])).astype(f32)
    arrays["kones"] = np.repeat(kones[:, :, None], S, axis=2)
    shift = 4 * (np.arange(P, dtype=np.int64) % 8)
    arrays["nib_par"] = np.stack([(15 << shift).astype(np.uint32).view(np.int32), shift.astype(np.int32)], axis=1)
    arrays["zsh"] = (4 * (np.arange(512) % 8)).astype(np.int32)

    def units(name, down):
        qw, zw, sc = (g[f"L0_ffn_{name}_{w}"] for w in ("qweight", "zeros", "scales"))
        qw, zw = np.repeat(qw, 8, axis=0), np.repeat(zw, 8, axis=1)
        if down:
            qw = np.pad(qw, ((0, FM * P - FI), (0, 0)))
            return qw.reshape(FM, P, D), zw, sc
        pad = ((0, 0), (0, FM * P - FI))
        qw, zw, sc = (np.pad(w, pad) for w in (qw, zw, sc))
        qw = qw.reshape(KT, P, FM, P).transpose(2, 1, 0, 3).reshape(FM, P, 512)
        zw, sc = (w.reshape(KT, FM, P).transpose(1, 0, 2).reshape(FM, 512) for w in (zw, sc))
        return qw, zw, sc
    parts = [units("gate", False), units("up", False), units("down", True)]
    for n, name in enumerate(("qpack", "zrep", "gsc")):
        arrays[name] = np.concatenate([p[n] for p in parts], axis=0)

    wq = g["L1_attn_Wq"].T.reshape(D, KVH, G, HD).transpose(0, 2, 1, 3).reshape(D, D)
    arrays["wqkv"] = np.concatenate([wq, g["L1_attn_Wk"].T, g["L1_attn_Wv"].T], axis=1)
    arrays["woT"] = g["L1_attn_Wo"].T
    arrays["bo"] = g["L1_attn_bo"]
    arrays["ffnWT"] = g["L1_ffn_W"].T
    arrays["lora_A"] = g["L1_ffn_lora_A"]
    arrays["lora_BT"] = g["L1_ffn_lora_B"].T
    arrays["mag"] = g["L1_ffn_magnitude"].reshape(KT, P).T

    nc = bacc.Bacc("TRN2", target_bir_lowering=False, num_devices=1)
    feeds, args = {}, {}
    for name, arr in arrays.items():
        arr = np.ascontiguousarray(arr)
        feeds["in_" + name] = arr
        args[name] = nc.dram_tensor("in_" + name, arr.shape, mybir.dt.from_np(arr.dtype), kind="ExternalInput").ap()
    out = nc.dram_tensor("out_x", (TOK, D), F32, kind="ExternalOutput").ap()
    build(nc, args, out)
    r = run_bass_kernel_spmd(nc, [feeds], core_ids=[0])
    return r.results[0]["out_x"].reshape(B, S, D)
```
